# Optimizing a Trainium2 kernel written in Bass

```python
import numpy as np
import jax
import jax.numpy as jnp

def _softmax(x, axis=-1):
    return jax.nn.softmax(x, axis=axis)

def _gelu(x):
    return jax.nn.gelu(x, approximate=True)

def _silu(x):
    return jax.nn.silu(x)

def _sigmoid(x):
    return jax.nn.sigmoid(x)

def _layernorm(x, axis=-1, eps=1e-05):
    m = jnp.mean(x, axis=axis, keepdims=True)
    v = jnp.var(x, axis=axis, keepdims=True)
    return (x - m) / jnp.sqrt(v + eps)

def _scatter_add(tgt, idx, src, axis=0):
    return tgt.at[idx].add(src)

def _segment_sum(src, seg, n):
    return jax.ops.segment_sum(src, seg, n)
kernel_name = 'mk_decoder_postln_d1_seqx_r8_fb930f'

def setup_inputs(seed: int=0):
    np.random.seed(seed)
    _w = jnp.asarray

    def _rec_inputs():
        import jax
        import jax.numpy as jnp
        _rk = jax.random.key(seed)
        x = -0.0002928 + 1 * jax.random.normal(jax.random.fold_in(_rk, 1), (4, 512, 128), jnp.float32)
        _lenS = 512 - jax.random.randint(jax.random.fold_in(_rk, 7), (4,), 0, max(1, 512 // 4) + 1, jnp.int32)
        _lenS2 = 32 - jax.random.randint(jax.random.fold_in(_rk, 8), (4,), 0, max(1, 32 // 4) + 1, jnp.int32)
        _ctx_1024P = jax.random.normal(jax.random.fold_in(_rk, 11), (4, 16, 128), jnp.float32)
        _ctx_1024c = jax.random.dirichlet(jax.random.fold_in(_rk, 511), 0.3 * jnp.ones((16,), jnp.float32), (4, 32))
        _ctx_1024t = jnp.einsum('bsk,bkd->bsd', _ctx_1024c, _ctx_1024P)
        _ctx_1024t = _ctx_1024t * jax.lax.rsqrt(jnp.mean(jnp.square(_ctx_1024t)) + 1e-12) * 0.953939
        ctx_1024 = -1.39393e-06 + 0.999914 * (_ctx_1024t + 0.3 * jax.random.normal(jax.random.fold_in(_rk, 611), (4, 32, 128), jnp.float32))
        return (x, ctx_1024)
    x, ctx_1024 = _rec_inputs()

    def _L0_attn_setup():
        import jax, jax.numpy as jnp
        import numpy as np
        import math
        B, T, D = (2, 256, 128)
        H = 16
        d = D // H
        I = 352
        RMS_EPS = 1e-06
        GN_EPS = 1e-05

        def _rmsnorm(x, w):
            var = jnp.mean(x * x, axis=-1, keepdims=True)
            return x * jax.lax.rsqrt(var + RMS_EPS) * w

        def _retnet_scan(q, k, v, gamma):
            qT = jnp.moveaxis(q, 1, 0)
            kT = jnp.moveaxis(k, 1, 0)
            vT = jnp.moveaxis(v, 1, 0)

            def step(S, qkv_t):
                q_t, k_t, v_t = qkv_t
                S = gamma[None, :, None, None] * S + k_t[..., :, None] * v_t[..., None, :]
                o_t = jnp.einsum('bhd,bhde->bhe', q_t, S)
                return (S, o_t)
            S0 = jnp.zeros((q.shape[0], H, d, d), q.dtype)
            _, yT = jax.lax.scan(step, S0, (qT, kT, vT))
            return jnp.moveaxis(yT, 0, 1)

        def _group_norm(y, gn_w, gn_b):
            mean = jnp.mean(y, axis=(1, 3), keepdims=True)
            var = jnp.var(y, axis=(1, 3), keepdims=True)
            yn = (y - mean) * jax.lax.rsqrt(var + GN_EPS)
            return yn * gn_w.reshape(1, 1, H, d) + gn_b.reshape(1, 1, H, d)
        key = jax.random.key(seed)
        ks = jax.random.split(key, 12)
        s = 0.02
        gammas = 1.0 - jnp.exp(jnp.linspace(math.log(0.1), math.log(0.001), H)).astype(jnp.float32)
        return {'x': jax.random.normal(ks[0], (B, T, D), dtype=jnp.float32), 'ln1_w': jnp.ones((D,), jnp.float32), 'ln2_w': jnp.ones((D,), jnp.float32), 'Wq': jax.random.normal(ks[1], (D, D), jnp.float32) * s, 'Wk': jax.random.normal(ks[2], (D, D), jnp.float32) * s, 'Wv': jax.random.normal(ks[3], (D, D), jnp.float32) * s, 'Wg': jax.random.normal(ks[4], (D, D), jnp.float32) * s, 'Wo': jax.random.normal(ks[5], (D, D), jnp.float32) * s, 'gamma': gammas, 'gn_w': jnp.ones((D,), jnp.float32), 'gn_b': jnp.zeros((D,), jnp.float32), 'gate_w': jax.random.normal(ks[6], (I, D), jnp.float32) * s, 'up_w': jax.random.normal(ks[7], (I, D), jnp.float32) * s, 'down_w': jax.random.normal(ks[8], (D, I), jnp.float32) * s}
    _L0_attn_all = _L0_attn_setup()
    _L0_attn_in = {k: v for k, v in _L0_attn_all.items() if k in ('ln1_w', 'ln2_w', 'Wq', 'Wk', 'Wv', 'Wg', 'Wo', 'gamma', 'gn_w', 'gn_b', 'gate_w', 'up_w', 'down_w')}
    del _L0_attn_all

    def _L0_xattn_setup():
        import jax, jax.numpy as jnp
        import numpy as np
        D_MODEL = 128
        NUM_HEADS = 16
        D_K = D_MODEL // NUM_HEADS
        key = jax.random.key(seed)
        ks = jax.random.split(key, 7)
        B, S = (2, 256)
        query = jax.random.normal(ks[0], (B, S, D_MODEL), dtype=jnp.float32)
        key_t = jax.random.normal(ks[1], (B, S, D_MODEL), dtype=jnp.float32)
        value = jax.random.normal(ks[2], (B, S, D_MODEL), dtype=jnp.float32)
        lim = float(np.sqrt(6.0 / (D_MODEL + D_MODEL)))
        W_q = jax.random.uniform(ks[3], (D_MODEL, D_MODEL), jnp.float32, -lim, lim)
        W_k = jax.random.uniform(ks[4], (D_MODEL, D_MODEL), jnp.float32, -lim, lim)
        W_v = jax.random.uniform(ks[5], (D_MODEL, D_MODEL), jnp.float32, -lim, lim)
        W_o = jax.random.uniform(ks[6], (D_MODEL, D_MODEL), jnp.float32, -lim, lim)
        return {'query': query, 'key': key_t, 'value': value, 'W_q': W_q, 'W_k': W_k, 'W_v': W_v, 'W_o': W_o}
    _L0_xattn_all = _L0_xattn_setup()
    _L0_xattn_in = {k: v for k, v in _L0_xattn_all.items() if k in ('W_q', 'W_k', 'W_v', 'W_o')}
    del _L0_xattn_all

    def _L0_ffn_setup():
        import math
        import jax, jax.numpy as jnp
        import numpy as np
        E = 8
        TOPK = 2
        CF = 1.25
        EPS = 1e-05
        NEG = -1e+30

        def _layer_norm(x, gamma, beta):
            mu = jnp.mean(x, axis=-1, keepdims=True)
            var = jnp.mean((x - mu) ** 2, axis=-1, keepdims=True)
            return (x - mu) * jax.lax.rsqrt(var + EPS) * gamma + beta
        key = jax.random.key(seed)
        ks = jax.random.split(key, 8)
        B, S, H, F = (4, 256, 128, 512)
        hidden_states = jax.random.normal(ks[0], (B, S, H), jnp.float32)
        token_mask = jnp.ones((B, S), jnp.int32)
        Wr = jax.random.normal(ks[1], (H, E), jnp.float32) * 0.001
        br = jnp.zeros((E,), jnp.float32)
        W1 = jax.random.normal(ks[2], (E, H, F), jnp.float32) * (1.0 / np.sqrt(H))
        b1 = jax.random.normal(ks[3], (E, F), jnp.float32) * 0.01
        W2 = jax.random.normal(ks[4], (E, F, H), jnp.float32) * (1.0 / np.sqrt(F))
        b2 = jax.random.normal(ks[5], (E, H), jnp.float32) * 0.01
        gamma = jnp.ones((H,), jnp.float32)
        beta = jnp.zeros((H,), jnp.float32)
        return {'hidden_states': hidden_states, 'Wr': Wr, 'br': br, 'W1': W1, 'b1': b1, 'W2': W2, 'b2': b2, 'gamma': gamma, 'beta': beta, 'token_mask': token_mask}
    _L0_ffn_all = _L0_ffn_setup()
    _L0_ffn_in = {k: v for k, v in _L0_ffn_all.items() if k in ('Wr', 'br', 'W1', 'b1', 'W2', 'b2', 'gamma', 'beta', 'token_mask')}
    del _L0_ffn_all
    return {'x': x, 'ctx_1024': ctx_1024, 'L0_attn_ln1_w': _L0_attn_in['ln1_w'], 'L0_attn_ln2_w': _L0_attn_in['ln2_w'], 'L0_attn_Wq': _L0_attn_in['Wq'], 'L0_attn_Wk': _L0_attn_in['Wk'], 'L0_attn_Wv': _L0_attn_in['Wv'], 'L0_attn_Wg': _L0_attn_in['Wg'], 'L0_attn_Wo': _L0_attn_in['Wo'], 'L0_attn_gamma': _L0_attn_in['gamma'], 'L0_attn_gn_w': _L0_attn_in['gn_w'], 'L0_attn_gn_b': _L0_attn_in['gn_b'], 'L0_attn_gate_w': _L0_attn_in['gate_w'], 'L0_attn_up_w': _L0_attn_in['up_w'], 'L0_attn_down_w': _L0_attn_in['down_w'], 'L0_xattn_W_q': _L0_xattn_in['W_q'], 'L0_xattn_W_k': _L0_xattn_in['W_k'], 'L0_xattn_W_v': _L0_xattn_in['W_v'], 'L0_xattn_W_o': _L0_xattn_in['W_o'], 'L0_ffn_Wr': _L0_ffn_in['Wr'], 'L0_ffn_br': _L0_ffn_in['br'], 'L0_ffn_W1': _L0_ffn_in['W1'], 'L0_ffn_b1': _L0_ffn_in['b1'], 'L0_ffn_W2': _L0_ffn_in['W2'], 'L0_ffn_b2': _L0_ffn_in['b2'], 'L0_ffn_gamma': _L0_ffn_in['gamma'], 'L0_ffn_beta': _L0_ffn_in['beta'], 'L0_ffn_token_mask': _L0_ffn_in['token_mask']}

def reference(x, ctx_1024, L0_attn_ln1_w, L0_attn_ln2_w, L0_attn_Wq, L0_attn_Wk, L0_attn_Wv, L0_attn_Wg, L0_attn_Wo, L0_attn_gamma, L0_attn_gn_w, L0_attn_gn_b, L0_attn_gate_w, L0_attn_up_w, L0_attn_down_w, L0_xattn_W_q, L0_xattn_W_k, L0_xattn_W_v, L0_xattn_W_o, L0_ffn_Wr, L0_ffn_br, L0_ffn_W1, L0_ffn_b1, L0_ffn_W2, L0_ffn_b2, L0_ffn_gamma, L0_ffn_beta, L0_ffn_token_mask):
    import jax
    import jax.numpy as jnp

    def _L0_attn_ref(x, ln1_w, ln2_w, Wq, Wk, Wv, Wg, Wo, gamma, gn_w, gn_b, gate_w, up_w, down_w):
        import jax, jax.numpy as jnp
        import numpy as np
        import math
        B, T, D = (2, 256, 128)
        H = 16
        d = D // H
        I = 352
        RMS_EPS = 1e-06
        GN_EPS = 1e-05

        def _rmsnorm(x, w):
            var = jnp.mean(x * x, axis=-1, keepdims=True)
            return x * jax.lax.rsqrt(var + RMS_EPS) * w

        def _retnet_scan(q, k, v, gamma):
            qT = jnp.moveaxis(q, 1, 0)
            kT = jnp.moveaxis(k, 1, 0)
            vT = jnp.moveaxis(v, 1, 0)

            def step(S, qkv_t):
                q_t, k_t, v_t = qkv_t
                S = gamma[None, :, None, None] * S + k_t[..., :, None] * v_t[..., None, :]
                o_t = jnp.einsum('bhd,bhde->bhe', q_t, S)
                return (S, o_t)
            S0 = jnp.zeros((q.shape[0], H, d, d), q.dtype)
            _, yT = jax.lax.scan(step, S0, (qT, kT, vT))
            return jnp.moveaxis(yT, 0, 1)

        def _group_norm(y, gn_w, gn_b):
            mean = jnp.mean(y, axis=(1, 3), keepdims=True)
            var = jnp.var(y, axis=(1, 3), keepdims=True)
            yn = (y - mean) * jax.lax.rsqrt(var + GN_EPS)
            return yn * gn_w.reshape(1, 1, H, d) + gn_b.reshape(1, 1, H, d)
        Bx, Tx, Dx = x.shape
        h = _rmsnorm(x, ln1_w)
        q = (h @ Wq.T).reshape(Bx, Tx, H, d)
        k = (h @ Wk.T).reshape(Bx, Tx, H, d)
        v = (h @ Wv.T).reshape(Bx, Tx, H, d)
        g = jax.nn.sigmoid(h @ Wg.T)
        gam = jax.nn.sigmoid(gamma)
        y = _retnet_scan(q, k, v, gam)
        y = _group_norm(y, gn_w, gn_b).reshape(Bx, Tx, Dx)
        y = g * y
        x = x + y @ Wo.T
        h2 = _rmsnorm(x, ln2_w)
        mlp = jax.nn.silu(h2 @ gate_w.T) * (h2 @ up_w.T) @ down_w.T
        return x + mlp

    def _L0_xattn_ref(query, key, value, W_q, W_k, W_v, W_o):
        import jax, jax.numpy as jnp
        import numpy as np
        D_MODEL = 128
        NUM_HEADS = 16
        D_K = D_MODEL // NUM_HEADS
        B, S, _ = query.shape

        def proj(x, W):
            return (x @ W.T).reshape(B, -1, NUM_HEADS, D_K).transpose(0, 2, 1, 3)
        q = proj(query, W_q)
        k = proj(key, W_k)
        v = proj(value, W_v)
        scale = 1.0 / jnp.sqrt(jnp.asarray(D_K, q.dtype))
        scores = jnp.einsum('bhqd,bhkd->bhqk', q, k) * scale
        p_attn = jax.nn.softmax(scores, axis=-1)
        x = jnp.einsum('bhqk,bhkd->bhqd', p_attn, v)
        x = x.transpose(0, 2, 1, 3).reshape(B, S, D_MODEL)
        return x @ W_o.T

    def _L0_ffn_ref(hidden_states, Wr, br, W1, b1, W2, b2, gamma, beta, token_mask):
        import math
        import jax, jax.numpy as jnp
        import numpy as np
        E = 8
        TOPK = 2
        CF = 1.25
        EPS = 1e-05
        NEG = -1e+30

        def _layer_norm(x, gamma, beta):
            mu = jnp.mean(x, axis=-1, keepdims=True)
            var = jnp.mean((x - mu) ** 2, axis=-1, keepdims=True)
            return (x - mu) * jax.lax.rsqrt(var + EPS) * gamma + beta
        B, S, H = hidden_states.shape
        x = hidden_states.reshape(-1, H)
        N = x.shape[0]
        logits = x @ Wr + br
        top_vals, top_idx = jax.lax.top_k(logits, TOPK)
        w = jax.nn.softmax(top_vals, axis=-1)
        flat_idx = top_idx.reshape(-1)
        flat_tok = jnp.repeat(jnp.arange(N), TOPK)
        w_flat = w.reshape(-1)
        cap = max(int(math.ceil(N / E * CF)), 1)
        key_mat = jnp.where(flat_idx[None, :] == jnp.arange(E)[:, None], w_flat[None, :], NEG)
        kv, ki = jax.lax.top_k(key_mat, cap)
        valid = kv > NEG / 2
        tok = flat_tok[ki]
        gate = jnp.where(valid, w_flat[ki], 0.0)
        xe = x[tok]
        h1 = jnp.einsum('ech,ehf->ecf', xe, W1) + b1[:, None, :]
        h1 = jax.nn.gelu(h1, approximate=False)
        y = jnp.einsum('ecf,efh->ech', h1, W2) + b2[:, None, :]
        out = jnp.zeros_like(x).at[tok.reshape(-1)].add((y * gate[..., None]).reshape(-1, H))
        out = out.reshape(B, S, H) + hidden_states
        return _layer_norm(out, gamma, beta)
    x = _layernorm(x + _L0_attn_ref(x, L0_attn_ln1_w, L0_attn_ln2_w, L0_attn_Wq, L0_attn_Wk, L0_attn_Wv, L0_attn_Wg, L0_attn_Wo, L0_attn_gamma, L0_attn_gn_w, L0_attn_gn_b, L0_attn_gate_w, L0_attn_up_w, L0_attn_down_w), axis=-1)
    x = _layernorm(x + _L0_xattn_ref(x, ctx_1024, ctx_1024, L0_xattn_W_q, L0_xattn_W_k, L0_xattn_W_v, L0_xattn_W_o), axis=-1)
    x = _layernorm(x + _L0_ffn_ref(x, L0_ffn_Wr, L0_ffn_br, L0_ffn_W1, L0_ffn_b1, L0_ffn_W2, L0_ffn_b2, L0_ffn_gamma, L0_ffn_beta, L0_ffn_token_mask), axis=-1)
    return x

_drawn_inputs = setup_inputs


def setup_inputs(seed=0):
    import zlib

    import numpy as np

    out = dict(_drawn_inputs(seed))
    spreads = {'L0_attn_ln1_w': (1.0, 0.6),
     'L0_attn_ln2_w': (1.0, 0.6),
     'L0_attn_gn_w': (1.0, 0.6),
     'L0_attn_gn_b': (0.0, 0.8),
     'L0_ffn_br': (0.0, 0.1),
     'L0_ffn_gamma': (1.0, 0.2),
     'L0_ffn_beta': (0.0, 0.1)}
    factors = {'L0_attn_Wg': 5.047,
     'L0_attn_gamma': 64.0,
     'L0_attn_gate_w': 6.069,
     'L0_attn_up_w': 6.408,
     'L0_attn_down_w': 7.011,
     'L0_ffn_b1': 57.137,
     'L0_ffn_b2': 41.274}
    for name, (base, spread) in spreads.items():
        noise = np.random.default_rng([zlib.crc32(name.encode()), seed]).standard_normal(out[name].shape)
        drawn = base * np.exp(spread * noise) if base else spread * noise
        out[name] = jnp.asarray(drawn.astype(out[name].dtype))
    for name, factor in factors.items():
        out[name] = (out[name] * factor).astype(out[name].dtype)
    return out
```

```python
from contextlib import ExitStack

import numpy as np

import concourse.bass as bass
from concourse import mybir

F32 = mybir.dt.float32
BF16 = mybir.dt.bfloat16
I32 = mybir.dt.int32
ALU = mybir.AluOpType
ACT = mybir.ActivationFunctionType
AX = mybir.AxisListType.X

P = 128
NB, T, D = 4, 512, 128
N = NB * T
NT = N // P
TB = T // P
H = 16
DH = D // H
HG = 4
HJ = H // HG
INNER = 352
MB = [128, 128, 96]
KC = 32
NE, TOPK = 8, 2
FF = 512
FB = FF // P
CAP = (N * 5 // 4 + NE - 1) // NE
CH = [128, 128, CAP - 256]
SLOT_A, SLOT_B = 32, CAP // 32
FAR = 4096
BITS = 30
ROUNDS = BITS // 2
PV = 32 + HJ
SCALE = float(DH) ** -0.5

CONST = {}
_at = 0
for _name, _n in [("ident", 128), ("blockdiag", 128), ("headmean", 128), ("causal", 128), ("dist", 128),
                  ("after", 128), ("same_expert", 128), ("earlier_tile", 128), ("left", 1), ("quad", HJ),
                  ("head", H), ("keyhead", HJ), ("iota_a", SLOT_A), ("iota_b", SLOT_B), ("token", NT),
                  ("iota_e", NE), ("eps6", 1), ("eps5", 1), ("ones", 128)]:
    CONST[_name] = (_at, _n)
    _at += _n
NCONST = _at

W1COLS = {n: (i * 128, 128) for i, n in enumerate(["q", "k", "v", "g", "o"])}
W2COLS = {}
_at = 0
for _name, _n in [("gate", INNER), ("up", INNER), ("down", 3 * 128), ("xq", 128), ("xk", 128), ("xv", 128),
                  ("xo", 128), ("ctx", NB * KC), ("ctxrep", NB * HJ * KC), ("router", NE)]:
    W2COLS[_name] = (_at, _n)
    _at += _n
NW2 = _at
VEC = {}
_at = 0
for _name, _n in [("ln1", 1), ("ln2", 1), ("gnw", 1), ("gnb", 1), ("gamma_col", 1), ("gamma_row", H),
                  ("br", NE), ("fg", D), ("fb", D), ("b1", NE * FB), ("b2", NE * D)]:
    VEC[_name] = (_at, _n)
    _at += _n
NVEC = _at


def plan_psum():
    jobs = []

    def job(key, sem, value):
        jobs.append((key, sem, value))

    job(("ck",), "ck_ready", 1)
    for b in range(NB):
        job(("cv", b), "cv_ready", b + 1)
    for b in range(NB):
        job(("hT", b), "hT_ready", b + 1)
    for b in range(NB):
        job(("q", b), "q_ready", b + 1)
        job(("k", b), "kexp_ready", b + 1)
        job(("kt", b), "kd_ready", b + 1)
        job(("v", b), "v_ready", b + 1)
    for b in range(NB):
        job(("g", b), "g_ready", b + 1)
    for s in range(NT + 4):
        if s < NT:
            for g in range(HG):
                job(("s", s, g), "p_ready", HG * s + g + 1)
            if s % TB < TB - 1:
                job(("kv", s), "state_ready", (TB - 1) * (s // TB) + s % TB + 1)
        if s >= 5 and s % TB == 1:
            job(("gn", s // TB - 1), "gn_var", s // TB)
        if s >= 7 and s % TB == 3:
            job(("o", s // TB - 1), "x1_ready", s // TB)
    for b in range(NB):
        job(("h2T", b), "h2T_ready", b + 1)
    for b in range(NB + 1):
        if b < NB:
            for m in range(3):
                job(("ga", b, m), "silu_ready", 3 * b + m + 1)
                job(("up", b, m), "a_ready", 3 * b + m + 1)
        if b:
            job(("dn", b - 1), "r_ready", b)
    for b in range(NB):
        job(("x2T", b), "x2T_ready", b + 1)
        job(("xq", b), "xq_ready", b + 1)
    for s in range(NT + 5):
        if s < NT:
            job(("xs", s), "sd_ready", s + 1)
        if 2 <= s < NT + 2:
            job(("pT", s - 2), "pT_ready", s - 1)
        if 3 <= s < NT + 3:
            job(("pv", s - 3), "att_ready", s - 2)
        if s >= 8 and s % TB == 0:
            job(("oT", s // TB - 2), "oT_ready", s // TB - 1)
    for b in range(NB):
        job(("xo", b), "r2_ready", b + 1)
    for b in range(NB):
        job(("x3T", b), "x3T_ready", b + 1)
    job(("rt",), "logits_ready", 1)
    job(("keyT",), "key_ready", 1)
    for r in range(ROUNDS):
        job(("cnt", r), "thr_ready", r + 2)
    job(("gt",), "eq_room", 1)
    job(("sel",), "pos_ready", 1)
    job(("posT",), "posT_ready", 1)
    job(("idx",), "gates_ready", 4)
    for e in range(NE):
        for c in range(3):
            job(("xeT", e, c), "xeT_ready", 3 * e + c + 1)
        for f in range(FB):
            job(("h1", e, f), "h1_ready", FB * e + f + 1)
        for c in range(3):
            job(("y", e, c), "ye_ready", 3 * e + c + 1)
    return jobs


def decoder_layer(nc, x, consts, bits, w1, w2, vecs, ew1, ew2, out):
    ctx = ExitStack()
    with ctx:
        def sb(name, shape, dt=F32):
            return ctx.enter_context(nc.sbuf_tensor(name, shape, dt))

        sems = {}

        def sem(name):
            if name not in sems:
                sems[name] = ctx.enter_context(nc.semaphore(name))
            return sems[name]

        ring = [ctx.enter_context(nc.psum_tensor(f"ring{i}", [P, 512], F32)) for i in range(6)]
        ybank = [ctx.enter_context(nc.psum_tensor(f"ybank{i}", [P, 512], F32)) for i in range(2)]
        jobs = plan_psum()
        seq = {key: n for n, (key, _, _) in enumerate(jobs)}

        def bank(key):
            return ring[seq[key] % 6]

        def room(pe, key):
            n = seq[key] - 6
            if n >= 0:
                pe.wait_ge(sem(jobs[n][1]), jobs[n][2])

        bank_full = [sem(f"bank_full{i}") for i in range(6)]

        def filled(eng, key):
            eng.wait_ge(bank_full[seq[key] % 6], seq[key] // 6 + 1)

        rows = nc.dram_tensor("rows_dram", [N, D], F32, kind="Internal").ap()
        acc = nc.dram_tensor("acc_dram", [N, D], F32, kind="Internal").ap()

        X = sb("X", [P, NT, D])
        Hb = sb("Hb", [P, NT, D])
        HT = sb("HT", [P, N])
        QT = sb("QT", [P, N])
        BIG = sb("BIG", [P, HJ * N])
        QD = sb("QD", [P, N])
        KD = sb("KD", [P, NT, D])
        V = sb("V", [P, NT, D])
        VZ = sb("VZ", [P, 4, H * D])
        GT = sb("GT", [P, N])
        M = sb("M", [P, H * P])
        X1 = sb("X1", [P, NT, D])
        PB = sb("PB", [P, 8, 512])
        SQ = sb("SQ", [P, 2, 512])
        ST = sb("ST", [P, NB * (TB - 1), D])
        YN = sb("YN", [P, 2, 512])
        YG = sb("YG", [P, 2, 512])
        C = sb("C", [P, NCONST])
        W1 = sb("W1", [P, 5 * 128])
        W2 = sb("W2", [P, NW2])
        VC = sb("VC", [P, NVEC])
        BT = sb("BT", [P, 3 * ROUNDS], I32)
        DQ = sb("DQ", [P, P])
        DK = sb("DK", [P, P])
        small = sb("small", [P, 256])
        mv = sb("mv", [P, NT, 2])
        stats = sb("stats", [P, NT, 6])
        rstd = sb("rstd", [P, NT])
        lnv = sb("lnv", [P, NT])
        CK = sb("CK", [P, NB * KC])
        VX = sb("VX", [P, NB, HG, PV])

        R = QD[:].rearrange("p (t d) -> p t d", d=D)
        X2 = KD
        XX = VZ[:, 3, :].rearrange("p (t d) -> p t d", d=D)
        ATT = V
        X3 = GT[:].rearrange("p (t d) -> p t d", d=D)
        OT = M
        KX = VZ[:, 0, :].rearrange("p (b c) -> p b c", b=NB)
        SD = VZ[:, 1, :].rearrange("p (s c) -> p s c", s=4)
        PT = VZ[:, 2, :].rearrange("p (s c) -> p s c", s=4)
        A = PB[:, 0:6, :]
        SG = YN
        EW1 = BIG[:, 0:NE * FF].rearrange("p (e f) -> p e f", e=NE)
        EW2 = BIG[:, NE * FF:2 * NE * FF].rearrange("p (e f d) -> p e f d", e=NE, d=D)

        def const(name, a=0, n=None):
            at, width = CONST[name]
            return C[:, at + a:at + a + (width if n is None else n)]

        def wa(name, a=0, n=None):
            at, width = W1COLS[name]
            return W1[:, at + a:at + a + (width if n is None else n)]

        def wb(name, a=0, n=None):
            at, width = W2COLS[name]
            return W2[:, at + a:at + a + (width if n is None else n)]

        def vec(name, a=0, n=None):
            at, width = VEC[name]
            return VC[:, at + a:at + a + (width if n is None else n)]

        def tiles(b):
            return slice(TB * b, TB * b + TB)

        def toks(b):
            return slice(T * b, T * b + T)

        def by_tile(ap):
            return ap.rearrange("p (t d) -> p t d", d=D)

        e_row, lg_row = small[:, 0:H], small[:, 16:16 + H]
        e_col, lg_col, g128 = small[:, 32:33], small[:, 33:34], small[:, 34:35]
        gs = small[:, 36:68].rearrange("p (b c) -> p b c", b=NB)
        xmax = small[:, 80:112].rearrange("p (s h) -> p s h", s=2)
        xden = small[:, 112:144].rearrange("p (s h) -> p s h", s=2)

        RB = PB[:, 0:2, :].rearrange("p s c -> p (s c)")
        logits = RB[:, 0:128].rearrange("p (t e) -> p t e", e=NE)
        rtmp = RB[:, 128:256].rearrange("p (t e) -> p t e", e=NE)
        pick1 = RB[:, 256:384].rearrange("p (t e) -> p t e", e=NE)
        pick2 = RB[:, 384:512].rearrange("p (t e) -> p t e", e=NE)
        key_et = RB[:, 512:640].rearrange("p (e t) -> p e t", e=NE)
        keyT = RB[:, 640:768]
        seltmp = RB[:, 768:896]
        selT = RB[:, 896:1024]
        RC = PB[:, 2, :]
        top = RC[:, 0:96].rearrange("p (n t) -> p n t", t=NT)
        thr = RC[:, 96:100]
        cand = RC[:, 100:104]
        nums = RC[:, 104:112]
        eqT = RC[:, 112:240]
        zeroT = RC[:, 240:368]
        posT = PB[:, 3, 0:128]
        posI = PB[:, 3, 128:256].bitcast(I32)
        posA = PB[:, 3, 256:384]
        posB = PB[:, 3, 384:512]
        onesb = sb("onesb", [P, P], BF16)
        cntb = sb("cntb", [P, 4], BF16)
        OA = VZ[:, 0:2, :].rearrange("p s (n a) -> p (s n) a", a=SLOT_A)
        OB = VZ[:, 2, 0:1280].rearrange("p (n b) -> p n b", b=SLOT_B)
        OV = X1[:].rearrange("p t d -> p (t d)")[:, 0:1280].rearrange("p (n b) -> p n b", b=SLOT_B)
        OG = Hb[:].rearrange("p t d -> p (t d)")[:, 0:1280].rearrange("p (n b) -> p n b", b=SLOT_B)
        idx = sb("idx", [P, NE, 3], I32)
        gates = sb("gates", [P, NE, 3])
        XE = QT[:, 0:3 * 3 * D].rearrange("p (s c d) -> p s c d", s=3, d=D)
        XET = QT[:, 1152:1152 + 2 * CAP].rearrange("p (s c) -> p s c", s=2)
        H1A = [M[:, 0:FB * CAP].rearrange("p (f c) -> p f c", f=FB),
               QD[:, 0:FB * CAP].rearrange("p (f c) -> p f c", f=FB)]
        YE = V[:].rearrange("p t d -> p (t d)")[:, 0:6 * D].rearrange("p (s d) -> p s d", d=D)
        AM = KD
        FIN = HT[:].rearrange("p (t d) -> p t d", d=D)

        block = ctx.enter_context(nc.Block())

        @block.sync
        def _(sp):
            sp.dma_start(C[:], consts).then_inc(sem("in_const"), 16)
            xv = x.rearrange("(t p) d -> p t d", p=P)
            for b in range(NB):
                sp.dma_start(X[:, tiles(b), :], xv[:, tiles(b), :]).then_inc(sem(f"in_x{b}"), 16)
                if b == 0:
                    sp.dma_start(VC[:], vecs).then_inc(sem("in_vec"), 16)
                    sp.dma_start(W1[:], w1).then_inc(sem("in_w1"), 16)
            sp.dma_start(W2[:], w2).then_inc(sem("in_w2"), 16)
            sp.dma_start(BT[:], bits).then_inc(sem("in_bits"), 16)
            sp.wait_ge(sem("av_done"), NT)
            sp.dma_start(EW1, ew1).then_inc(sem("in_ew"), 16)
            sp.dma_start(EW2, ew2).then_inc(sem("in_ew"), 16)
            for b in range(NB):
                sp.wait_ge(sem("x3_ready"), b + 1)
                for dst in (rows, acc):
                    sp.dma_start(dst.rearrange("(t p) d -> p t d", p=P)[:, tiles(b), :],
                                 X3[:, tiles(b), :]).then_inc(sem("x3_stored"), 16)
            sp.wait_ge(sem("added"), 16 * 3 * NE)
            for b in range(NB):
                sp.dma_start(AM[:, tiles(b), :], acc.rearrange("(t p) d -> p t d", p=P)[:, tiles(b), :]).then_inc(
                    sem(f"in_sum{b}"), 16)
            for b in range(NB):
                sp.wait_ge(sem("fin_ready"), b + 1)
                sp.dma_start(out.rearrange("(t p) d -> p t d", p=P)[:, tiles(b), :],
                             FIN[:, tiles(b), :]).then_inc(sem("stored"), 16)
            sp.wait_ge(sem("stored"), 16 * NB)

        @block.gpsimd
        def _(pool):
            nc.gpsimd.memset(VZ[:], 0.0).then_inc(sem("vz_zero"), 1)
            pool.wait_ge(sem("vz_zero"), 1)
            def q_decay(b):
                pool.wait_ge(sem("q_ready"), b + 1)
                pool.wait_ge(sem("dq_ready"), 1)
                nc.gpsimd.tensor_tensor(by_tile(QD[:, toks(b)]), by_tile(QT[:, toks(b)]),
                                        DQ[:].unsqueeze(1).to_broadcast([P, TB, P]), ALU.mult).then_inc(
                                            sem("qd_ready"), 1)

            def spread_v(s):
                pool.wait_ge(sem("v_ready"), s // TB + 1)
                if s >= 4:
                    pool.wait_ge(sem("av_done"), s - 3)
                if s >= 4:
                    pool.wait_ge(sem("vz_ready"), s - 3)
                dst = VZ[:, s % 4, 0:H * D].rearrange("p (h c) -> p h c", h=H)
                strip = bass.AP(dst.tensor, dst.offset, [list(dst.ap[0]), [D + DH, H], [1, DH]])
                nc.gpsimd.tensor_copy(strip, V[:, s, :].rearrange("p (h e) -> p h e", h=H)).then_inc(
                    sem("vz_ready"), 1)

            for b in range(NB):
                q_decay(b)
                if b == 0:
                    for s in range(4):
                        spread_v(s)
            for s in range(4, NT):
                spread_v(s)
            for b in range(NB):
                pool.wait_ge(sem("x1_ready"), b + 1)
                pool.wait_ge(sem("h2_ready"), b + 1)
                nc.gpsimd.tensor_tensor(XX[:, tiles(b), :], X[:, tiles(b), :], X1[:, tiles(b), :],
                                        ALU.add).then_inc(sem("xx_ready"), 1)
            pool.wait_ge(sem("x3T_ready"), NB)
            nc.gpsimd.memset(XE, 0.0).then_inc(sem("xe_zero"), 1)
            pool.wait_ge(sem("xe_zero"), 1)
            pool.wait_ge(sem("x3_stored"), 16 * 2 * NB)
            pool.wait_ge(sem("idx_ready"), 4)

            def gather(e):
                if e >= 3:
                    pool.wait_ge(sem("xeT_ready"), 3 * (e - 2))
                for c in range(3):
                    nc.gpsimd.indirect_dma_start(
                        out=XE[0:CH[c], e % 3, c, :], out_offset=None, in_=rows,
                        in_offset=bass.IndirectOffsetOnAxis(ap=idx[0:CH[c], e, c:c + 1], axis=0),
                        bounds_check=N - 1, oob_is_err=False).then_inc(sem(f"gathered{e % 3}"), 16)

            def scatter(e):
                for c in range(3):
                    pool.wait_ge(sem("ye_ready"), 3 * e + c + 1)
                    if 3 * e + c:
                        pool.wait_ge(sem("added"), 16 * (3 * e + c))
                    nc.gpsimd.indirect_dma_start(
                        out=acc, out_offset=bass.IndirectOffsetOnAxis(ap=idx[0:CH[c], e, c:c + 1], axis=0),
                        in_=YE[0:CH[c], 3 * (e % 2) + c, :], in_offset=None,
                        bounds_check=N - 1, oob_is_err=False, compute_op=ALU.add).then_inc(sem("added"), 16)

            gather(0)
            gather(1)
            for e in range(NE):
                if e + 2 < NE:
                    gather(e + 2)
                scatter(e)

        @block.tensor
        def _(pe):
            def transposes(key, src, n=TB):
                room(pe, key)
                for t in range(n):
                    last = nc.tensor.transpose(bank(key)[:, t * P:(t + 1) * P], src(t), const("ident"))
                last.then_inc(bank_full[seq[key] % 6], 1)

            def done(key, last):
                last.then_inc(bank_full[seq[key] % 6], 1)

            pe.wait_ge(sem("in_w2"), 16)
            room(pe, ("ck",))
            done(("ck",), nc.tensor.matmul(bank(("ck",))[:, 0:NB * KC], wb("xk"), wb("ctx"), start=True, stop=True))
            for b in range(NB):
                key = ("cv", b)
                room(pe, key)
                done(key, nc.tensor.matmul(bank(key)[:, 0:D], wb("ctxrep", b * P, P), wb("xv"), start=True, stop=True))

            pe.wait_ge(sem("in_const"), 16)
            for b in range(NB):
                pe.wait_ge(sem("h_ready"), b + 1)
                transposes(("hT", b), lambda t: Hb[:, TB * b + t, :])
            pe.wait_ge(sem("in_w1"), 16)

            def token_layout(key, b, w):
                room(pe, key)
                for t in range(TB):
                    s = TB * b + t
                    last = nc.tensor.matmul(bank(key)[:, t * D:(t + 1) * D], HT[:, s * P:(s + 1) * P], w,
                                            start=True, stop=True)
                done(key, last)

            for b in range(NB):
                pe.wait_ge(sem("hT_ready"), b + 1)
                for n in "qk":
                    room(pe, (n, b))
                    done((n, b), nc.tensor.matmul(bank((n, b))[:], wa(n), HT[:, toks(b)], start=True, stop=True))
                token_layout(("kt", b), b, wa("k"))
                token_layout(("v", b), b, wa("v"))
            for b in range(NB):
                key = ("g", b)
                room(pe, key)
                done(key, nc.tensor.matmul(bank(key)[:], wa("g"), HT[:, toks(b)], start=True, stop=True))

            def scores(s):
                pe.wait_ge(sem("kexp_ready"), s // TB + 1)
                pe.wait_ge(sem("q_ready"), s // TB + 1)
                for g in range(HG):
                    key = ("s", s, g)
                    room(pe, key)
                    q = slice(32 * g, 32 * g + 32)
                    for j in range(HJ):
                        last = nc.tensor.matmul(bank(key)[:, j * P:(j + 1) * P],
                                                BIG[q, j * N + s * P:j * N + (s + 1) * P],
                                                QT[q, s * P:(s + 1) * P], start=True, stop=True)
                    done(key, last)

            def chunk_state(s):
                key = ("kv", s)
                pe.wait_ge(sem("kd_ready"), s // TB + 1)
                pe.wait_ge(sem("v_ready"), s // TB + 1)
                room(pe, key)
                done(key, nc.tensor.matmul(bank(key)[:, 0:D], KD[:, s, :], V[:, s, :], start=True, stop=True))

            def retained(s):
                b, c = s // TB, s % TB
                if c == 0 and b >= 2:
                    pe.wait_ge(sem("yn_ready"), b - 1)
                y = ybank[b % 2][:, c * P:(c + 1) * P]
                if c:
                    pe.wait_ge(sem("state_ready"), (TB - 1) * b + c)
                    pe.wait_ge(sem("qd_ready"), b + 1)
                    nc.tensor.matmul(y, ST[:, (TB - 1) * b + c - 1, :], QD[:, s * P:(s + 1) * P],
                                     start=True, stop=False)
                pe.wait_ge(sem("vz_ready"), s + 1)
                for g in range(HG):
                    pe.wait_ge(sem("p_ready"), HG * s + g + 1)
                    for j in range(HJ):
                        h = HJ * g + j
                        last = nc.tensor.matmul(y, VZ[:, s % 4, h * D:(h + 1) * D],
                                                PB[:, HG * (s % 2) + g, j * P:(j + 1) * P],
                                                start=(c == 0 and h == 0), stop=(h == H - 1))
                last.then_inc(sem("av_done"), 1)

            for s in range(NT + 4):
                if s < NT:
                    scores(s)
                    if s % TB < TB - 1:
                        chunk_state(s)
                if 1 <= s <= NT:
                    retained(s - 1)
                if s >= 5 and s % TB == 1:
                    b = s // TB - 1
                    key = ("gn", b)
                    room(pe, key)
                    pe.wait_ge(sem("gn_part"), b + 1)
                    done(key, nc.tensor.matmul(bank(key)[:, 0:2], const("headmean"), gs[:, b, 0:2],
                                               start=True, stop=True))
                if s >= 7 and s % TB == 3:
                    b = s // TB - 1
                    key = ("o", b)
                    room(pe, key)
                    pe.wait_ge(sem("yg_ready"), b + 1)
                    for t in range(TB):
                        last = nc.tensor.matmul(bank(key)[:, t * D:(t + 1) * D],
                                                YG[:, b % 2, t * P:(t + 1) * P], wa("o"), start=True, stop=True)
                    done(key, last)

            for b in range(NB):
                pe.wait_ge(sem("h2_ready"), b + 1)
                transposes(("h2T", b), lambda t: Hb[:, TB * b + t, :])
            for b in range(NB + 1):
                if b < NB:
                    pe.wait_ge(sem("h2T_ready"), b + 1)
                    for m in range(3):
                        for name, w in (("ga", "gate"), ("up", "up")):
                            key = (name, b, m)
                            room(pe, key)
                            done(key, nc.tensor.matmul(bank(key)[0:MB[m], :], wb(w, 128 * m, MB[m]),
                                                       HT[:, toks(b)], start=True, stop=True))
                if b:
                    key = ("dn", b - 1)
                    room(pe, key)
                    pe.wait_ge(sem("a_ready"), 3 * b)
                    for t in range(TB):
                        for m in range(3):
                            last = nc.tensor.matmul(bank(key)[:, t * D:(t + 1) * D],
                                                    A[0:MB[m], 3 * ((b - 1) % 2) + m, t * P:(t + 1) * P],
                                                    wb("down", 128 * m, 128)[0:MB[m], :],
                                                    start=(m == 0), stop=(m == 2))
                    last.then_inc(bank_full[seq[key] % 6], 1)

            for b in range(NB):
                pe.wait_ge(sem("x2_ready"), b + 1)
                transposes(("x2T", b), lambda t: X2[:, TB * b + t, :])
                key = ("xq", b)
                room(pe, key)
                pe.wait_ge(sem("x2T_ready"), b + 1)
                done(key, nc.tensor.matmul(bank(key)[:], wb("xq"), HT[:, toks(b)], start=True, stop=True))
            pe.wait_ge(sem("kx_ready"), NB)
            pe.wait_ge(sem("vx_ready"), 1)
            for s in range(NT + 5):
                if s < NT:
                    key = ("xs", s)
                    pe.wait_ge(sem("xq_ready"), s // TB + 1)
                    room(pe, key)
                    done(key, nc.tensor.matmul(bank(key)[:], QT[:, s * P:(s + 1) * P], KX[:, s // TB, :],
                                               start=True, stop=True))
                if 2 <= s < NT + 2:
                    pe.wait_ge(sem("xp_ready"), s - 1)
                    transposes(("pT", s - 2), lambda t: SD[:, (s - 2) % 4, t * P:(t + 1) * P])
                if 3 <= s < NT + 3:
                    key = ("pv", s - 3)
                    room(pe, key)
                    pe.wait_ge(sem("pT_ready"), s - 2)
                    for g in range(HG):
                        last = nc.tensor.matmul(bank(key)[:, g * PV:(g + 1) * PV],
                                                PT[:, (s - 3) % 4, g * P:(g + 1) * P],
                                                VX[:, (s - 3) // TB, g, :], start=True, stop=True)
                    done(key, last)
                if s >= 8 and s % TB == 0:
                    b = s // TB - 2
                    pe.wait_ge(sem("att_ready"), TB * (b + 1))
                    transposes(("oT", b), lambda t: ATT[:, TB * b + t, :])
            for b in range(NB):
                key = ("xo", b)
                room(pe, key)
                pe.wait_ge(sem("oT_ready"), b + 1)
                for t in range(TB):
                    s = TB * b + t
                    last = nc.tensor.matmul(bank(key)[:, t * D:(t + 1) * D], OT[:, s * P:(s + 1) * P], wb("xo"),
                                            start=True, stop=True)
                done(key, last)
            for b in range(NB):
                pe.wait_ge(sem("x3_ready"), b + 1)
                transposes(("x3T", b), lambda t: X3[:, TB * b + t, :])

            room(pe, ("rt",))
            pe.wait_ge(sem("x3T_ready"), NB)
            for s in range(NT):
                last = nc.tensor.matmul(bank(("rt",))[:, s * NE:(s + 1) * NE], HT[:, s * P:(s + 1) * P],
                                        wb("router"), start=True, stop=True)
            done(("rt",), last)
            pe.wait_ge(sem("gate_ready"), 1)
            transposes(("keyT",), lambda t: key_et.rearrange("p e t -> p (e t)"), 1)
            for r in range(ROUNDS):
                key = ("cnt", r)
                room(pe, key)
                pe.wait_ge(sem("cnt_ready"), r + 1)
                done(key, nc.tensor.matmul(bank(key)[:, 0:3], onesb[:], cntb[:, 0:3], start=True, stop=True))
            room(pe, ("gt",))
            pe.wait_ge(sem("rows_ready"), 1)
            nc.tensor.matmul(bank(("gt",))[:, 0:1], const("same_expert"), nums[:, 0:1], start=True, stop=True)
            done(("gt",), nc.tensor.matmul(bank(("gt",))[:, 1:2], const("earlier_tile"), nums[:, 1:2],
                                           start=True, stop=True))
            room(pe, ("sel",))
            pe.wait_ge(sem("sel_ready"), 1)
            done(("sel",), nc.tensor.matmul(bank(("sel",))[:, 0:1], const("earlier_tile"), nums[:, 4:5],
                                            start=True, stop=True))
            pe.wait_ge(sem("pos_ready"), 1)
            transposes(("posT",), lambda t: posT, 1)
            room(pe, ("idx",))
            pe.wait_ge(sem("onehot_ready"), 1)
            pe.wait_ge(sem("ov_ready"), 1)
            for e in range(NE):
                for v, src in enumerate((OV, OG)):
                    for t in range(NT):
                        n = e * NT + t
                        last = nc.tensor.matmul(bank(("idx",))[0:SLOT_A, (2 * e + v) * SLOT_B:(2 * e + v + 1) * SLOT_B],
                                                OA[:, n, :], src[:, n, :], start=(t == 0), stop=(t == NT - 1))
            done(("idx",), last)

            pe.wait_ge(sem("in_ew"), 32)
            for e in range(NE):
                for c in range(3):
                    key = ("xeT", e, c)
                    room(pe, key)
                    pe.wait_ge(sem(f"gathered{e % 3}"), 16 * 3 * (e // 3 + 1))
                    done(key, nc.tensor.transpose(bank(key)[:, 0:CH[c]], XE[0:CH[c], e % 3, c, :],
                                                  const("ident")[0:CH[c], 0:CH[c]]))
                pe.wait_ge(sem("xeT_ready"), 3 * e + 3)
                for f in range(FB):
                    key = ("h1", e, f)
                    room(pe, key)
                    done(key, nc.tensor.matmul(bank(key)[:, 0:CAP], EW1[:, e, f * P:(f + 1) * P], XET[:, e % 2, :],
                                               start=True, stop=True))
                pe.wait_ge(sem("h1_ready"), FB * (e + 1))
                for c in range(3):
                    key = ("y", e, c)
                    room(pe, key)
                    o = bank(key)[0:CH[c], 0:D]
                    for f in range(FB):
                        nc.tensor.matmul(o, H1A[e % 2][:, f, c * P:c * P + CH[c]], EW2[:, e, f, :],
                                         start=(f == 0), stop=False)
                    done(key, nc.tensor.matmul(o, const("ones", 0, CH[c])[0:1, :], vec("b2", e * D, D)[0:1, :],
                                               start=False, stop=True))

        @block.scalar
        def _(act):
            chain = [0]

            def link(ins):
                chain[0] += 1
                ins.then_inc(sem("act_step"), 1)
                act.wait_ge(sem("act_step"), chain[0])

            def inv_sqrt(dst, tmp, src, name, scale, eps):
                link(nc.scalar.activation(tmp, src, ACT.Ln, bias=const(eps), scale=scale))
                nc.scalar.activation(dst, tmp, ACT.Exp, scale=-0.5).then_inc(sem(name), 1)

            act.preload_act_table_set("natural_log_exp_and_others")
            act.wait_ge(sem("in_const"), 16)
            act.wait_ge(sem("in_vec"), 16)
            nc.scalar.activation(e_row, vec("gamma_row"), ACT.Exp, scale=-1.0).then_inc(sem("e_ready"), 1)
            nc.scalar.activation(e_col, vec("gamma_col"), ACT.Exp, scale=-1.0).then_inc(sem("e_ready"), 1)
            act.wait_ge(sem("e1_ready"), 2)
            link(nc.scalar.activation(lg_row, e_row, ACT.Ln))
            link(nc.scalar.activation(lg_col, e_col, ACT.Ln))
            link(nc.scalar.mul(small[:, 144:145], lg_col, -1.0))
            nc.scalar.activation(g128, lg_col, ACT.Exp, scale=-float(P)).then_inc(sem("g128_ready"), 1)
            nc.scalar.activation(DQ[:], const("after"), ACT.Exp, scale=small[:, 144:145]).then_inc(sem("dq_ready"), 1)
            link(nc.scalar.mul(small[:, 145:146], const("left"), -1.0))
            nc.scalar.activation(DK[:].rearrange("p (h d) -> p h d", h=H),
                                 lg_row.unsqueeze(2).to_broadcast([P, H, DH]), ACT.Exp,
                                 scale=small[:, 145:146]).then_inc(sem("dk_ready"), 1)
            act.wait_ge(sem("logmask_ready"), 1)
            nc.scalar.activation(M[:], M[:], ACT.Exp, scale=-1.0).then_inc(sem("mask_exp"), 1)

            for b in range(NB):
                act.wait_ge(sem("rms_sum"), b + 1)
                inv_sqrt(rstd[:, tiles(b)], lnv[:, tiles(b)], mv[:, tiles(b), 0], "rms_rstd", 1.0 / D, "eps6")

            for b in range(NB):
                filled(act, ("hT", b))
                nc.scalar.activation(HT[:, toks(b)], bank(("hT", b))[:], ACT.Copy,
                                     scale=vec("ln1")).then_inc(sem("hT_ready"), 1)
            for b in range(NB):
                filled(act, ("q", b))
                nc.scalar.copy(QT[:, toks(b)], bank(("q", b))[:]).then_inc(sem("q_ready"), 1)
                filled(act, ("v", b))
                nc.scalar.copy(V[:, tiles(b), :], by_tile(bank(("v", b))[:])).then_inc(sem("v_ready"), 1)
            for b in range(NB):
                filled(act, ("g", b))
                nc.scalar.activation(GT[:, toks(b)], bank(("g", b))[:], ACT.Sigmoid).then_inc(sem("g_ready"), 1)
            for b in range(NB):
                act.wait_ge(sem("gn_var"), b + 1)
                inv_sqrt(gs[:, b, 5:6], gs[:, b, 4:5], gs[:, b, 3:4], "gn_rstd", -1.0, "eps5")
                act.wait_ge(sem("gn_affine"), b + 1)
                if b >= 2:
                    act.wait_ge(sem("yg_ready"), b - 1)
                nc.scalar.activation(YN[:, b % 2, :], ybank[b % 2][:], ACT.Identity, bias=gs[:, b, 7:8],
                                     scale=gs[:, b, 6:7]).then_inc(sem("yn_ready"), 1)
            for b in range(NB):
                act.wait_ge(sem("rms2_sum"), b + 1)
                inv_sqrt(rstd[:, tiles(b)], lnv[:, tiles(b)], mv[:, tiles(b), 0], "rms2_rstd", 1.0 / D, "eps6")
            for b in range(NB):
                filled(act, ("h2T", b))
                nc.scalar.activation(HT[:, toks(b)], bank(("h2T", b))[:], ACT.Copy,
                                     scale=vec("ln2")).then_inc(sem("h2T_ready"), 1)
            act.wait_ge(sem("yg_ready"), NB)
            for b in range(NB):
                for m in range(3):
                    n = 3 * b + m
                    filled(act, ("ga", b, m))
                    if n >= 2:
                        act.wait_ge(sem("a_ready"), n - 1)
                    nc.scalar.activation(SG[0:MB[m], n % 2, :], bank(("ga", b, m))[0:MB[m], :],
                                         ACT.Silu).then_inc(sem("silu_ready"), 1)

            def ln_rstd(b, which):
                act.wait_ge(sem(f"{which}_stats"), b + 1)
                inv_sqrt(rstd[:, tiles(b)], lnv[:, tiles(b)], mv[:, tiles(b), 1], f"{which}_rstd", 1.0, "eps5")

            for b in range(NB):
                ln_rstd(b, "ln1")
            for b in range(NB):
                filled(act, ("x2T", b))
                nc.scalar.copy(HT[:, toks(b)], bank(("x2T", b))[:]).then_inc(sem("x2T_ready"), 1)
                filled(act, ("xq", b))
                nc.scalar.copy(QT[:, toks(b)], bank(("xq", b))[:]).then_inc(sem("xq_ready"), 1)
            for s in range(NT + 5):
                if s < NT:
                    act.wait_ge(sem("sd_ready"), s + 1)
                    nc.scalar.activation(SD[:, s % 4, :], SD[:, s % 4, :], ACT.Exp, scale=SCALE).then_inc(
                        sem("xp_ready"), 1)
                if 2 <= s < NT + 2:
                    filled(act, ("pT", s - 2))
                    if s - 2 >= 4:
                        filled(act, ("pv", s - 6))
                    nc.scalar.copy(PT[:, (s - 2) % 4, :], bank(("pT", s - 2))[:]).then_inc(sem("pT_ready"), 1)
                if s >= 8 and s % TB == 0:
                    b = s // TB - 2
                    filled(act, ("oT", b))
                    nc.scalar.copy(OT[:, toks(b)], bank(("oT", b))[:]).then_inc(sem("oT_ready"), 1)
            for b in range(NB):
                ln_rstd(b, "ln2")
            for b in range(NB):
                filled(act, ("x3T", b))
                nc.scalar.copy(HT[:, toks(b)], bank(("x3T", b))[:]).then_inc(sem("x3T_ready"), 1)
            act.wait_ge(sem("top_ready"), 1)
            nc.scalar.activation(top[:, 2, :], top[:, 2, :], ACT.Exp).then_inc(sem("top_exp"), 1)
            for e in range(NE):
                for f in range(FB):
                    filled(act, ("h1", e, f))
                    if e >= 2:
                        filled(act, ("y", e - 2, 2))
                    nc.scalar.activation(H1A[e % 2][:, f, :], bank(("h1", e, f))[:, 0:CAP], ACT.Gelu,
                                         bias=vec("b1", e * FB + f, 1)).then_inc(sem("h1_ready"), 1)
            for b in range(NB):
                ln_rstd(b, "ln3")
            for b in range(NB):
                ln_rstd(b, "ln4")

        @block.vector
        def _(dve):
            chain = [0]

            def link(ins):
                chain[0] += 1
                ins.then_inc(sem("dve_step"), 1)
                dve.wait_ge(sem("dve_step"), chain[0])

            tt, ts, stt = nc.vector.tensor_tensor, nc.vector.tensor_scalar, nc.vector.scalar_tensor_tensor

            dve.wait_ge(sem("e_ready"), 2)
            link(ts(e_row, e_row, 1e19, None, ALU.min))
            ts(e_row, e_row, 1.0, None, ALU.add).then_inc(sem("e1_ready"), 1)
            link(ts(e_col, e_col, 1e19, None, ALU.min))
            ts(e_col, e_col, 1.0, None, ALU.add).then_inc(sem("e1_ready"), 1)
            dve.wait_ge(sem("g128_ready"), 1)
            tt(M[:].rearrange("p (h t) -> p h t", h=H), const("dist").unsqueeze(1).to_broadcast([P, H, P]),
               lg_row.unsqueeze(2).to_broadcast([P, H, P]), ALU.mult).then_inc(sem("logmask_ready"), 1)

            def sum_squares(b, src, name):
                link(tt(by_tile(SQ[:, b % 2, :]), src[:, tiles(b), :], src[:, tiles(b), :], ALU.mult))
                nc.vector.tensor_reduce(mv[:, tiles(b), 0], by_tile(SQ[:, b % 2, :]), AX, ALU.add).then_inc(
                    sem(name), 1)

            for b in range(NB):
                dve.wait_ge(sem(f"in_x{b}"), 16)
                if b >= 2:
                    dve.wait_ge(sem("rms_sum"), b - 1)
                sum_squares(b, X, "rms_sum")
            for b in range(NB):
                dve.wait_ge(sem("rms_rstd"), b + 1)
                tt(Hb[:, tiles(b), :], X[:, tiles(b), :], rstd[:, tiles(b)].unsqueeze(2).to_broadcast([P, TB, D]),
                   ALU.mult).then_inc(sem("h_ready"), 1)
            dve.wait_ge(sem("mask_exp"), 1)
            tt(M[:].rearrange("p (h t) -> p h t", h=H), M[:].rearrange("p (h t) -> p h t", h=H),
               const("causal").unsqueeze(1).to_broadcast([P, H, P]), ALU.mult).then_inc(sem("mask_ready"), 1)
            filled(dve, ("ck",))
            nc.vector.tensor_copy(CK[:], bank(("ck",))[:, 0:NB * KC]).then_inc(sem("ck_ready"), 1)
            for b in range(NB):
                filled(dve, ("cv", b))
                tt(VX[:, b, :, 0:32].rearrange("p g (j e) -> p g j e", j=HJ),
                   bank(("cv", b))[:, 0:D].rearrange("p (g j e) -> p g j e", g=HG, j=HJ),
                   const("keyhead").unsqueeze(1).unsqueeze(3).to_broadcast([P, HG, HJ, DH]), ALU.mult).then_inc(
                       sem("cv_ready"), 1)
            nc.vector.tensor_copy(VX[:, :, :, 32:PV].rearrange("p b g j -> p (b g) j"),
                                  const("keyhead").unsqueeze(1).to_broadcast([P, NB * HG, HJ])).then_inc(
                                      sem("vx_ready"), 1)
            for b in range(NB):
                filled(dve, ("k", b))
                tt(BIG[:].rearrange("p (j n) -> p j n", j=HJ)[:, :, toks(b)],
                   bank(("k", b))[:].unsqueeze(1).to_broadcast([P, HJ, T]),
                   const("quad").unsqueeze(2).to_broadcast([P, HJ, T]), ALU.mult).then_inc(sem("kexp_ready"), 1)
                filled(dve, ("kt", b))
                dve.wait_ge(sem("dk_ready"), 1)
                tt(KD[:, tiles(b), :], by_tile(bank(("kt", b))[:]), DK[:].unsqueeze(1).to_broadcast([P, TB, D]),
                   ALU.mult).then_inc(sem("kd_ready"), 1)

            dve.wait_ge(sem("mask_ready"), 1)
            for s in range(NT + 4):
                gb = s // TB - 1
                if s >= 5 and s % TB == 1:
                    b = gb
                    dve.wait_ge(sem("av_done"), TB * (b + 1))
                    link(nc.vector.bn_stats(stats[:, b, :], ybank[b % 2][:]))
                    link(nc.vector.bn_aggr(gs[:, b, 0:2], stats[:, b, :]))
                    stt(gs[:, b, 1:2], gs[:, b, 0:1], gs[:, b, 0:1], gs[:, b, 1:2], ALU.mult, ALU.add).then_inc(
                        sem("gn_part"), 1)
                if s >= 6 and s % TB == 2:
                    b = gb
                    dve.wait_ge(sem("gn_rstd"), b + 1)
                    link(tt(gs[:, b, 6:7], gs[:, b, 5:6], vec("gnw"), ALU.mult))
                    link(stt(gs[:, b, 7:8], gs[:, b, 2:3], gs[:, b, 6:7], vec("gnb"), ALU.mult, ALU.subtract))
                    ts(gs[:, b, 7:8], gs[:, b, 7:8], -1.0, None, ALU.mult).then_inc(sem("gn_affine"), 1)
                if s < NT:
                    for g in range(HG):
                        filled(dve, ("s", s, g))
                        if s >= 2 and g == 0:
                            dve.wait_ge(sem("av_done"), s - 1)
                            dve.wait_ge(sem("p_ready"), HG * (s - 1))
                        tt(PB[:, HG * (s % 2) + g, :], bank(("s", s, g))[:], M[:, g * 512:(g + 1) * 512],
                           ALU.mult).then_inc(sem("p_ready"), 1)
                    c = s % TB
                    if c < TB - 1:
                        n = (TB - 1) * (s // TB) + c
                        filled(dve, ("kv", s))
                        if c == 0:
                            tt(ST[:, n, :], bank(("kv", s))[:, 0:D], const("blockdiag"), ALU.mult).then_inc(
                                sem("state_ready"), 1)
                        else:
                            dve.wait_ge(sem("state_ready"), n)
                            link(tt(SQ[:, 0, 0:D], bank(("kv", s))[:, 0:D], const("blockdiag"), ALU.mult))
                            stt(ST[:, n, :], ST[:, n - 1, :], g128, SQ[:, 0, 0:D], ALU.mult, ALU.add).then_inc(
                                sem("state_ready"), 1)
                if s >= 5 and s % TB == 1:
                    b = gb
                    filled(dve, ("gn", b))
                    link(nc.vector.tensor_copy(gs[:, b, 2:4], bank(("gn", b))[:, 0:2]))
                    stt(gs[:, b, 3:4], gs[:, b, 2:3], gs[:, b, 2:3], gs[:, b, 3:4], ALU.mult,
                        ALU.subtract).then_inc(sem("gn_var"), 1)
                if s >= 6 and s % TB == 2:
                    b = gb
                    dve.wait_ge(sem("yn_ready"), b + 1)
                    dve.wait_ge(sem("g_ready"), b + 1)
                    if b >= 2:
                        filled(dve, ("o", b - 2))
                    tt(YG[:, b % 2, :], YN[:, b % 2, :], GT[:, toks(b)], ALU.mult).then_inc(sem("yg_ready"), 1)
                if s >= 7 and s % TB == 3:
                    b = gb
                    filled(dve, ("o", b))
                    tt(X1[:, tiles(b), :], by_tile(bank(("o", b))[:]), X[:, tiles(b), :], ALU.add).then_inc(
                        sem("x1_ready"), 1)

            for b in range(NB):
                dve.wait_ge(sem("x1_ready"), b + 1)
                if b >= 2:
                    dve.wait_ge(sem("rms2_sum"), b - 1)
                sum_squares(b, X1, "rms2_sum")
            for b in range(NB):
                dve.wait_ge(sem("rms2_rstd"), b + 1)
                tt(Hb[:, tiles(b), :], X1[:, tiles(b), :], rstd[:, tiles(b)].unsqueeze(2).to_broadcast([P, TB, D]),
                   ALU.mult).then_inc(sem("h2_ready"), 1)

            def layer_stats(b, src, which):
                for t in range(TB * b, TB * b + TB):
                    last = nc.vector.bn_stats(stats[:, t, :], src[:, t, :])
                link(last)
                for t in range(TB * b, TB * b + TB):
                    last = nc.vector.bn_aggr(mv[:, t, :], stats[:, t, :])
                last.then_inc(sem(f"{which}_stats"), 1)

            def layer_apply(b, dst, src, which):
                dve.wait_ge(sem(f"{which}_rstd"), b + 1)
                dve.wait_ge(sem(f"{which}_stats"), b + 1)
                for t in range(TB * b, TB * b + TB):
                    last = ts(dst[:, t, :], src[:, t, :], mv[:, t, 0:1], rstd[:, t:t + 1], ALU.subtract, ALU.mult)
                return last

            def mlp_out(b):
                filled(dve, ("dn", b))
                dve.wait_ge(sem("xx_ready"), b + 1)
                tt(R[:, tiles(b), :], by_tile(bank(("dn", b))[:]), XX[:, tiles(b), :], ALU.add).then_inc(
                    sem("r_ready"), 1)
                dve.wait_ge(sem("r_ready"), b + 1)
                layer_stats(b, R, "ln1")

            for b in range(NB):
                for m in range(3):
                    n = 3 * b + m
                    filled(dve, ("up", b, m))
                    dve.wait_ge(sem("silu_ready"), n + 1)
                    if b >= 2:
                        filled(dve, ("dn", b - 2))
                    tt(A[0:MB[m], 3 * (b % 2) + m, :], bank(("up", b, m))[0:MB[m], :], SG[0:MB[m], n % 2, :],
                       ALU.mult).then_inc(sem("a_ready"), 1)
                if b:
                    mlp_out(b - 1)
            mlp_out(NB - 1)
            dve.wait_ge(sem("av_done"), NT)
            dve.wait_ge(sem("ck_ready"), 1)
            for b in range(NB):
                tt(KX[:, b, :].rearrange("p (h k) -> p h k", h=H),
                   CK[:, b * KC:(b + 1) * KC].unsqueeze(1).to_broadcast([P, H, KC]),
                   const("head").unsqueeze(2).to_broadcast([P, H, KC]), ALU.mult).then_inc(sem("kx_ready"), 1)
            for b in range(NB):
                layer_apply(b, X2, R, "ln1").then_inc(sem("x2_ready"), 1)

            def cross_out(s):
                filled(dve, ("pv", s))
                pv = bank(("pv", s))[:, 0:HG * PV].rearrange("p (g c) -> p g c", g=HG)
                if s >= 2:
                    dve.wait_ge(sem("att_ready"), s - 1)
                link(nc.vector.reciprocal(xden[:, s % 2, :].rearrange("p (g j) -> p g j", g=HG), pv[:, :, 32:PV]))
                tt(ATT[:, s, :].rearrange("p (g j e) -> p g j e", g=HG, j=HJ),
                   pv[:, :, 0:32].rearrange("p g (j e) -> p g j e", j=HJ),
                   xden[:, s % 2, :].rearrange("p (g j) -> p g j", g=HG).unsqueeze(3).to_broadcast([P, HG, HJ, DH]),
                   ALU.mult).then_inc(sem("att_ready"), 1)

            for s in range(NT + 3):
                if s < NT:
                    filled(dve, ("xs", s))
                    sc = bank(("xs", s))[:].rearrange("p (h k) -> p h k", h=H)
                    link(nc.vector.tensor_reduce(xmax[:, s % 2, :], sc, AX, ALU.max))
                    if s >= 4:
                        filled(dve, ("pT", s - 4))
                    tt(SD[:, s % 4, :].rearrange("p (h k) -> p h k", h=H), sc,
                       xmax[:, s % 2, :].unsqueeze(2).to_broadcast([P, H, KC]), ALU.subtract).then_inc(
                           sem("sd_ready"), 1)
                if s >= 3:
                    cross_out(s - 3)
            for b in range(NB):
                filled(dve, ("xo", b))
                tt(R[:, tiles(b), :], by_tile(bank(("xo", b))[:]), X2[:, tiles(b), :], ALU.add).then_inc(
                    sem("r2_ready"), 1)
                dve.wait_ge(sem("r2_ready"), b + 1)
                layer_stats(b, R, "ln2")
            for b in range(NB):
                layer_apply(b, X3, R, "ln2").then_inc(sem("x3_ready"), 1)

            link(nc.vector.tensor_copy(onesb[:], const("same_expert")))
            link(nc.vector.memset(zeroT, 0.0))
            filled(dve, ("rt",))
            tt(logits, bank(("rt",))[:, 0:NT * NE].rearrange("p (t e) -> p t e", e=NE),
               vec("br").unsqueeze(1).to_broadcast([P, NT, NE]), ALU.add).then_inc(sem("logits_ready"), 1)
            dve.wait_ge(sem("logits_ready"), 1)
            iota_te = const("iota_e").unsqueeze(1).to_broadcast([P, NT, NE])

            def wide(v):
                return v.unsqueeze(2).to_broadcast([P, NT, NE])

            def pick(n, src, dst):
                link(nc.vector.tensor_reduce(top[:, n, :], src, AX, ALU.max))
                link(tt(rtmp, src, wide(top[:, n, :]), ALU.is_lt))
                link(stt(rtmp, rtmp, 100.0, iota_te, ALU.mult, ALU.add))
                link(nc.vector.tensor_reduce(top[:, 3, :], rtmp, AX, ALU.min))
                link(tt(dst, iota_te, wide(top[:, 3, :]), ALU.is_equal))

            pick(0, logits, pick1)
            link(stt(logits, pick1, -3e38, logits, ALU.mult, ALU.add))
            pick(1, logits, pick2)
            tt(top[:, 2, :], top[:, 1, :], top[:, 0, :], ALU.subtract).then_inc(sem("top_ready"), 1)
            dve.wait_ge(sem("top_exp"), 1)
            link(ts(top[:, 4, :], top[:, 2, :], 1.0, None, ALU.add))
            link(nc.vector.reciprocal(top[:, 4, :], top[:, 4, :]))
            link(tt(top[:, 5, :], top[:, 2, :], top[:, 4, :], ALU.mult))
            link(tt(rtmp, pick1, pick2, ALU.add))
            link(ts(rtmp, rtmp, -1.0, None, ALU.add))
            link(tt(pick1, pick1, wide(top[:, 4, :]), ALU.mult))
            link(tt(pick2, pick2, wide(top[:, 5, :]), ALU.mult))
            link(tt(pick1, pick1, pick2, ALU.add))
            tt(key_et.rearrange("p e t -> p t e"), pick1, rtmp, ALU.add).then_inc(sem("gate_ready"), 1)

            filled(dve, ("keyT",))
            nc.vector.tensor_copy(keyT, bank(("keyT",))[:, 0:P]).then_inc(sem("key_ready"), 1)
            dve.wait_ge(sem("key_ready"), 1)
            nc.vector.memset(thr[:, 0:1], 0.0).then_inc(sem("thr_ready"), 1)
            dve.wait_ge(sem("in_bits"), 16)
            for r in range(ROUNDS):
                dve.wait_ge(sem("thr_ready"), r + 1)
                link(tt(thr[:, 1:4].bitcast(I32), thr[:, 0:1].bitcast(I32).to_broadcast([P, 3]),
                        BT[:, 3 * r:3 * r + 3], ALU.bitwise_or))
                for j in range(3):
                    last = ts(seltmp if j == 0 else eqT if j == 1 else selT, keyT, thr[:, j + 1:j + 2], None,
                              ALU.is_ge, ALU.add, accum_out=cntb[:, j:j + 1])
                    last.then_inc(sem("cnt_part"), 1)
                dve.wait_ge(sem("cnt_part"), 3 * r + 3)
                nc.vector.tensor_copy(cand[:, 0:1], thr[:, 0:1]).then_inc(sem("cnt_ready"), 1)
                dve.wait_ge(sem("cnt_ready"), r + 1)
                filled(dve, ("cnt", r))
                link(stt(cand[:, 1:4], bank(("cnt", r))[:, 0:3], float(CAP), thr[:, 1:4], ALU.is_ge, ALU.mult))
                nc.vector.tensor_reduce(thr[:, 0:1], cand, AX, ALU.max).then_inc(sem("thr_ready"), 1)
            dve.wait_ge(sem("thr_ready"), ROUNDS + 1)
            link(ts(seltmp, keyT, thr[:, 0:1], None, ALU.is_gt, ALU.add, accum_out=nums[:, 0:1]))
            link(ts(eqT, keyT, thr[:, 0:1], None, ALU.is_equal, ALU.add, accum_out=nums[:, 1:2]))
            nc.vector.tensor_tensor_scan(selT, eqT, zeroT, 0.0, ALU.add, ALU.add).then_inc(sem("rows_ready"), 1)
            dve.wait_ge(sem("rows_ready"), 1)
            filled(dve, ("gt",))
            nc.vector.tensor_copy(nums[:, 2:4], bank(("gt",))[:, 0:2]).then_inc(sem("eq_room"), 1)
            dve.wait_ge(sem("eq_room"), 1)
            link(ts(selT, selT, nums[:, 2:3], nums[:, 3:4], ALU.add, ALU.add))
            link(stt(eqT, selT, float(CAP), eqT, ALU.is_le, ALU.mult))
            link(tt(seltmp, seltmp, eqT, ALU.add))
            link(ts(eqT, seltmp, 0.0, None, ALU.add, ALU.add, accum_out=nums[:, 4:5]))
            nc.vector.tensor_tensor_scan(selT, seltmp, zeroT, 0.0, ALU.add, ALU.add).then_inc(sem("sel_ready"), 1)
            dve.wait_ge(sem("sel_ready"), 1)
            filled(dve, ("sel",))
            link(ts(selT, selT, bank(("sel",))[:, 0:1], -1.0 - FAR, ALU.add, ALU.add))
            link(tt(selT, selT, seltmp, ALU.mult))
            ts(posT, selT, float(FAR), None, ALU.add).then_inc(sem("pos_ready"), 1)
            filled(dve, ("posT",))
            nc.vector.tensor_copy(posI, bank(("posT",))[:, 0:P]).then_inc(sem("posT_ready"), 1)
            dve.wait_ge(sem("posT_ready"), 1)
            link(ts(posA.bitcast(I32), posI, SLOT_A - 1, None, ALU.bitwise_and))
            link(ts(posB.bitcast(I32), posI, 5, None, ALU.logical_shift_right))
            link(tt(OB, const("iota_b").unsqueeze(1).to_broadcast([P, P, SLOT_B]),
                    posB.bitcast(I32).unsqueeze(2).to_broadcast([P, P, SLOT_B]), ALU.is_equal))
            tt(OA, const("iota_a").unsqueeze(1).to_broadcast([P, P, SLOT_A]),
               posA.bitcast(I32).unsqueeze(2).to_broadcast([P, P, SLOT_A]), ALU.is_equal).then_inc(
                   sem("onehot_ready"), 1)
            link(tt(OG, OB, key_et.rearrange("p e t -> p (e t)").unsqueeze(2).to_broadcast([P, P, SLOT_B]), ALU.mult))
            for e in range(NE):
                last = tt(OV[:, e * NT:(e + 1) * NT, :], OB[:, e * NT:(e + 1) * NT, :],
                          const("token").unsqueeze(2).to_broadcast([P, NT, SLOT_B]), ALU.mult)
            last.then_inc(sem("ov_ready"), 1)
            filled(dve, ("idx",))
            lists = bank(("idx",))[0:SLOT_A, 0:NE * 2 * SLOT_B].rearrange("p (e v b) -> p e v b", e=NE, v=2)
            for q in range(4):
                n = 3 if q < SLOT_B - 8 else 2
                rowsq = slice(32 * q, 32 * q + 32)
                ts(idx[rowsq, :, 0:n], lists[:, :, 0, q:SLOT_B:4], float(FAR), None, ALU.add).then_inc(
                    sem("idx_ready"), 1)
                nc.vector.tensor_copy(gates[rowsq, :, 0:n], lists[:, :, 1, q:SLOT_B:4]).then_inc(
                    sem("gates_ready"), 1)

            for e in range(NE + 1):
                if e < NE:
                    for c in range(3):
                        filled(dve, ("xeT", e, c))
                        nc.vector.tensor_copy(XET[:, e % 2, c * P:c * P + CH[c]],
                                              bank(("xeT", e, c))[:, 0:CH[c]]).then_inc(sem("xeT_ready"), 1)
                for c in range(3) if e < NE else []:
                    filled(dve, ("y", e, c))
                    if e == 0 and c == 0:
                        dve.wait_ge(sem("gates_ready"), 4)
                    if e >= 2:
                        dve.wait_ge(sem("added"), 16 * (3 * (e - 2) + c + 1))
                    ts(YE[0:CH[c], 3 * (e % 2) + c, :], bank(("y", e, c))[0:CH[c], 0:D],
                       gates[0:CH[c], e, c:c + 1], None, ALU.mult).then_inc(sem("ye_ready"), 1)

            for b in range(NB):
                dve.wait_ge(sem(f"in_sum{b}"), 16)
                layer_stats(b, AM, "ln3")
            for b in range(NB):
                link(layer_apply(b, AM, AM, "ln3"))
                link(tt(AM[:, tiles(b), :], AM[:, tiles(b), :], vec("fg").unsqueeze(1).to_broadcast([P, TB, D]),
                        ALU.mult))
                link(tt(AM[:, tiles(b), :], AM[:, tiles(b), :], vec("fb").unsqueeze(1).to_broadcast([P, TB, D]),
                        ALU.add))
                link(tt(AM[:, tiles(b), :], AM[:, tiles(b), :], X3[:, tiles(b), :], ALU.add))
                layer_stats(b, AM, "ln4")
            for b in range(NB):
                layer_apply(b, FIN, AM, "ln4").then_inc(sem("fin_ready"), 1)


def constants():
    c = np.zeros((P, NCONST), np.float32)
    i, j = np.arange(P)[:, None], np.arange(P)[None, :]

    def put(name, value):
        at, n = CONST[name]
        c[:, at:at + n] = value

    put("ident", i == j)
    put("blockdiag", i // DH == j // DH)
    put("headmean", (i // DH == j // DH) / DH)
    put("causal", j >= i)
    put("dist", np.maximum(j - i, 0))
    put("after", j + 1)
    put("same_expert", i // NT == j // NT)
    put("earlier_tile", (i // NT == j // NT) & (i % NT < j % NT))
    put("left", P - 1 - i)
    put("quad", (i % 32) // DH == np.arange(HJ))
    put("head", i // DH == np.arange(H))
    put("keyhead", i // KC == np.arange(HJ))
    put("iota_a", np.arange(SLOT_A))
    put("iota_b", np.arange(SLOT_B))
    put("token", i + P * np.arange(NT) - FAR)
    put("iota_e", np.arange(NE))
    put("eps6", 1e-6)
    put("eps5", 1e-5)
    put("ones", 1)
    bits = np.zeros((P, 3 * ROUNDS), np.int32)
    for r in range(ROUNDS):
        for n in range(3):
            bits[:, 3 * r + n] = (n + 1) << (BITS - 2 - 2 * r)
    return c, bits


def kernel(**inputs):
    import concourse.bacc as bacc
    from concourse.bass_utils import run_bass_kernel_spmd

    a = {k: np.asarray(v) for k, v in inputs.items()}

    def attn(n):
        return a["L0_attn_" + n]

    c, bits = constants()
    w1 = np.concatenate([attn(n).T for n in ("Wq", "Wk", "Wv", "Wg", "Wo")], 1)
    down = np.zeros((P, 3, D), np.float32)
    for m in range(3):
        down[:MB[m], m] = attn("down_w").T[P * m:P * m + MB[m]]
    ctx = a["ctx_1024"].transpose(2, 0, 1)
    ctxrep = np.broadcast_to(ctx[:, :, None, :], (D, NB, HJ, KC))
    w2 = np.concatenate([attn("gate_w").T, attn("up_w").T, down.reshape(P, -1)]
                        + [a["L0_xattn_W_" + n].T for n in "qkvo"]
                        + [ctx.reshape(D, -1), ctxrep.reshape(D, -1), a["L0_ffn_Wr"]], 1)

    def row(v):
        return np.broadcast_to(v.reshape(1, -1), (P, v.size))

    vecs = np.concatenate([attn("ln1_w")[:, None], attn("ln2_w")[:, None], attn("gn_w")[:, None],
                           attn("gn_b")[:, None], np.repeat(attn("gamma"), DH)[:, None], row(attn("gamma")),
                           row(a["L0_ffn_br"]), row(a["L0_ffn_gamma"]), row(a["L0_ffn_beta"]),
                           a["L0_ffn_b1"].reshape(NE * FB, P).T, row(a["L0_ffn_b2"])], 1)
    ew1 = a["L0_ffn_W1"].transpose(1, 0, 2)
    ew2 = a["L0_ffn_W2"].reshape(NE, FB, P, D).transpose(2, 0, 1, 3)
    arrays = {"x_dram": a["x"].reshape(N, D), "const_dram": c, "bits_dram": bits, "w1_dram": w1, "w2_dram": w2,
              "vec_dram": vecs, "ew1_dram": ew1, "ew2_dram": ew2}
    arrays = {k: np.ascontiguousarray(v) for k, v in arrays.items()}
    nc = bacc.Bacc("TRN2", target_bir_lowering=False, num_devices=1)
    args = [nc.dram_tensor(k, v.shape, mybir.dt.from_np(v.dtype), kind="ExternalInput").ap()
            for k, v in arrays.items()]
    args.append(nc.dram_tensor("out_dram", [N, D], F32, kind="ExternalOutput").ap())
    decoder_layer(nc, *args)
    r = run_bass_kernel_spmd(nc, [arrays], core_ids=[0])
    return r.results[0]["out_dram"].reshape(NB, T, D)
```

```python
from contextlib import ExitStack

import numpy as np

import concourse.bass as bass
from concourse import mybir

F32 = mybir.dt.float32
BF16 = mybir.dt.bfloat16
I32 = mybir.dt.int32
ALU = mybir.AluOpType
ACT = mybir.ActivationFunctionType
AX = mybir.AxisListType.X

P = 128
NB, T, D = 4, 512, 128
N = NB * T
NT = N // P
TB = T // P
H = 16
DH = D // H
HG = 4
HJ = H // HG
INNER = 352
MB = [128, 128, 96]
CS = 64
TC = T // CS
NPAIR = H // 2
SC = 4
NS = N // (CS * SC)
SB = NS // NB
KC = 32
NE, TOPK = 8, 2
FF = 512
FB = FF // P
CAP = (N * 5 // 4 + NE - 1) // NE
CH = [128, 128, CAP - 256]
SLOT_A, SLOT_B = 32, CAP // 32
FAR = 4096
BITS = 30
ROUNDS = BITS // 2
PV = 32 + HJ
SCALE = float(DH) ** -0.5

CONST = {}
_at = 0
for _name, _n in [("ident", 128), ("blockdiag", 128), ("headmean", 128), ("causal", CS), ("dist", CS),
                  ("after", CS), ("same_expert", 128), ("earlier_tile", 128), ("left", 1), ("quad", HJ),
                  ("head", H), ("keyhead", HJ), ("iota_a", SLOT_A), ("iota_b", SLOT_B), ("token_hi", NT), ("token_lo", 1),
                  ("iota_e", NE), ("eps6", 1), ("eps5", 1), ("ones", 128)]:
    CONST[_name] = (_at, _n)
    _at += _n
NCONST = _at

W1COLS = {n: (i * 128, 128) for i, n in enumerate(["q", "k", "v", "g", "o"])}
W2COLS = {}
_at = 0
for _name, _n in [("gate", INNER), ("up", INNER), ("down", 3 * 128), ("xq", 128), ("xk", 128), ("xv", 128),
                  ("xo", 128), ("ctx", NB * KC), ("ctxrep", NB * HJ * KC), ("router", NE)]:
    W2COLS[_name] = (_at, _n)
    _at += _n
NW2 = _at
VEC = {}
_at = 0
for _name, _n in [("ln1", 1), ("ln2", 1), ("gnw", 1), ("gnb", 1), ("gamma_col", 1), ("gamma_row", H), ("gamma_pair", NPAIR),
                  ("br", NE), ("fg", D), ("fb", D), ("b1", NE * FB), ("b2", NE * D)]:
    VEC[_name] = (_at, _n)
    _at += _n
NVEC = _at


def states(u, half):
    chunks = [SC * u + 2 * k + half for k in range(SC // 2)]
    return [c for c in chunks if c % TC < TC - 1]


def state_number(c):
    return (TC - 1) * (c // TC) + c % TC


def last_state(u, half):
    return state_number(states(u, half)[-1])


def plan_psum():
    jobs = []

    def job(key, sem, value):
        jobs.append((key, sem, value))

    job(("ck",), "ck_ready", 1)
    for b in range(NB):
        job(("cv", b), "cv_ready", b + 1)
    for b in range(NB):
        job(("hT", b), "hT_ready", b + 1)
    for b in range(NB):
        job(("q", b), "qd_ready", b + 1)
        job(("k", b), "klo_ready", b + 1)
        job(("kt", b), "kd_ready", b + 1)
        job(("v", b), "vlo_ready", b + 1)
    for b in range(NB):
        job(("g", b), "g_ready", b + 1)
    for u in range(NS + 4):
        if u < NS:
            for g in range(HG):
                job(("s", u, g), "p_ready", HG * u + g + 1)
            for half in range(2):
                job(("kv", u, half), "raw_ready", last_state(u, half) + 1)
        if u >= 3 and u % 2 == 1 and u < 3 + 2 * NB:
            job(("gn", (u - 3) // 2), "gn_var", (u - 1) // 2)
        if u >= 5 and u % 2 == 1:
            job(("o", (u - 5) // 2), "x1_ready", (u - 3) // 2)
    for b in range(NB):
        job(("h2T", b), "h2T_ready", b + 1)
    for b in range(NB + 1):
        if b < NB:
            for m in range(3):
                job(("ga", b, m), "silu_ready", 3 * b + m + 1)
                job(("up", b, m), "a_ready", 3 * b + m + 1)
        if b:
            job(("dn", b - 1), "r_ready", b)
    for b in range(NB):
        job(("x2T", b), "x2T_ready", b + 1)
        job(("xq", b), "xq_ready", b + 1)
    for s in range(NT + 5):
        if s < NT:
            job(("xs", s), "sd_ready", s + 1)
        if 2 <= s < NT + 2:
            job(("pT", s - 2), "pT_ready", s - 1)
        if 3 <= s < NT + 3:
            job(("pv", s - 3), "att_ready", s - 2)
        if s >= 8 and s % TB == 0:
            job(("oT", s // TB - 2), "oT_ready", s // TB - 1)
    for b in range(NB):
        job(("xo", b), "r2_ready", b + 1)
    for b in range(NB):
        job(("x3T", b), "x3T_ready", b + 1)
    job(("rt",), "logits_ready", 1)
    job(("keyT",), "key_ready", 1)
    for r in range(ROUNDS):
        job(("cnt", r), "thr_ready", r + 2)
    job(("gt",), "eq_room", 1)
    job(("sel",), "pos_ready", 1)
    job(("posT",), "posT_ready", 1)
    for g in range(NE // 2):
        job(("idx", g), "idx_ready", 4 * (g + 1))
    for e in range(NE):
        for c in range(3):
            job(("xeT", e, c), "xeT_ready", 3 * e + c + 1)
        for f in range(FB):
            job(("h1", e, f), "h1_ready", FB * e + f + 1)
        for c in range(3):
            job(("y", e, c), "ye_ready", 3 * e + c + 1)
    return jobs


def decoder_layer(nc, x, consts, bits, w1, w2, vecs, ew1, ew2, out):
    ctx = ExitStack()
    with ctx:
        def sb(name, shape, dt=F32):
            return ctx.enter_context(nc.sbuf_tensor(name, shape, dt))

        sems = {}

        def sem(name):
            if name not in sems:
                sems[name] = ctx.enter_context(nc.semaphore(name))
            return sems[name]

        ring = [ctx.enter_context(nc.psum_tensor(f"ring{i}", [P, 512], F32)) for i in range(6)]
        ybank = [ctx.enter_context(nc.psum_tensor(f"ybank{i}", [P, 512], F32)) for i in range(2)]
        jobs = plan_psum()
        seq = {key: n for n, (key, _, _) in enumerate(jobs)}

        def bank(key):
            return ring[seq[key] % 6]

        def room(pe, key):
            n = seq[key] - 6
            if n >= 0:
                pe.wait_ge(sem(jobs[n][1]), jobs[n][2])

        bank_full = [sem(f"bank_full{i}") for i in range(6)]

        def filled(eng, key):
            eng.wait_ge(bank_full[seq[key] % 6], seq[key] // 6 + 1)

        rows = nc.dram_tensor("rows_dram", [N, D + NE], F32, kind="Internal").ap()
        acc = nc.dram_tensor("acc_dram", [N, D], F32, kind="Internal").ap()

        X = sb("X", [P, NT, D])
        Hb = sb("Hb", [P, NT, D])
        HT = sb("HT", [P, N])
        QT = sb("QT", [P, N])
        BIG = sb("BIG", [P, HJ * N])
        QD = sb("QD", [P, N])
        KD = sb("KD", [P, NT, D])
        V = sb("V", [P, NT, D])
        VZB = sb("VZB", [P, 4 * 2 * N], BF16)[:]
        VZ = VZB.bitcast(F32).rearrange("p (s c) -> p s c", s=4)
        GT = sb("GT", [P, N])
        M = sb("M", [P, H * P])
        X1 = sb("X1", [P, NT, D])
        PB = sb("PB", [P, 8, 512])
        SQ = sb("SQ", [P, 2, 512])
        SR = sb("SR", [P, 2, D])
        SM = sb("SM", [P, 4, D])
        P32 = sb("P32", [P, 3, 512])
        YN = sb("YN", [P, 2, 512])
        YG = sb("YG", [P, 2, 512])
        C = sb("C", [P, NCONST])
        W1 = sb("W1", [P, 5 * 128])
        W2 = sb("W2", [P, NW2])
        VC = sb("VC", [P, NVEC])
        BT = sb("BT", [P, 3 * ROUNDS], I32)
        DQ = sb("DQ", [P, CS])
        DK = sb("DK", [P, P])
        small = sb("small", [P, 256])
        mv = sb("mv", [P, NT, 2])
        stats = sb("stats", [P, NT, 6])
        rstd = sb("rstd", [P, NT])
        lnv = sb("lnv", [P, NT])
        CK = sb("CK", [P, NB * KC])
        VX = sb("VX", [P, NB, HG, PV])

        QP = QT[:].bitcast(BF16).rearrange("p (w n) -> p w n", w=2)
        KE = BIG[:].bitcast(BF16).rearrange(
            "p (w c j s) -> p w c j s", w=2, j=HJ, s=CS)
        KP = YG[:].rearrange("p s c -> p (s c)").bitcast(BF16).rearrange("p (s w n) -> p s w n", s=2, w=2)
        VP = Hb[:].rearrange("p t d -> p (t d)").bitcast(BF16).rearrange("p (w t d) -> p w t d", w=2, d=D)
        PP = PB[:].rearrange("p s c -> p (s c)").bitcast(BF16).rearrange("p (w s c) -> p w s c", w=2, c=512)
        VS = VZB.rearrange(
            "p (u i w r d) -> p u i w r d", u=2, i=SC, w=2, r=NPAIR)
        R = QD[:].rearrange("p (t d) -> p t d", d=D)
        X2 = KD
        XX = VZ[:, 3, :].rearrange("p (t d) -> p t d", d=D)
        ATT = V
        X3 = GT[:].rearrange("p (t d) -> p t d", d=D)
        OT = M
        KX = VZ[:, 0, :].rearrange("p (b c) -> p b c", b=NB)
        SD = VZ[:, 1, :].rearrange("p (s c) -> p s c", s=4)
        PT = VZ[:, 2, :].rearrange("p (s c) -> p s c", s=4)
        A = PB[:, 0:6, :]
        SG = YN
        EW1 = BIG[:, 0:NE * FF].rearrange("p (e f) -> p e f", e=NE)
        EW2 = BIG[:, NE * FF:2 * NE * FF].rearrange("p (e f d) -> p e f d", e=NE, d=D)

        def const(name, a=0, n=None):
            at, width = CONST[name]
            return C[:, at + a:at + a + (width if n is None else n)]

        def wa(name, a=0, n=None):
            at, width = W1COLS[name]
            return W1[:, at + a:at + a + (width if n is None else n)]

        def wb(name, a=0, n=None):
            at, width = W2COLS[name]
            return W2[:, at + a:at + a + (width if n is None else n)]

        def vec(name, a=0, n=None):
            at, width = VEC[name]
            return VC[:, at + a:at + a + (width if n is None else n)]

        def tiles(b):
            return slice(TB * b, TB * b + TB)

        def toks(b):
            return slice(T * b, T * b + T)

        def by_tile(ap):
            return ap.rearrange("p (t d) -> p t d", d=D)

        e_row, lg_row = small[:, 0:H], small[:, 16:16 + H]
        e_col, lg_col, g64 = small[:, 32:33], small[:, 33:34], small[:, 34:35]
        e_pair, lg_pair = small[:, 150:158], small[:, 158:166]
        gs = small[:, 36:68].rearrange("p (b c) -> p b c", b=NB)
        xmax = small[:, 80:112].rearrange("p (s h) -> p s h", s=2)
        xden = small[:, 112:144].rearrange("p (s h) -> p s h", s=2)

        RB = PB[:, 0:2, :].rearrange("p s c -> p (s c)")
        logits = RB[:, 0:128].rearrange("p (t e) -> p t e", e=NE)
        rtmp = RB[:, 128:256].rearrange("p (t e) -> p t e", e=NE)
        pick1 = RB[:, 256:384].rearrange("p (t e) -> p t e", e=NE)
        pick2 = RB[:, 384:512].rearrange("p (t e) -> p t e", e=NE)
        key_et = RB[:, 512:640].rearrange("p (e t) -> p e t", e=NE)
        keyT = RB[:, 640:768]
        seltmp = RB[:, 768:896]
        selT = RB[:, 896:1024]
        RC = PB[:, 2, :]
        top = RC[:, 0:96].rearrange("p (n t) -> p n t", t=NT)
        thr = RC[:, 96:100]
        cand = RC[:, 100:104]
        nums = RC[:, 104:112]
        eqT = RC[:, 112:240]
        zeroT = RC[:, 240:368]
        posT = PB[:, 3, 0:128]
        posI = PB[:, 3, 128:256].bitcast(I32)
        posA = PB[:, 3, 256:384]
        posB = PB[:, 3, 384:512]
        onesb = sb("onesb", [P, P], BF16)
        cntb = sb("cntb", [P, 4], BF16)
        OA = VZB[:, 0:P * SLOT_A].rearrange("p (n a) -> p n a", a=SLOT_A)
        OB, OHI, OLO = [VZB[:, P * (SLOT_A + k * SLOT_B):P * (SLOT_A + (k + 1) * SLOT_B)].rearrange(
            "p (n b) -> p n b", b=SLOT_B) for k in range(3)]
        key_te = PB[:, 4, 0:128].rearrange("p (t e) -> p t e", e=NE)
        X3F = V
        idx = sb("idx", [P, NE, 3], I32)
        XE = QT[:, 0:9 * (D + NE)].rearrange("p (s c d) -> p s c d", s=3, d=D + NE)
        XET = QT[:, 9 * (D + NE):9 * (D + NE) + 2 * CAP].rearrange("p (s c) -> p s c", s=2)
        H1A = [M[:, 0:FB * CAP].rearrange("p (f c) -> p f c", f=FB),
               QD[:, 0:FB * CAP].rearrange("p (f c) -> p f c", f=FB)]
        YE = PB[:, 5:7, :].rearrange("p s c -> p (s c)")[:, 0:6 * D].rearrange("p (s d) -> p s d", d=D)
        AM = KD
        FIN = HT[:].rearrange("p (t d) -> p t d", d=D)

        def strips(u, half, part, head):
            base = VS[CS * head:CS * head + CS, u % 2, half, part, 0, DH * head:DH * head + DH]
            chunk = SC // 2 * 2 * NPAIR * D
            return bass.AP(base.tensor, base.offset, [list(base.ap[0]), [chunk, SC // 2], [D + 2 * DH, NPAIR],
                                                      [1, DH]])

        block = ctx.enter_context(nc.Block())

        @block.sync
        def _(sp):
            sp.dma_start(C[:], consts).then_inc(sem("in_const"), 16)
            xv = x.rearrange("(t p) d -> p t d", p=P)
            for b in range(NB):
                sp.dma_start(X[:, tiles(b), :], xv[:, tiles(b), :]).then_inc(sem(f"in_x{b}"), 16)
                if b == 0:
                    sp.dma_start(VC[:], vecs).then_inc(sem("in_vec"), 16)
                    sp.dma_start(W1[:], w1).then_inc(sem("in_w1"), 16)
            sp.dma_start(W2[:], w2).then_inc(sem("in_w2"), 16)
            sp.dma_start(BT[:], bits).then_inc(sem("in_bits"), 16)
            sp.wait_ge(sem("av_done"), NB * TC)
            sp.dma_start(EW1, ew1).then_inc(sem("in_ew"), 16)
            sp.dma_start(EW2, ew2).then_inc(sem("in_ew"), 16)
            for b in range(NB):
                sp.wait_ge(sem("x3_ready"), b + 1)
                for dst in (rows[:, 0:D], acc):
                    sp.dma_start(dst.rearrange("(t p) d -> p t d", p=P)[:, tiles(b), :],
                                 X3[:, tiles(b), :]).then_inc(sem("x3_stored"), 16)
            sp.wait_ge(sem("gates_ready"), 1)
            sp.dma_start(rows[:, D:D + NE].rearrange("(t p) e -> p t e", p=P), key_te).then_inc(sem("x3_stored"), 16)
            sp.wait_ge(sem("added"), 16 * 3 * NE)
            for b in range(NB):
                sp.dma_start(AM[:, tiles(b), :], acc.rearrange("(t p) d -> p t d", p=P)[:, tiles(b), :]).then_inc(
                    sem(f"in_sum{b}"), 16)
            for b in range(NB):
                sp.wait_ge(sem("fin_ready"), b + 1)
                sp.dma_start(out.rearrange("(t p) d -> p t d", p=P)[:, tiles(b), :],
                             FIN[:, tiles(b), :]).then_inc(sem("stored"), 16)
            sp.wait_ge(sem("stored"), 16 * NB)

        @block.gpsimd
        def _(pool):
            nc.gpsimd.memset(VZ, 0.0).then_inc(sem("vz_zero"), 1)
            pool.wait_ge(sem("vz_zero"), 1)

            def spread_v(u):
                pool.wait_ge(sem("vlo_ready"), u // SB + 1)
                if u >= 2:
                    pool.wait_ge(sem("av_done"), SC * (u - 1))
                    pool.wait_ge(sem("vz_ready"), 8 * (u - 1))
                for part in range(2):
                    for half in range(2):
                        for head in range(2):
                            src = VP[CS * half:CS * half + CS, part, 2 * u:2 * u + 2, :].rearrange(
                                "p t (r a e) -> p t r a e", a=2, e=DH)[:, :, :, head, :]
                            nc.gpsimd.tensor_copy(strips(u, half, part, head), src).then_inc(sem("vz_ready"), 1)
                            pool.wait_ge(sem("vz_ready"), 8 * u + 4 * part + 2 * half + head + 1)

            def mask_state(c):
                n = state_number(c)
                pool.wait_ge(sem("raw_ready"), n + 1)
                if c > 2:
                    pool.wait_ge(sem("av_done"), c - 2)
                if n:
                    pool.wait_ge(sem("state_ready"), n)
                nc.gpsimd.tensor_tensor(SM[:, c % 4, :], SR[:, n % 2, :], const("blockdiag"), ALU.mult).then_inc(
                    sem("state_ready"), 1)

            spread_v(0)
            for u in range(NS):
                if u + 1 < NS and u < 1:
                    spread_v(u + 1)
                for c in range(SC * u, SC * u + SC):
                    if c % TC < TC - 1:
                        mask_state(c)
                if u >= 1 and u + 1 < NS:
                    spread_v(u + 1)
            for b in range(NB):
                pool.wait_ge(sem("x1_ready"), b + 1)
                pool.wait_ge(sem("h2_ready"), b + 1)
                nc.gpsimd.tensor_tensor(XX[:, tiles(b), :], X[:, tiles(b), :], X1[:, tiles(b), :],
                                        ALU.add).then_inc(sem("xx_ready"), 1)
            pool.wait_ge(sem("x3T_ready"), NB)
            nc.gpsimd.memset(XE, 0.0).then_inc(sem("xe_zero"), 1)
            pool.wait_ge(sem("xe_zero"), 1)
            pool.wait_ge(sem("x3_stored"), 16 * (2 * NB + 1))

            def gather(e):
                pool.wait_ge(sem("idx_ready"), 4 * (e // 2 + 1))
                if e >= 3:
                    pool.wait_ge(sem("ye_ready"), 3 * (e - 2))
                for c in range(3):
                    nc.gpsimd.indirect_dma_start(
                        out=XE[0:CH[c], e % 3, c, :], out_offset=None, in_=rows,
                        in_offset=bass.IndirectOffsetOnAxis(ap=idx[0:CH[c], e, c:c + 1], axis=0),
                        bounds_check=N - 1, oob_is_err=False).then_inc(sem(f"gathered{e % 3}"), 16)

            def scatter(e):
                for c in range(3):
                    pool.wait_ge(sem("ye_ready"), 3 * e + c + 1)
                    if e and c == 0:
                        pool.wait_ge(sem("added"), 16 * 3 * e)
                    nc.gpsimd.indirect_dma_start(
                        out=acc, out_offset=bass.IndirectOffsetOnAxis(ap=idx[0:CH[c], e, c:c + 1], axis=0),
                        in_=YE[0:CH[c], 3 * (e % 2) + c, :], in_offset=None,
                        bounds_check=N - 1, oob_is_err=False, compute_op=ALU.add).then_inc(sem("added"), 16)

            gather(0)
            gather(1)
            for b in range(NB):
                nc.gpsimd.tensor_tensor(X3F[:, tiles(b), :], X3[:, tiles(b), :],
                                        vec("fb").unsqueeze(1).to_broadcast([P, TB, D]), ALU.add).then_inc(
                                            sem("x3f_ready"), 1)
            for e in range(NE):
                if e + 2 < NE:
                    gather(e + 2)
                scatter(e)
            pool.wait_ge(sem("x3f_ready"), NB)
            for b in range(NB):
                pool.wait_ge(sem("scaled_ready"), b + 1)
                nc.gpsimd.tensor_tensor(AM[:, tiles(b), :], AM[:, tiles(b), :], X3F[:, tiles(b), :],
                                        ALU.add).then_inc(sem("sum_ready"), 1)

        @block.tensor
        def _(pe):
            def transposes(key, src, n=TB):
                room(pe, key)
                for t in range(n):
                    last = nc.tensor.transpose(bank(key)[:, t * P:(t + 1) * P], src(t), const("ident"))
                last.then_inc(bank_full[seq[key] % 6], 1)

            def done(key, last):
                last.then_inc(bank_full[seq[key] % 6], 1)

            pe.wait_ge(sem("in_w2"), 16)
            room(pe, ("ck",))
            done(("ck",), nc.tensor.matmul(bank(("ck",))[:, 0:NB * KC], wb("xk"), wb("ctx"), start=True, stop=True))
            for b in range(NB):
                key = ("cv", b)
                room(pe, key)
                done(key, nc.tensor.matmul(bank(key)[:, 0:D], wb("ctxrep", b * P, P), wb("xv"), start=True, stop=True))

            pe.wait_ge(sem("in_const"), 16)
            for b in range(NB):
                pe.wait_ge(sem("h_ready"), b + 1)
                transposes(("hT", b), lambda t: Hb[:, TB * b + t, :])
            pe.wait_ge(sem("in_w1"), 16)

            def token_layout(key, b, w):
                room(pe, key)
                for t in range(TB):
                    s = TB * b + t
                    last = nc.tensor.matmul(bank(key)[:, t * D:(t + 1) * D], HT[:, s * P:(s + 1) * P], w,
                                            start=True, stop=True)
                done(key, last)

            for b in range(NB):
                pe.wait_ge(sem("hT_ready"), b + 1)
                for n in "qk":
                    room(pe, (n, b))
                    done((n, b), nc.tensor.matmul(bank((n, b))[:], wa(n), HT[:, toks(b)], start=True, stop=True))
                token_layout(("kt", b), b, wa("k"))
                token_layout(("v", b), b, wa("v"))
            for b in range(NB):
                key = ("g", b)
                room(pe, key)
                done(key, nc.tensor.matmul(bank(key)[:], wa("g"), HT[:, toks(b)], start=True, stop=True))

            PARTS = ((0, 0), (0, 1), (1, 0))

            def scores(u):
                pe.wait_ge(sem("kexp_ready"), u // SB + 1)
                pe.wait_ge(sem("qd_ready"), u // SB + 1)
                for g in range(HG):
                    key = ("s", u, g)
                    room(pe, key)
                    rows32 = slice(32 * g, 32 * g + 32)
                    for i in range(SC):
                        at = slice(CS * (SC * u + i), CS * (SC * u + i + 1))
                        for r in range(2):
                            for wk, wq in PARTS:
                                last = nc.tensor.matmul(bank(key)[:, (2 * i + r) * CS:(2 * i + r + 1) * CS],
                                                        KE[rows32, wk, SC * u + i, 2 * r:2 * r + 2, :].rearrange(
                                                            "p j s -> p (j s)"),
                                                        QP[rows32, wq, at], start=(wk == wq == 0), stop=(wk == 1))
                    done(key, last)

            def chunk_states(u):
                pe.wait_ge(sem("kd_ready"), u // SB + 1)
                pe.wait_ge(sem("v_ready"), u // SB + 1)
                for half in range(2):
                    key = ("kv", u, half)
                    room(pe, key)
                    here = slice(CS * half, CS * half + CS)
                    for k, c in enumerate(states(u, half)):
                        last = nc.tensor.matmul(bank(key)[:, k * D:(k + 1) * D], KD[here, c // 2, :],
                                                V[here, c // 2, :], start=True, stop=True)
                    done(key, last)

            def retained(c):
                b, u, i = c // TC, c // SC, c % SC
                if c % TC == 0 and b >= 2:
                    pe.wait_ge(sem("yn_ready"), b - 1)
                y = ybank[b % 2][:, (c % TC) * CS:(c % TC + 1) * CS]
                if c % TC:
                    pe.wait_ge(sem("state_ready"), state_number(c - 1) + 1)
                    nc.tensor.matmul(y, SM[:, (c - 1) % 4, :], QD[:, c * CS:(c + 1) * CS], start=True, stop=False)
                pe.wait_ge(sem("vz_ready"), 8 * (u + 1))
                for r in range(NPAIR):
                    g = r // 2
                    if i == 0 and r % 2 == 0:
                        pe.wait_ge(sem("plo_ready"), HG * u + g + 1)
                    for wv, wp in PARTS:
                        at = (2 * i + r % 2) * CS
                        last = nc.tensor.matmul(y, VS[:, u % 2, i, wv, r, :],
                                                PP[:, wp, HG * (u % 2) + g, at:at + CS],
                                                start=(c % TC == 0 and r == wv == wp == 0),
                                                stop=(r == NPAIR - 1 and wv == 1))
                last.then_inc(sem("av_done"), 1)

            for u in range(NS + 4):
                if u < NS:
                    scores(u)
                    chunk_states(u)
                if 1 <= u <= NS:
                    for c in range(SC * (u - 1), SC * u):
                        retained(c)
                if u >= 3 and u % 2 == 1 and u < 3 + 2 * NB:
                    b = (u - 3) // 2
                    key = ("gn", b)
                    room(pe, key)
                    pe.wait_ge(sem("gn_part"), b + 1)
                    done(key, nc.tensor.matmul(bank(key)[:, 0:2], const("headmean"), gs[:, b, 0:2],
                                               start=True, stop=True))
                if u >= 5 and u % 2 == 1:
                    b = (u - 5) // 2
                    key = ("o", b)
                    room(pe, key)
                    pe.wait_ge(sem("yg_ready"), b + 1)
                    for t in range(TB):
                        last = nc.tensor.matmul(bank(key)[:, t * D:(t + 1) * D],
                                                YG[:, b % 2, t * P:(t + 1) * P], wa("o"), start=True, stop=True)
                    done(key, last)

            for b in range(NB):
                pe.wait_ge(sem("h2_ready"), b + 1)
                transposes(("h2T", b), lambda t: Hb[:, TB * b + t, :])
            for b in range(NB + 1):
                if b < NB:
                    pe.wait_ge(sem("h2T_ready"), b + 1)
                    for m in range(3):
                        for name, w in (("ga", "gate"), ("up", "up")):
                            key = (name, b, m)
                            room(pe, key)
                            done(key, nc.tensor.matmul(bank(key)[0:MB[m], :], wb(w, 128 * m, MB[m]),
                                                       HT[:, toks(b)], start=True, stop=True))
                if b:
                    key = ("dn", b - 1)
                    room(pe, key)
                    pe.wait_ge(sem("a_ready"), 3 * b)
                    for t in range(TB):
                        for m in range(3):
                            last = nc.tensor.matmul(bank(key)[:, t * D:(t + 1) * D],
                                                    A[0:MB[m], 3 * ((b - 1) % 2) + m, t * P:(t + 1) * P],
                                                    wb("down", 128 * m, 128)[0:MB[m], :],
                                                    start=(m == 0), stop=(m == 2))
                    last.then_inc(bank_full[seq[key] % 6], 1)

            for b in range(NB):
                pe.wait_ge(sem("x2_ready"), b + 1)
                transposes(("x2T", b), lambda t: X2[:, TB * b + t, :])
                key = ("xq", b)
                room(pe, key)
                pe.wait_ge(sem("x2T_ready"), b + 1)
                done(key, nc.tensor.matmul(bank(key)[:], wb("xq"), HT[:, toks(b)], start=True, stop=True))
            pe.wait_ge(sem("kx_ready"), NB)
            pe.wait_ge(sem("vx_ready"), 1)
            for s in range(NT + 5):
                if s < NT:
                    key = ("xs", s)
                    pe.wait_ge(sem("xq_ready"), s // TB + 1)
                    room(pe, key)
                    done(key, nc.tensor.matmul(bank(key)[:], QT[:, s * P:(s + 1) * P], KX[:, s // TB, :],
                                               start=True, stop=True))
                if 2 <= s < NT + 2:
                    pe.wait_ge(sem("xp_ready"), s - 1)
                    transposes(("pT", s - 2), lambda t: SD[:, (s - 2) % 4, t * P:(t + 1) * P])
                if 3 <= s < NT + 3:
                    key = ("pv", s - 3)
                    room(pe, key)
                    pe.wait_ge(sem("pT_ready"), s - 2)
                    for g in range(HG):
                        last = nc.tensor.matmul(bank(key)[:, g * PV:(g + 1) * PV],
                                                PT[:, (s - 3) % 4, g * P:(g + 1) * P],
                                                VX[:, (s - 3) // TB, g, :], start=True, stop=True)
                    done(key, last)
                if s >= 8 and s % TB == 0:
                    b = s // TB - 2
                    pe.wait_ge(sem("att_ready"), TB * (b + 1))
                    transposes(("oT", b), lambda t: ATT[:, TB * b + t, :])
            for b in range(NB):
                key = ("xo", b)
                room(pe, key)
                pe.wait_ge(sem("oT_ready"), b + 1)
                for t in range(TB):
                    s = TB * b + t
                    last = nc.tensor.matmul(bank(key)[:, t * D:(t + 1) * D], OT[:, s * P:(s + 1) * P], wb("xo"),
                                            start=True, stop=True)
                done(key, last)
            for b in range(NB):
                pe.wait_ge(sem("x3_ready"), b + 1)
                transposes(("x3T", b), lambda t: X3[:, TB * b + t, :])

            room(pe, ("rt",))
            pe.wait_ge(sem("x3T_ready"), NB)
            for s in range(NT):
                last = nc.tensor.matmul(bank(("rt",))[:, s * NE:(s + 1) * NE], HT[:, s * P:(s + 1) * P],
                                        wb("router"), start=True, stop=True)
            done(("rt",), last)
            pe.wait_ge(sem("gate_ready"), 1)
            transposes(("keyT",), lambda t: key_et.rearrange("p e t -> p (e t)"), 1)
            for r in range(ROUNDS):
                key = ("cnt", r)
                room(pe, key)
                pe.wait_ge(sem("cnt_ready"), 3 * (r + 1))
                done(key, nc.tensor.matmul(bank(key)[:, 0:3], onesb[:], cntb[:, 0:3], start=True, stop=True))
            room(pe, ("gt",))
            pe.wait_ge(sem("rows_ready"), 1)
            nc.tensor.matmul(bank(("gt",))[:, 0:1], const("same_expert"), nums[:, 0:1], start=True, stop=True)
            done(("gt",), nc.tensor.matmul(bank(("gt",))[:, 1:2], const("earlier_tile"), nums[:, 1:2],
                                           start=True, stop=True))
            room(pe, ("sel",))
            pe.wait_ge(sem("sel_ready"), 1)
            done(("sel",), nc.tensor.matmul(bank(("sel",))[:, 0:1], const("earlier_tile"), nums[:, 4:5],
                                            start=True, stop=True))
            pe.wait_ge(sem("pos_ready"), 1)
            transposes(("posT",), lambda t: posT, 1)
            for g in range(NE // 2):
                key = ("idx", g)
                room(pe, key)
                pe.wait_ge(sem("onehot_ready"), g + 1)
                for e in (2 * g, 2 * g + 1):
                    o = bank(key)[0:SLOT_A, (e % 2) * SLOT_B:(e % 2 + 1) * SLOT_B]
                    for t in range(NT):
                        n = e * NT + t
                        nc.tensor.matmul(o, OA[:, n, :], OHI[:, n, :], start=(t == 0), stop=False)
                        last = nc.tensor.matmul(o, OA[:, n, :], OLO[:, n, :], start=False, stop=(t == NT - 1))
                done(key, last)

            pe.wait_ge(sem("in_ew"), 32)
            for e in range(NE):
                for c in range(3):
                    key = ("xeT", e, c)
                    room(pe, key)
                    pe.wait_ge(sem(f"gathered{e % 3}"), 16 * 3 * (e // 3 + 1))
                    done(key, nc.tensor.transpose(bank(key)[:, 0:CH[c]], XE[0:CH[c], e % 3, c, 0:D],
                                                  const("ident")[0:CH[c], 0:CH[c]]))
                pe.wait_ge(sem("xeT_ready"), 3 * e + 3)
                for f in range(FB):
                    key = ("h1", e, f)
                    room(pe, key)
                    done(key, nc.tensor.matmul(bank(key)[:, 0:CAP], EW1[:, e, f * P:(f + 1) * P], XET[:, e % 2, :],
                                               start=True, stop=True))
                pe.wait_ge(sem("h1_ready"), FB * (e + 1))
                for c in range(3):
                    key = ("y", e, c)
                    room(pe, key)
                    o = bank(key)[0:CH[c], 0:D]
                    for f in range(FB):
                        nc.tensor.matmul(o, H1A[e % 2][:, f, c * P:c * P + CH[c]], EW2[:, e, f, :],
                                         start=(f == 0), stop=False)
                    done(key, nc.tensor.matmul(o, const("ones", 0, CH[c])[0:1, :], vec("b2", e * D, D)[0:1, :],
                                               start=False, stop=True))

        @block.scalar
        def _(act):
            chain = [0]

            def link(ins):
                chain[0] += 1
                ins.then_inc(sem("act_step"), 1)
                act.wait_ge(sem("act_step"), chain[0])

            def inv_sqrt(dst, tmp, src, name, scale, eps):
                link(nc.scalar.activation(tmp, src, ACT.Ln, bias=const(eps), scale=scale))
                nc.scalar.activation(dst, tmp, ACT.Exp, scale=-0.5).then_inc(sem(name), 1)

            act.preload_act_table_set("natural_log_exp_and_others")
            act.wait_ge(sem("in_const"), 16)
            act.wait_ge(sem("in_vec"), 16)
            nc.scalar.activation(e_row, vec("gamma_row"), ACT.Exp, scale=-1.0).then_inc(sem("e_ready"), 1)
            nc.scalar.activation(e_pair, vec("gamma_pair"), ACT.Exp, scale=-1.0).then_inc(sem("e_ready"), 1)
            nc.scalar.activation(e_col, vec("gamma_col"), ACT.Exp, scale=-1.0).then_inc(sem("e_ready"), 1)
            act.wait_ge(sem("e1_ready"), 3)
            link(nc.scalar.activation(lg_pair, e_pair, ACT.Ln))
            link(nc.scalar.activation(lg_row, e_row, ACT.Ln))
            link(nc.scalar.activation(lg_col, e_col, ACT.Ln))
            link(nc.scalar.mul(small[:, 144:145], lg_col, -1.0))
            nc.scalar.activation(g64, lg_col, ACT.Exp, scale=-float(CS)).then_inc(sem("g64_ready"), 1)
            nc.scalar.activation(DQ[:], const("after"), ACT.Exp, scale=small[:, 144:145]).then_inc(sem("dq_ready"), 1)
            link(nc.scalar.mul(small[:, 145:146], const("left"), -1.0))
            nc.scalar.activation(DK[:].rearrange("p (h d) -> p h d", h=H),
                                 lg_row.unsqueeze(2).to_broadcast([P, H, DH]), ACT.Exp,
                                 scale=small[:, 145:146]).then_inc(sem("dk_ready"), 1)
            act.wait_ge(sem("logmask_ready"), 1)
            nc.scalar.activation(M[:, 0:512], M[:, 0:512], ACT.Exp, scale=-1.0).then_inc(sem("mask_exp"), 1)

            for b in range(NB):
                act.wait_ge(sem("rms_sum"), b + 1)
                inv_sqrt(rstd[:, tiles(b)], lnv[:, tiles(b)], mv[:, tiles(b), 0], "rms_rstd", 1.0 / D, "eps6")

            for b in range(NB):
                filled(act, ("hT", b))
                nc.scalar.activation(HT[:, toks(b)], bank(("hT", b))[:], ACT.Copy,
                                     scale=vec("ln1")).then_inc(sem("hT_ready"), 1)
            for b in range(NB):
                filled(act, ("q", b))
                nc.scalar.copy(QP[:, 0, toks(b)], bank(("q", b))[:]).then_inc(sem("q_ready"), 1)
                filled(act, ("k", b))
                if b >= 2:
                    act.wait_ge(sem("kexp_ready"), b - 1)
                nc.scalar.copy(KP[:, b % 2, 0, :], bank(("k", b))[:]).then_inc(sem("k_ready"), 1)
                filled(act, ("v", b))
                nc.scalar.copy(VP[:, 0, tiles(b), :], by_tile(bank(("v", b))[:])).then_inc(sem("vhi_ready"), 1)
                nc.scalar.copy(V[:, tiles(b), :], by_tile(bank(("v", b))[:])).then_inc(sem("v_ready"), 1)
            for b in range(NB):
                filled(act, ("g", b))
                nc.scalar.activation(GT[:, toks(b)], bank(("g", b))[:], ACT.Sigmoid).then_inc(sem("g_ready"), 1)
            act.preload_act_table_set("natural_log_exp_and_others")
            for u in range(NS + 4):
                for g in range(HG) if u < NS else []:
                    n = HG * u + g
                    act.wait_ge(sem("p_ready"), n + 1)
                    if u >= 2:
                        act.wait_ge(sem("av_done"), SC * (u - 1))
                    nc.scalar.copy(PP[:, 0, n % 8, :], P32[:, n % 3, :]).then_inc(sem("phi_ready"), 1)
                if u < 3 or u % 2 == 0:
                    continue
                b = (u - 3) // 2
                if b >= NB:
                    continue
                act.wait_ge(sem("gn_var"), b + 1)
                inv_sqrt(gs[:, b, 5:6], gs[:, b, 4:5], gs[:, b, 3:4], "gn_rstd", -1.0, "eps5")
                act.wait_ge(sem("gn_affine"), b + 1)
                if b >= 2:
                    act.wait_ge(sem("yg_ready"), b - 1)
                nc.scalar.activation(YN[:, b % 2, :], ybank[b % 2][:], ACT.Identity, bias=gs[:, b, 7:8],
                                     scale=gs[:, b, 6:7]).then_inc(sem("yn_ready"), 1)
            for b in range(NB):
                act.wait_ge(sem("rms2_sum"), b + 1)
                inv_sqrt(rstd[:, tiles(b)], lnv[:, tiles(b)], mv[:, tiles(b), 0], "rms2_rstd", 1.0 / D, "eps6")
            for b in range(NB):
                filled(act, ("h2T", b))
                nc.scalar.activation(HT[:, toks(b)], bank(("h2T", b))[:], ACT.Copy,
                                     scale=vec("ln2")).then_inc(sem("h2T_ready"), 1)
            act.wait_ge(sem("yg_ready"), NB)
            for b in range(NB):
                for m in range(3):
                    n = 3 * b + m
                    filled(act, ("ga", b, m))
                    if n >= 2:
                        act.wait_ge(sem("a_ready"), n - 1)
                    nc.scalar.activation(SG[0:MB[m], n % 2, :], bank(("ga", b, m))[0:MB[m], :],
                                         ACT.Silu).then_inc(sem("silu_ready"), 1)

            def ln_rstd(b, which):
                act.wait_ge(sem(f"{which}_stats"), b + 1)
                inv_sqrt(rstd[:, tiles(b)], lnv[:, tiles(b)], mv[:, tiles(b), 1], f"{which}_rstd", 1.0, "eps5")

            act.preload_act_table_set("natural_log_exp_and_others")
            for b in range(NB):
                ln_rstd(b, "ln1")
            for b in range(NB):
                filled(act, ("x2T", b))
                nc.scalar.copy(HT[:, toks(b)], bank(("x2T", b))[:]).then_inc(sem("x2T_ready"), 1)
                filled(act, ("xq", b))
                nc.scalar.copy(QT[:, toks(b)], bank(("xq", b))[:]).then_inc(sem("xq_ready"), 1)
            for s in range(NT + 5):
                if s < NT:
                    act.wait_ge(sem("sd_ready"), s + 1)
                    nc.scalar.activation(SD[:, s % 4, :], SD[:, s % 4, :], ACT.Exp, scale=SCALE).then_inc(
                        sem("xp_ready"), 1)
                if 2 <= s < NT + 2:
                    filled(act, ("pT", s - 2))
                    if s - 2 >= 4:
                        filled(act, ("pv", s - 6))
                    nc.scalar.copy(PT[:, (s - 2) % 4, :], bank(("pT", s - 2))[:]).then_inc(sem("pT_ready"), 1)
                if s >= 8 and s % TB == 0:
                    b = s // TB - 2
                    filled(act, ("oT", b))
                    nc.scalar.copy(OT[:, toks(b)], bank(("oT", b))[:]).then_inc(sem("oT_ready"), 1)
            for b in range(NB):
                ln_rstd(b, "ln2")
            for b in range(NB):
                filled(act, ("x3T", b))
                nc.scalar.copy(HT[:, toks(b)], bank(("x3T", b))[:]).then_inc(sem("x3T_ready"), 1)
            act.wait_ge(sem("top_ready"), 1)
            nc.scalar.activation(top[:, 2, :], top[:, 2, :], ACT.Exp).then_inc(sem("top_exp"), 1)
            for e in range(NE):
                for f in range(FB):
                    filled(act, ("h1", e, f))
                    if e >= 2:
                        filled(act, ("y", e - 2, 2))
                    nc.scalar.activation(H1A[e % 2][:, f, :], bank(("h1", e, f))[:, 0:CAP], ACT.Gelu,
                                         bias=vec("b1", e * FB + f, 1)).then_inc(sem("h1_ready"), 1)
            act.preload_act_table_set("natural_log_exp_and_others")
            def apply(b, dst, which, name):
                act.wait_ge(sem(f"{which}_shift"), b + 1)
                for t in range(TB * b, TB * b + TB):
                    last = nc.scalar.activation(dst[:, t, :], AM[:, t, :], ACT.Identity, bias=lnv[:, t:t + 1],
                                                scale=rstd[:, t:t + 1])
                last.then_inc(sem(name), 1)

            for b in range(NB + 2):
                if b < NB:
                    ln_rstd(b, "ln3")
                if 2 <= b:
                    ln_rstd(b - 2, "ln4")
                if b < NB:
                    apply(b, AM, "ln3", "ln3_applied")
                if 2 <= b:
                    apply(b - 2, FIN, "ln4", "fin_ready")

        @block.vector
        def _(dve):
            chain = [0]

            def link(ins):
                chain[0] += 1
                ins.then_inc(sem("dve_step"), 1)
                dve.wait_ge(sem("dve_step"), chain[0])

            tt, ts, stt = nc.vector.tensor_tensor, nc.vector.tensor_scalar, nc.vector.scalar_tensor_tensor

            dve.wait_ge(sem("e_ready"), 3)
            link(ts(e_pair, e_pair, 1e19, None, ALU.min))
            ts(e_pair, e_pair, 1.0, None, ALU.add).then_inc(sem("e1_ready"), 1)
            link(ts(e_row, e_row, 1e19, None, ALU.min))
            ts(e_row, e_row, 1.0, None, ALU.add).then_inc(sem("e1_ready"), 1)
            link(ts(e_col, e_col, 1e19, None, ALU.min))
            ts(e_col, e_col, 1.0, None, ALU.add).then_inc(sem("e1_ready"), 1)
            dve.wait_ge(sem("g64_ready"), 1)
            mask = M[:, 0:512].rearrange("p (r t) -> p r t", r=NPAIR)
            tt(mask, const("dist").unsqueeze(1).to_broadcast([P, NPAIR, CS]),
               lg_pair.unsqueeze(2).to_broadcast([P, NPAIR, CS]), ALU.mult).then_inc(sem("logmask_ready"), 1)

            def sum_squares(b, src, name):
                link(tt(by_tile(SQ[:, b % 2, :]), src[:, tiles(b), :], src[:, tiles(b), :], ALU.mult))
                nc.vector.tensor_reduce(mv[:, tiles(b), 0], by_tile(SQ[:, b % 2, :]), AX, ALU.add).then_inc(
                    sem(name), 1)

            for b in range(NB):
                dve.wait_ge(sem(f"in_x{b}"), 16)
                if b >= 2:
                    dve.wait_ge(sem("rms_sum"), b - 1)
                sum_squares(b, X, "rms_sum")
            for b in range(NB):
                dve.wait_ge(sem("rms_rstd"), b + 1)
                tt(Hb[:, tiles(b), :], X[:, tiles(b), :], rstd[:, tiles(b)].unsqueeze(2).to_broadcast([P, TB, D]),
                   ALU.mult).then_inc(sem("h_ready"), 1)
            dve.wait_ge(sem("mask_exp"), 1)
            tt(mask, mask, const("causal").unsqueeze(1).to_broadcast([P, NPAIR, CS]), ALU.mult).then_inc(
                sem("mask_ready"), 1)
            filled(dve, ("ck",))
            nc.vector.tensor_copy(CK[:], bank(("ck",))[:, 0:NB * KC]).then_inc(sem("ck_ready"), 1)
            for b in range(NB):
                filled(dve, ("cv", b))
                tt(VX[:, b, :, 0:32].rearrange("p g (j e) -> p g j e", j=HJ),
                   bank(("cv", b))[:, 0:D].rearrange("p (g j e) -> p g j e", g=HG, j=HJ),
                   const("keyhead").unsqueeze(1).unsqueeze(3).to_broadcast([P, HG, HJ, DH]), ALU.mult).then_inc(
                       sem("cv_ready"), 1)
            nc.vector.tensor_copy(VX[:, :, :, 32:PV].rearrange("p b g j -> p (b g) j"),
                                  const("keyhead").unsqueeze(1).to_broadcast([P, NB * HG, HJ])).then_inc(
                                      sem("vx_ready"), 1)
            for b in range(NB):
                filled(dve, ("q", b))
                dve.wait_ge(sem("q_ready"), b + 1)
                tt(QP[:, 1, toks(b)], bank(("q", b))[:], QP[:, 0, toks(b)], ALU.subtract).then_inc(sem("qlo_ready"), 1)
                dve.wait_ge(sem("dq_ready"), 1)
                tt(QD[:, toks(b)].rearrange("p (c t) -> p c t", t=CS),
                   bank(("q", b))[:].rearrange("p (c t) -> p c t", t=CS),
                   DQ[:].unsqueeze(1).to_broadcast([P, TC, CS]), ALU.mult).then_inc(sem("qd_ready"), 1)
                dve.wait_ge(sem("k_ready"), b + 1)
                if b >= 2:
                    dve.wait_ge(sem("kexp_ready"), b - 1)
                tt(KP[:, b % 2, 1, :], bank(("k", b))[:], KP[:, b % 2, 0, :], ALU.subtract).then_inc(
                    sem("klo_ready"), 1)
                filled(dve, ("kt", b))
                dve.wait_ge(sem("dk_ready"), 1)
                tt(KD[:, tiles(b), :], by_tile(bank(("kt", b))[:]), DK[:].unsqueeze(1).to_broadcast([P, TB, D]),
                   ALU.mult).then_inc(sem("kd_ready"), 1)
                dve.wait_ge(sem("klo_ready"), b + 1)
                for w in range(2):
                    for j in range(HJ):
                        last = ts(KE[:, w, TC * b:TC * b + TC, j, :],
                                  KP[:, b % 2, w, :].rearrange("p (c s) -> p c s", s=CS), const("quad", j, 1), None, ALU.mult)
                last.then_inc(sem("kexp_ready"), 1)
                filled(dve, ("v", b))
                dve.wait_ge(sem("v_ready"), b + 1)
                tt(VP[:, 1, tiles(b), :], by_tile(bank(("v", b))[:]), VP[:, 0, tiles(b), :], ALU.subtract).then_inc(
                    sem("vlo_ready"), 1)

            dve.wait_ge(sem("mask_ready"), 1)

            def score_rest(n):
                dve.wait_ge(sem("phi_ready"), n + 1)
                tt(PP[:, 1, n % 8, :], P32[:, n % 3, :], PP[:, 0, n % 8, :], ALU.subtract).then_inc(
                    sem("plo_ready"), 1)

            for u in range(NS + 4):
                if u >= 3 and u % 2 == 1 and u < 3 + 2 * NB:
                    b = (u - 3) // 2
                    dve.wait_ge(sem("av_done"), TC * (b + 1))
                    link(nc.vector.bn_stats(stats[:, b, :], ybank[b % 2][:]))
                    link(nc.vector.bn_aggr(gs[:, b, 0:2], stats[:, b, :]))
                    stt(gs[:, b, 1:2], gs[:, b, 0:1], gs[:, b, 0:1], gs[:, b, 1:2], ALU.mult, ALU.add).then_inc(
                        sem("gn_part"), 1)
                if u >= 4 and u % 2 == 0:
                    b = (u - 4) // 2
                    dve.wait_ge(sem("gn_rstd"), b + 1)
                    link(tt(gs[:, b, 6:7], gs[:, b, 5:6], vec("gnw"), ALU.mult))
                    link(stt(gs[:, b, 7:8], gs[:, b, 2:3], gs[:, b, 6:7], vec("gnb"), ALU.mult, ALU.subtract))
                    ts(gs[:, b, 7:8], gs[:, b, 7:8], -1.0, None, ALU.mult).then_inc(sem("gn_affine"), 1)
                if u < NS:
                    for g in range(HG):
                        n = HG * u + g
                        filled(dve, ("s", u, g))
                        if n >= 3:
                            dve.wait_ge(sem("plo_ready"), n - 2)
                        tt(P32[:, n % 3, :].rearrange("p (i c) -> p i c", i=SC),
                           bank(("s", u, g))[:].rearrange("p (i c) -> p i c", i=SC),
                           M[:, g * P:(g + 1) * P].unsqueeze(1).to_broadcast([P, SC, P]), ALU.mult).then_inc(
                               sem("p_ready"), 1)
                        if n:
                            score_rest(n - 1)
                    for c in range(SC * u, SC * u + SC):
                        if c % TC == TC - 1:
                            continue
                        n = state_number(c)
                        half = c % 2
                        filled(dve, ("kv", u, half))
                        if n >= 2:
                            dve.wait_ge(sem("state_ready"), n - 1)
                        k = states(u, half).index(c)
                        kv = bank(("kv", u, half))[:, k * D:(k + 1) * D]
                        if c % TC == 0:
                            nc.vector.tensor_copy(SR[:, n % 2, :], kv).then_inc(sem("raw_ready"), 1)
                        else:
                            dve.wait_ge(sem("raw_ready"), n)
                            stt(SR[:, n % 2, :], SR[:, (n - 1) % 2, :], g64, kv, ALU.mult, ALU.add).then_inc(
                                sem("raw_ready"), 1)
                if u == NS:
                    score_rest(HG * NS - 1)
                if u >= 3 and u % 2 == 1 and u < 3 + 2 * NB:
                    b = (u - 3) // 2
                    filled(dve, ("gn", b))
                    link(nc.vector.tensor_copy(gs[:, b, 2:4], bank(("gn", b))[:, 0:2]))
                    stt(gs[:, b, 3:4], gs[:, b, 2:3], gs[:, b, 2:3], gs[:, b, 3:4], ALU.mult,
                        ALU.subtract).then_inc(sem("gn_var"), 1)
                if u >= 4 and u % 2 == 0:
                    b = (u - 4) // 2
                    dve.wait_ge(sem("yn_ready"), b + 1)
                    dve.wait_ge(sem("g_ready"), b + 1)
                    if b >= 2:
                        filled(dve, ("o", b - 2))
                    tt(YG[:, b % 2, :], YN[:, b % 2, :], GT[:, toks(b)], ALU.mult).then_inc(sem("yg_ready"), 1)
                if u >= 5 and u % 2 == 1:
                    b = (u - 5) // 2
                    filled(dve, ("o", b))
                    tt(X1[:, tiles(b), :], by_tile(bank(("o", b))[:]), X[:, tiles(b), :], ALU.add).then_inc(
                        sem("x1_ready"), 1)

            for b in range(NB):
                dve.wait_ge(sem("x1_ready"), b + 1)
                if b >= 2:
                    dve.wait_ge(sem("rms2_sum"), b - 1)
                sum_squares(b, X1, "rms2_sum")
            for b in range(NB):
                dve.wait_ge(sem("rms2_rstd"), b + 1)
                tt(Hb[:, tiles(b), :], X1[:, tiles(b), :], rstd[:, tiles(b)].unsqueeze(2).to_broadcast([P, TB, D]),
                   ALU.mult).then_inc(sem("h2_ready"), 1)

            def layer_stats(b, src, which):
                for t in range(TB * b, TB * b + TB):
                    last = nc.vector.bn_stats(stats[:, t, :], src[:, t, :])
                link(last)
                for t in range(TB * b, TB * b + TB):
                    last = nc.vector.bn_aggr(mv[:, t, :], stats[:, t, :])
                last.then_inc(sem(f"{which}_stats"), 1)

            def layer_apply(b, dst, src, which):
                dve.wait_ge(sem(f"{which}_rstd"), b + 1)
                dve.wait_ge(sem(f"{which}_stats"), b + 1)
                for t in range(TB * b, TB * b + TB):
                    last = ts(dst[:, t, :], src[:, t, :], mv[:, t, 0:1], rstd[:, t:t + 1], ALU.subtract, ALU.mult)
                return last

            def mlp_out(b):
                filled(dve, ("dn", b))
                dve.wait_ge(sem("xx_ready"), b + 1)
                tt(R[:, tiles(b), :], by_tile(bank(("dn", b))[:]), XX[:, tiles(b), :], ALU.add).then_inc(
                    sem("r_ready"), 1)
                dve.wait_ge(sem("r_ready"), b + 1)
                layer_stats(b, R, "ln1")

            for b in range(NB):
                for m in range(3):
                    n = 3 * b + m
                    filled(dve, ("up", b, m))
                    dve.wait_ge(sem("silu_ready"), n + 1)
                    if b >= 2:
                        filled(dve, ("dn", b - 2))
                    tt(A[0:MB[m], 3 * (b % 2) + m, :], bank(("up", b, m))[0:MB[m], :], SG[0:MB[m], n % 2, :],
                       ALU.mult).then_inc(sem("a_ready"), 1)
                if b:
                    mlp_out(b - 1)
            mlp_out(NB - 1)
            dve.wait_ge(sem("av_done"), NB * TC)
            dve.wait_ge(sem("ck_ready"), 1)
            for b in range(NB):
                tt(KX[:, b, :].rearrange("p (h k) -> p h k", h=H),
                   CK[:, b * KC:(b + 1) * KC].unsqueeze(1).to_broadcast([P, H, KC]),
                   const("head").unsqueeze(2).to_broadcast([P, H, KC]), ALU.mult).then_inc(sem("kx_ready"), 1)
            for b in range(NB):
                layer_apply(b, X2, R, "ln1").then_inc(sem("x2_ready"), 1)

            def cross_out(s):
                filled(dve, ("pv", s))
                pv = bank(("pv", s))[:, 0:HG * PV].rearrange("p (g c) -> p g c", g=HG)
                if s >= 2:
                    dve.wait_ge(sem("att_ready"), s - 1)
                link(nc.vector.reciprocal(xden[:, s % 2, :].rearrange("p (g j) -> p g j", g=HG), pv[:, :, 32:PV]))
                tt(ATT[:, s, :].rearrange("p (g j e) -> p g j e", g=HG, j=HJ),
                   pv[:, :, 0:32].rearrange("p g (j e) -> p g j e", j=HJ),
                   xden[:, s % 2, :].rearrange("p (g j) -> p g j", g=HG).unsqueeze(3).to_broadcast([P, HG, HJ, DH]),
                   ALU.mult).then_inc(sem("att_ready"), 1)

            for s in range(NT + 3):
                if s < NT:
                    filled(dve, ("xs", s))
                    sc = bank(("xs", s))[:].rearrange("p (h k) -> p h k", h=H)
                    link(nc.vector.tensor_reduce(xmax[:, s % 2, :], sc, AX, ALU.max))
                    if s >= 4:
                        filled(dve, ("pT", s - 4))
                    tt(SD[:, s % 4, :].rearrange("p (h k) -> p h k", h=H), sc,
                       xmax[:, s % 2, :].unsqueeze(2).to_broadcast([P, H, KC]), ALU.subtract).then_inc(
                           sem("sd_ready"), 1)
                if s >= 3:
                    cross_out(s - 3)
            for b in range(NB):
                filled(dve, ("xo", b))
                tt(R[:, tiles(b), :], by_tile(bank(("xo", b))[:]), X2[:, tiles(b), :], ALU.add).then_inc(
                    sem("r2_ready"), 1)
                dve.wait_ge(sem("r2_ready"), b + 1)
                layer_stats(b, R, "ln2")
            for b in range(NB):
                layer_apply(b, X3, R, "ln2").then_inc(sem("x3_ready"), 1)

            link(nc.vector.tensor_copy(onesb[:], const("same_expert")))
            link(nc.vector.memset(zeroT, 0.0))
            filled(dve, ("rt",))
            tt(logits, bank(("rt",))[:, 0:NT * NE].rearrange("p (t e) -> p t e", e=NE),
               vec("br").unsqueeze(1).to_broadcast([P, NT, NE]), ALU.add).then_inc(sem("logits_ready"), 1)
            dve.wait_ge(sem("logits_ready"), 1)
            iota_te = const("iota_e").unsqueeze(1).to_broadcast([P, NT, NE])

            def wide(v):
                return v.unsqueeze(2).to_broadcast([P, NT, NE])

            def pick(n, src, dst):
                link(nc.vector.tensor_reduce(top[:, n, :], src, AX, ALU.max))
                link(tt(rtmp, src, wide(top[:, n, :]), ALU.is_lt))
                link(stt(rtmp, rtmp, 100.0, iota_te, ALU.mult, ALU.add))
                link(nc.vector.tensor_reduce(top[:, 3, :], rtmp, AX, ALU.min))
                link(tt(dst, iota_te, wide(top[:, 3, :]), ALU.is_equal))

            pick(0, logits, pick1)
            link(stt(logits, pick1, -3e38, logits, ALU.mult, ALU.add))
            pick(1, logits, pick2)
            tt(top[:, 2, :], top[:, 1, :], top[:, 0, :], ALU.subtract).then_inc(sem("top_ready"), 1)
            dve.wait_ge(sem("top_exp"), 1)
            link(ts(top[:, 4, :], top[:, 2, :], 1.0, None, ALU.add))
            link(nc.vector.reciprocal(top[:, 4, :], top[:, 4, :]))
            link(tt(top[:, 5, :], top[:, 2, :], top[:, 4, :], ALU.mult))
            link(tt(rtmp, pick1, pick2, ALU.add))
            link(ts(rtmp, rtmp, -1.0, None, ALU.add))
            link(tt(pick1, pick1, wide(top[:, 4, :]), ALU.mult))
            link(tt(pick2, pick2, wide(top[:, 5, :]), ALU.mult))
            link(tt(pick1, pick1, pick2, ALU.add))
            tt(key_et.rearrange("p e t -> p t e"), pick1, rtmp, ALU.add).then_inc(sem("gate_ready"), 1)
            tt(key_te, pick1, rtmp, ALU.add).then_inc(sem("gates_ready"), 1)

            filled(dve, ("keyT",))
            nc.vector.tensor_copy(keyT, bank(("keyT",))[:, 0:P]).then_inc(sem("key_ready"), 1)
            dve.wait_ge(sem("key_ready"), 1)
            nc.vector.memset(cand[:, 0:1], 0.0).then_inc(sem("thr_ready"), 1)
            dve.wait_ge(sem("in_bits"), 16)
            for r in range(ROUNDS):
                dve.wait_ge(sem("thr_ready"), r + 1)
                link(tt(thr[:, 0:3].bitcast(I32), cand[:, 0:1].bitcast(I32).to_broadcast([P, 3]),
                        BT[:, 3 * r:3 * r + 3], ALU.bitwise_or))
                for j, junk in enumerate((seltmp, eqT, selT)):
                    ts(junk, keyT, thr[:, j:j + 1], None, ALU.is_ge, ALU.add,
                       accum_out=cntb[:, j:j + 1]).then_inc(sem("cnt_ready"), 1)
                filled(dve, ("cnt", r))
                link(stt(cand[:, 1:4], bank(("cnt", r))[:, 0:3], float(CAP), thr[:, 0:3], ALU.is_ge, ALU.mult))
                nc.vector.tensor_reduce(cand[:, 0:1], cand, AX, ALU.max).then_inc(sem("thr_ready"), 1)
            dve.wait_ge(sem("thr_ready"), ROUNDS + 1)
            link(ts(seltmp, keyT, cand[:, 0:1], None, ALU.is_gt, ALU.add, accum_out=nums[:, 0:1]))
            link(ts(eqT, keyT, cand[:, 0:1], None, ALU.is_equal, ALU.add, accum_out=nums[:, 1:2]))
            nc.vector.tensor_tensor_scan(selT, eqT, zeroT, 0.0, ALU.add, ALU.add).then_inc(sem("rows_ready"), 1)
            dve.wait_ge(sem("rows_ready"), 1)
            filled(dve, ("gt",))
            nc.vector.tensor_copy(nums[:, 2:4], bank(("gt",))[:, 0:2]).then_inc(sem("eq_room"), 1)
            dve.wait_ge(sem("eq_room"), 1)
            link(ts(selT, selT, nums[:, 2:3], nums[:, 3:4], ALU.add, ALU.add))
            link(stt(eqT, selT, float(CAP), eqT, ALU.is_le, ALU.mult))
            link(tt(seltmp, seltmp, eqT, ALU.add))
            link(ts(eqT, seltmp, 0.0, None, ALU.add, ALU.add, accum_out=nums[:, 4:5]))
            nc.vector.tensor_tensor_scan(selT, seltmp, zeroT, 0.0, ALU.add, ALU.add).then_inc(sem("sel_ready"), 1)
            dve.wait_ge(sem("sel_ready"), 1)
            filled(dve, ("sel",))
            link(ts(selT, selT, bank(("sel",))[:, 0:1], -1.0 - FAR, ALU.add, ALU.add))
            link(tt(selT, selT, seltmp, ALU.mult))
            ts(posT, selT, float(FAR), None, ALU.add).then_inc(sem("pos_ready"), 1)
            filled(dve, ("posT",))
            nc.vector.tensor_copy(posI, bank(("posT",))[:, 0:P]).then_inc(sem("posT_ready"), 1)
            dve.wait_ge(sem("posT_ready"), 1)
            link(ts(posA.bitcast(I32), posI, SLOT_A - 1, None, ALU.bitwise_and))
            link(ts(posB.bitcast(I32), posI, 5, None, ALU.logical_shift_right))

            def one_hots(g):
                n = slice(2 * NT * g, 2 * NT * (g + 1))
                link(tt(OB[:, n, :], const("iota_b").unsqueeze(1).to_broadcast([P, 2 * NT, SLOT_B]),
                        posB.bitcast(I32)[:, n].unsqueeze(2).to_broadcast([P, 2 * NT, SLOT_B]), ALU.is_equal))
                tt(OA[:, n, :], const("iota_a").unsqueeze(1).to_broadcast([P, 2 * NT, SLOT_A]),
                   posA.bitcast(I32)[:, n].unsqueeze(2).to_broadcast([P, 2 * NT, SLOT_A]),
                   ALU.is_equal).then_inc(sem("onehot_a"), 1)
                for e in (2 * g, 2 * g + 1):
                    m = slice(NT * e, NT * (e + 1))
                    tt(OHI[:, m, :], OB[:, m, :], const("token_hi").unsqueeze(2).to_broadcast([P, NT, SLOT_B]),
                       ALU.mult).then_inc(sem("onehot_hi"), 1)
                ts(OLO[:, n, :], OB[:, n, :], const("token_lo"), None, ALU.mult).then_inc(sem("onehot_ready"), 1)

            def slot_tokens(g):
                filled(dve, ("idx", g))
                lists = bank(("idx", g))[0:SLOT_A, 0:2 * SLOT_B].rearrange("p (e b) -> p e b", e=2)
                for q in range(4):
                    n = 3 if q < SLOT_B - 8 else 2
                    ts(idx[32 * q:32 * q + 32, 2 * g:2 * g + 2, 0:n], lists[:, :, q:SLOT_B:4], float(FAR), None,
                       ALU.add).then_inc(sem("idx_ready"), 1)

            for g in range(NE // 2 + 1):
                if g < NE // 2:
                    one_hots(g)
                if g:
                    slot_tokens(g - 1)

            for e in range(NE + 1):
                if e < NE:
                    for c in range(3):
                        filled(dve, ("xeT", e, c))
                        nc.vector.tensor_copy(XET[:, e % 2, c * P:c * P + CH[c]],
                                              bank(("xeT", e, c))[:, 0:CH[c]]).then_inc(sem("xeT_ready"), 1)
                for c in range(3) if e < NE else []:
                    filled(dve, ("y", e, c))
                    if e >= 2 and c == 0:
                        dve.wait_ge(sem("added"), 16 * 3 * (e - 1))
                    ts(YE[0:CH[c], 3 * (e % 2) + c, :], bank(("y", e, c))[0:CH[c], 0:D],
                       XE[0:CH[c], e % 3, c, D + e:D + e + 1], None, ALU.mult).then_inc(sem("ye_ready"), 1)

            def shift(b, which):
                dve.wait_ge(sem(f"{which}_rstd"), b + 1)
                stt(lnv[:, tiles(b)], mv[:, tiles(b), 0], -1.0, rstd[:, tiles(b)], ALU.mult, ALU.mult).then_inc(
                    sem(f"{which}_shift"), 1)

            for b in range(NB + 2):
                if b < NB:
                    dve.wait_ge(sem(f"in_sum{b}"), 16)
                    layer_stats(b, AM, "ln3")
                if 2 <= b:
                    dve.wait_ge(sem("sum_ready"), b - 1)
                    layer_stats(b - 2, AM, "ln4")
                if b < NB:
                    shift(b, "ln3")
                if 2 <= b:
                    shift(b - 2, "ln4")
                if 1 <= b <= NB:
                    dve.wait_ge(sem("ln3_applied"), b)
                    tt(AM[:, tiles(b - 1), :], AM[:, tiles(b - 1), :],
                       vec("fg").unsqueeze(1).to_broadcast([P, TB, D]), ALU.mult).then_inc(sem("scaled_ready"), 1)


def constants():
    c = np.zeros((P, NCONST), np.float32)
    i, j = np.arange(P)[:, None], np.arange(P)[None, :]

    def put(name, value):
        at, n = CONST[name]
        c[:, at:at + n] = value

    put("ident", i == j)
    put("blockdiag", i // DH == j // DH)
    put("headmean", (i // DH == j // DH) / DH)
    jc = np.arange(CS)[None, :]
    put("causal", jc >= i % CS)
    put("dist", np.maximum(jc - i % CS, 0))
    put("after", jc + 1)
    put("same_expert", i // NT == j // NT)
    put("earlier_tile", (i // NT == j // NT) & (i % NT < j % NT))
    put("left", CS - 1 - i % CS)
    put("quad", (i % 32) // DH == np.arange(HJ))
    put("head", i // DH == np.arange(H))
    put("keyhead", i // KC == np.arange(HJ))
    put("iota_a", np.arange(SLOT_A))
    put("iota_b", np.arange(SLOT_B))
    put("token_hi", P * np.arange(NT) - FAR)
    put("token_lo", i)
    put("iota_e", np.arange(NE))
    put("eps6", 1e-6)
    put("eps5", 1e-5)
    put("ones", 1)
    bits = np.zeros((P, 3 * ROUNDS), np.int32)
    for r in range(ROUNDS):
        for n in range(3):
            bits[:, 3 * r + n] = (n + 1) << (BITS - 2 - 2 * r)
    return c, bits


def kernel(**inputs):
    import concourse.bacc as bacc
    from concourse.bass_utils import run_bass_kernel_spmd

    a = {k: np.asarray(v) for k, v in inputs.items()}

    def attn(n):
        return a["L0_attn_" + n]

    c, bits = constants()
    w1 = np.concatenate([attn(n).T for n in ("Wq", "Wk", "Wv", "Wg", "Wo")], 1)
    down = np.zeros((P, 3, D), np.float32)
    for m in range(3):
        down[:MB[m], m] = attn("down_w").T[P * m:P * m + MB[m]]
    ctx = a["ctx_1024"].transpose(2, 0, 1)
    ctxrep = np.broadcast_to(ctx[:, :, None, :], (D, NB, HJ, KC))
    w2 = np.concatenate([attn("gate_w").T, attn("up_w").T, down.reshape(P, -1)]
                        + [a["L0_xattn_W_" + n].T for n in "qkvo"]
                        + [ctx.reshape(D, -1), ctxrep.reshape(D, -1), a["L0_ffn_Wr"]], 1)

    def row(v):
        return np.broadcast_to(v.reshape(1, -1), (P, v.size))

    vecs = np.concatenate([attn("ln1_w")[:, None], attn("ln2_w")[:, None], attn("gn_w")[:, None],
                           attn("gn_b")[:, None], np.repeat(attn("gamma"), DH)[:, None], row(attn("gamma")),
                           attn("gamma").reshape(NPAIR, 2).T.repeat(CS, 0),
                           row(a["L0_ffn_br"]), row(a["L0_ffn_gamma"]), row(a["L0_ffn_beta"]),
                           a["L0_ffn_b1"].reshape(NE * FB, P).T, row(a["L0_ffn_b2"])], 1)
    ew1 = a["L0_ffn_W1"].transpose(1, 0, 2)
    ew2 = a["L0_ffn_W2"].reshape(NE, FB, P, D).transpose(2, 0, 1, 3)
    arrays = {"x_dram": a["x"].reshape(N, D), "const_dram": c, "bits_dram": bits, "w1_dram": w1, "w2_dram": w2,
              "vec_dram": vecs, "ew1_dram": ew1, "ew2_dram": ew2}
    arrays = {k: np.ascontiguousarray(v) for k, v in arrays.items()}
    nc = bacc.Bacc("TRN2", target_bir_lowering=False, num_devices=1)
    args = [nc.dram_tensor(k, v.shape, mybir.dt.from_np(v.dtype), kind="ExternalInput").ap()
            for k, v in arrays.items()]
    args.append(nc.dram_tensor("out_dram", [N, D], F32, kind="ExternalOutput").ap())
    decoder_layer(nc, *args)
    r = run_bass_kernel_spmd(nc, [arrays], core_ids=[0])
    return r.results[0]["out_dram"].reshape(NB, T, D)
```

```python
from contextlib import ExitStack

import numpy as np

import concourse.bass as bass
from concourse import mybir

F32 = mybir.dt.float32
BF16 = mybir.dt.bfloat16
I32 = mybir.dt.int32
ALU = mybir.AluOpType
ACT = mybir.ActivationFunctionType
AX = mybir.AxisListType.X

P = 128
NB, T, D = 4, 512, 128
N = NB * T
NT = N // P
TB = T // P
H = 16
DH = D // H
HG = 4
HJ = H // HG
INNER = 352
MB = [128, 128, 96]
CS = 64
TC = T // CS
NPAIR = H // 2
SC = 4
NS = N // (CS * SC)
SB = NS // NB
KC = 32
NE, TOPK = 8, 2
FF = 512
FB = FF // P
CAP = (N * 5 // 4 + NE - 1) // NE
CH = [128, 128, CAP - 256]
SLOT_A, SLOT_B = 32, CAP // 32
XS = 4
FAR = 4096
BITS = 30
ROUND_BITS = 3
ROUNDS = BITS // ROUND_BITS
NC = 2 ** ROUND_BITS - 1
NT_FIRST = 9
PV = 32 + HJ
SCALE = float(DH) ** -0.5
ACT_BATCHES = (0, 1, 2)

GATES_AT, CONTEXT_AT = 1, 2
GN_AT = {3: 0, 5: 1, 7: 2}
YG_AT = {4: 0, 6: 1, 8: 2}
OUT_AT = {5: 0, 7: 1}
H2_AT = {6: 0, 8: 1}
H2T_AT = {7: 0}
X2_AT = {2: 3}
X2T_AT = {1: 2, 4: 3}
XQ_AT = {3: 2, 6: 3}
UNITS = [(0, TB), (TB, TB), (2 * TB, TB), (3 * TB, TB // 2), (3 * TB + TB // 2, TB // 2)]
NU = len(UNITS)
OT_AT = {8: 0, 12: 1, 16: 2, 18: 3, 19: 4}
XO_AT = {9: 0, 13: 1, 17: 2, 19: 3, 20: 4}
X3_AT = {10: 0, 14: 1, 18: 2, 20: 3, 21: 4}
X3T_AT = {13: 0, 17: 1, 20: 2, 21: 3, 22: 4}
RT_AT = {14: 0, 18: 1, 21: 2, 22: 3, 23: 4}
CROSS_STEPS = NT + 8

CONST = {}
_at = 0
for _name, _n in [("ident", 128), ("blockdiag", 128), ("headmean", 128), ("causal", CS), ("dist", CS),
                  ("after", CS), ("same_tile", 128), ("later", 128), ("left", 1), ("quad", HJ),
                  ("head", H), ("keyhead", HJ), ("iota_a", SLOT_A), ("iota_b", SLOT_B), ("token_hi", NT), ("token_lo", 1),
                  ("same_token", P), ("eps6", 1), ("eps5", 1), ("ones", 128)]:
    CONST[_name] = (_at, _n)
    _at += _n
NCONST = _at

W1COLS = {n: (i * 128, 128) for i, n in enumerate(["q", "k", "v", "g", "o"])}
W2COLS = {}
_at = 0
for _name, _n in [("gate", INNER), ("up", INNER), ("down", 3 * 128), ("xq", 128), ("xk", 128), ("xv", 128),
                  ("xo", 128), ("ctx", NB * KC), ("ctxrep", NB * HJ * KC), ("router", NE)]:
    W2COLS[_name] = (_at, _n)
    _at += _n
NW2 = _at
VEC = {}
_at = 0
for _name, _n in [("ln1", 1), ("ln2", 1), ("gnw", 1), ("gnb", 1), ("gamma_col", 1), ("gamma_row", H), ("gamma_pair", NPAIR),
                  ("br", NE), ("fg", D), ("fb", D), ("b1", NE * FB), ("b2", NE * D)]:
    VEC[_name] = (_at, _n)
    _at += _n
NVEC = _at


def states(u, half):
    chunks = [SC * u + 2 * k + half for k in range(SC // 2)]
    return [c for c in chunks if c % TC < TC - 1]


def state_number(c):
    return (TC - 1) * (c // TC) + c % TC


def last_state(u, half):
    return state_number(states(u, half)[-1])


def plan_psum():
    jobs = []

    def job(key, sem, value):
        jobs.append((key, sem, value))

    for b in range(2):
        job(("hT", b), "hT_ready", b + 1)
    for b in range(NB):
        job(("q", b), "qd_ready", b + 1)
        job(("k", b), "klo_ready", b + 1)
        if b + 2 < NB:
            job(("hT", b + 2), "hT_ready", b + 3)
        job(("kt", b), "kd_ready", b + 1)
        job(("v", b), "v_ready", b + 1)
    for u in range(NS + 1):
        if u < NS:
            for g in range(HG):
                job(("s", u, g), "p_ready", HG * u + g + 1)
            for half in range(2):
                job(("kv", u, half), "raw_ready", last_state(u, half) + 1)
        if u == GATES_AT:
            for b in range(NB):
                job(("g", b), "g_ready", b + 1)
        if u == CONTEXT_AT:
            job(("ck",), "ck_ready", 1)
            for b in range(NB):
                job(("cv", b), "cv_ready", b + 1)
        if u in GN_AT:
            job(("gn", GN_AT[u]), "gn_var", GN_AT[u] + 1)
        if u in OUT_AT:
            job(("o", OUT_AT[u]), "x1_ready", OUT_AT[u] + 1)
        if u in H2T_AT:
            job(("h2T", H2T_AT[u]), "h2lo_ready", H2T_AT[u] + 1)

    def gates_up(b):
        for m in range(3):
            job(("ga", b, m), "silu_ready", 3 * b + m + 1)
            job(("up", b, m), "a_ready", 3 * b + m + 1)

    job(("gn", 3), "gn_var", 4)
    job(("o", 2), "x1_ready", 3)
    job(("h2T", 1), "h2lo_ready", 2)
    gates_up(0)
    job(("o", 3), "x1_ready", 4)
    job(("h2T", 2), "h2lo_ready", 3)
    gates_up(1)
    job(("dn", 0), "r_ready", 1)
    job(("h2T", 3), "h2lo_ready", 4)
    gates_up(2)
    job(("dn", 1), "r_ready", 2)
    job(("x2T", 0), "x2T_ready", 1)
    gates_up(3)
    job(("xq", 0), "xq_ready", 1)
    job(("dn", 2), "r_ready", 3)
    job(("x2T", 1), "x2T_ready", 2)
    job(("dn", 3), "r_ready", 4)
    job(("xq", 1), "xq_ready", 2)
    for s in range(CROSS_STEPS):
        if s < NT:
            job(("xs", s), "sd_ready", s + 1)
        if s in X2T_AT:
            job(("x2T", X2T_AT[s]), "x2T_ready", X2T_AT[s] + 1)
        if s in XQ_AT:
            job(("xq", XQ_AT[s]), "xq_ready", XQ_AT[s] + 1)
        if 2 <= s < NT + 2:
            job(("pT", s - 2), "pT_ready", s - 1)
        if 4 <= s < NT + 4:
            job(("pv", s - 4), "att_ready", s - 3)
        if s in OT_AT:
            job(("oT", OT_AT[s]), "oT_ready", OT_AT[s] + 1)
        if s in XO_AT:
            job(("xo", XO_AT[s]), "r2_ready", XO_AT[s] + 1)
        if s in X3T_AT:
            job(("x3T", X3T_AT[s]), "x3T_ready", X3T_AT[s] + 1)
        if s in RT_AT:
            job(("rt", RT_AT[s]), "logits_ready", RT_AT[s] + 1)
    for r in range(ROUNDS):
        job(("cnt", r), "thr_ready", r + 2)
    job(("eq",), "sel_ready", 1)
    job(("sel",), "pos_ready", 1)

    def slots(e):
        job(("idx", e), "idx_ready", 4 * (e + 1))

    def transposed(e, chunks=range(3)):
        for c in chunks:
            job(("xeT", e, c), "xeT_ready", 3 * e + c + 1)

    def hidden(e):
        for f in range(FB):
            job(("h1", e, f), "h1_ready", FB * e + f + 1)

    for e in range(4):
        slots(e)
    transposed(0)
    slots(4)
    hidden(0)
    transposed(1)
    for e in range(NE):
        if e + 1 < NE:
            hidden(e + 1)
        job(("y", e, 0), "ye_ready", 3 * e + 1)
        if e + 2 < NE:
            transposed(e + 2)
        job(("y", e, 1), "ye_ready", 3 * e + 2)
        job(("y", e, 2), "ye_ready", 3 * e + 3)
        if e + 5 < NE:
            slots(e + 5)
    return jobs


def decoder_layer(nc, x, consts, bits, w1, w2, vecs, ew1, ew2, out):
    ctx = ExitStack()
    with ctx:
        def sb(name, shape, dt=F32):
            return ctx.enter_context(nc.sbuf_tensor(name, shape, dt))

        sems = {}

        def sem(name):
            if name not in sems:
                sems[name] = ctx.enter_context(nc.semaphore(name))
            return sems[name]

        ring = [ctx.enter_context(nc.psum_tensor(f"ring{i}", [P, 512], F32)) for i in range(6)]
        ybank = [ctx.enter_context(nc.psum_tensor(f"ybank{i}", [P, 512], F32)) for i in range(2)]
        jobs = plan_psum()
        wide = [key for key, _, _ in jobs].index(("ga", 1, 0))
        later = [6, 7] + [(wide + i) % 6 for i in range(6)]
        place, number, before, fills = {}, {}, {}, [0] * 8
        release = [None] * 6 + [("yn_ready", NB)] * 2
        for n, (key, done_sem, value) in enumerate(jobs):
            i = n % 6 if n < wide else later[(n - wide) % 8]
            fills[i] += 1
            place[key], number[key], before[key] = i, fills[i], release[i]
            release[i] = (done_sem, value)

        def bank(key):
            return (ring + ybank)[place[key]]

        def room(pe, key):
            if before[key]:
                pe.wait_ge(sem(before[key][0]), before[key][1])

        bank_full = [sem(f"bank_full{i}") for i in range(8)]

        def filled(eng, key):
            eng.wait_ge(bank_full[place[key]], number[key])

        rows = nc.dram_tensor("rows_dram", [N, D + NE], F32, kind="Internal").ap()
        acc = nc.dram_tensor("acc_dram", [N, D], F32, kind="Internal").ap()

        X = sb("X", [P, NT, D])
        Hb = sb("Hb", [P, NT, D])
        HT = sb("HT", [P, N])
        QT = sb("QT", [P, N])
        BIG = sb("BIG", [P, HJ * N])
        QD = sb("QD", [P, N])
        KD = sb("KD", [P, NT, D])
        V = sb("V", [P, NT, D])
        VZB = sb("VZB", [P, 4 * 2 * N], BF16)[:]
        VZ = VZB.bitcast(F32).rearrange("p (s c) -> p s c", s=4)
        GT = sb("GT", [P, N])
        M = sb("M", [P, H * P])
        X1 = sb("X1", [P, NT, D])
        PB = sb("PB", [P, 8, 512])
        SR = sb("SR", [P, 4, D])
        SM = sb("SM", [P, 4, D])
        P32 = sb("P32", [P, 3, 512])
        YN = sb("YN", [P, 2, 512])
        YG = sb("YG", [P, 2, 512])
        C = sb("C", [P, NCONST])
        W1 = sb("W1", [P, 5 * 128])
        W2 = sb("W2", [P, NW2])
        VC = sb("VC", [P, NVEC])
        BT = sb("BT", [P, NC * ROUNDS], I32)
        DQ = sb("DQ", [P, CS])
        DK = sb("DK", [P, P])
        small = sb("small", [P, 256])
        mv = sb("mv", [P, NT, 2])
        stats = sb("stats", [P, NT, 6])
        rstd = sb("rstd", [P, NT])
        lnv = sb("lnv", [P, NT])
        CK = sb("CK", [P, NB * KC])
        GU = sb("GU", [P, 2, 2 * INNER], BF16)
        VX = sb("VX", [P, NB, HG, PV])

        H2P = HT[:].bitcast(BF16).rearrange("p (b w n) -> p b w n", b=NB, w=2)
        QP = QT[:].bitcast(BF16).rearrange("p (w n) -> p w n", w=2)
        KE = BIG[:].bitcast(BF16).rearrange(
            "p (w c j s) -> p w c j s", w=2, j=HJ, s=CS)
        KP = YG[:].rearrange("p s c -> p (s c)").bitcast(BF16).rearrange("p (s w n) -> p s w n", s=2, w=2)
        VP = Hb[:].rearrange("p t d -> p (t d)").bitcast(BF16).rearrange("p (w t d) -> p w t d", w=2, d=D)
        PP = PB[:].rearrange("p s c -> p (s c)").bitcast(BF16).rearrange("p (w s c) -> p w s c", w=2, c=512)
        VS = VZB.rearrange(
            "p (u i w r d) -> p u i w r d", u=2, i=SC, w=2, r=NPAIR)
        R = QD[:].rearrange("p (t d) -> p t d", d=D)
        X2 = KD
        H2 = KD
        ATT = V
        X3 = GT[:].rearrange("p (t d) -> p t d", d=D)
        OT = M
        KX = VZ[:, 0, :].rearrange("p (b c) -> p b c", b=NB)
        SD = VZ[:, 1, :].rearrange("p (s c) -> p s c", s=4)
        PT = VZ[:, 2, :].rearrange("p (s c) -> p s c", s=4)
        A = PB[:, 0:6, :]
        SG = P32
        EW1 = BIG[:, 0:NE * FF].rearrange("p (e f) -> p e f", e=NE)
        EW2 = BIG[:, NE * FF:2 * NE * FF].rearrange("p (e f d) -> p e f d", e=NE, d=D)

        def const(name, a=0, n=None):
            at, width = CONST[name]
            return C[:, at + a:at + a + (width if n is None else n)]

        def wa(name, a=0, n=None):
            at, width = W1COLS[name]
            return W1[:, at + a:at + a + (width if n is None else n)]

        def wb(name, a=0, n=None):
            at, width = W2COLS[name]
            return W2[:, at + a:at + a + (width if n is None else n)]

        def vec(name, a=0, n=None):
            at, width = VEC[name]
            return VC[:, at + a:at + a + (width if n is None else n)]

        def tiles(b):
            return slice(TB * b, TB * b + TB)

        def toks(b):
            return slice(T * b, T * b + T)

        def by_tile(ap):
            return ap.rearrange("p (t d) -> p t d", d=D)

        e_row, lg_row = small[:, 0:H], small[:, 16:16 + H]
        e_col, lg_col, g64 = small[:, 32:33], small[:, 33:34], small[:, 34:35]
        e_pair, lg_pair = small[:, 150:158], small[:, 158:166]
        gs = small[:, 36:68].rearrange("p (b c) -> p b c", b=NB)
        xmax = small[:, 80:112].rearrange("p (s h) -> p s h", s=2)
        xden = small[:, 112:144].rearrange("p (s h) -> p s h", s=2)

        RB = PB[:, 0:2, :].rearrange("p s c -> p (s c)")
        logits = RB[:, 0:128].rearrange("p (t e) -> p t e", e=NE)
        rtmp = RB[:, 128:256].rearrange("p (t e) -> p t e", e=NE)
        pick1 = RB[:, 256:384].rearrange("p (t e) -> p t e", e=NE)
        pick2 = RB[:, 384:512].rearrange("p (t e) -> p t e", e=NE)
        key_et = RB[:, 512:640].rearrange("p (e t) -> p e t", e=NE)
        RC = PB[:, 2, :]
        top = RC[:, 0:96].rearrange("p (n t) -> p n t", t=NT)
        thr = RC[:, 96:96 + NC * NE].rearrange("p (c e) -> p c e", e=NE)
        cand = RC[:, 152:152 + 2 * (NC + 1) * NE].rearrange("p (s c e) -> p s c e", s=2, e=NE)
        above = PB[:, 7, :].bitcast(BF16)[:, 0:NC * P].rearrange("p (c e t) -> p c e t", e=NE, t=NT)
        chosen = PB[:, 3, 0:256].bitcast(BF16)
        gt_th, eq_th, running, sel = [chosen[:, k * P:(k + 1) * P].rearrange("p (e t) -> p e t", e=NE)
                                      for k in range(4)]
        gt_sum = RC[:, 280:284].bitcast(BF16)
        slot = RC[:, 288:416]
        slotI = PB[:, 4, 128:256].bitcast(I32)
        posA = PB[:, 3, 256:384]
        posB = PB[:, 3, 384:512]
        onesb = sb("onesb", [P, P], BF16)
        laterb = PB[:, 6, 256:320].bitcast(BF16)
        segb = PB[:, 6, 320:384].bitcast(BF16)
        OA = VZB[:, 0:P * SLOT_A].rearrange("p (n a) -> p n a", a=SLOT_A)
        OB, OHI, OLO = [VZB[:, P * (SLOT_A + k * SLOT_B):P * (SLOT_A + (k + 1) * SLOT_B)].rearrange(
            "p (n b) -> p n b", b=SLOT_B) for k in range(3)]
        key_te = PB[:, 4, 0:128].rearrange("p (t e) -> p t e", e=NE)
        X3F = V
        idx = sb("idx", [P, NE, 3], I32)
        XE = QT[:, 0:XS * 3 * (D + NE)].rearrange("p (s c d) -> p s c d", s=XS, d=D + NE)
        XET = X1[:].rearrange("p t d -> p (t d)")[:, 0:2 * CAP].rearrange("p (s c) -> p s c", s=2)
        H1A = [M[:, 0:FB * CAP].rearrange("p (f c) -> p f c", f=FB),
               QD[:, 0:FB * CAP].rearrange("p (f c) -> p f c", f=FB)]
        YE = PB[:, 5:7, :].rearrange("p s c -> p (s c)")[:, 0:6 * D].rearrange("p (s d) -> p s d", d=D)
        AM = KD
        FIN = HT[:].rearrange("p (t d) -> p t d", d=D)

        def strips(u, half, part, head):
            base = VS[CS * head:CS * head + CS, u % 2, half, part, 0, DH * head:DH * head + DH]
            chunk = SC // 2 * 2 * NPAIR * D
            return bass.AP(base.tensor, base.offset, [list(base.ap[0]), [chunk, SC // 2], [D + 2 * DH, NPAIR],
                                                      [1, DH]])

        def unit(k):
            return slice(UNITS[k][0], sum(UNITS[k]))

        def x3_made(eng, k):
            if k < NB - 1:
                eng.wait_ge(sem("x3_ready"), k + 1)
            else:
                eng.wait_ge(sem("x3_last"), k - NB + 2)

        block = ctx.enter_context(nc.Block())

        @block.sync
        def _(sp):
            xv = x.rearrange("(t p) d -> p t d", p=P)
            few = VEC["fg"][0]
            sp.dma_start(X[:, tiles(0), :], xv[:, tiles(0), :]).then_inc(sem("in_x0"), 16)
            sp.dma_start(VC[:, 0:few], vecs[:, 0:few]).then_inc(sem("in_vec"), 16)
            sp.dma_start(C[:], consts).then_inc(sem("in_const"), 16)
            sp.dma_start(X[:, tiles(1), :], xv[:, tiles(1), :]).then_inc(sem("in_x1"), 16)
            sp.dma_start(W1[:], w1).then_inc(sem("in_w1"), 16)
            for b in range(2, NB):
                sp.dma_start(X[:, tiles(b), :], xv[:, tiles(b), :]).then_inc(sem(f"in_x{b}"), 16)
            sp.dma_start(W2[:], w2).then_inc(sem("in_w2"), 16)
            sp.dma_start(VC[:, few:], vecs[:, few:]).then_inc(sem("in_vec2"), 16)
            sp.dma_start(BT[:], bits).then_inc(sem("in_bits"), 16)
            sp.wait_ge(sem("av_done"), NB * TC)
            sp.dma_start(EW1, ew1).then_inc(sem("in_ew"), 16)
            sp.dma_start(EW2, ew2).then_inc(sem("in_ew"), 16)
            for k in range(NU):
                x3_made(sp, k)
                for dst in (rows[:, 0:D], acc):
                    sp.dma_start(dst.rearrange("(t p) d -> p t d", p=P)[:, unit(k), :],
                                 X3[:, unit(k), :]).then_inc(sem("x3_stored"), 16)
            sp.wait_ge(sem("gates_ready"), 1)
            sp.dma_start(rows[:, D:D + NE].rearrange("(t p) e -> p t e", p=P), key_te).then_inc(sem("x3_stored"), 16)
            sp.wait_ge(sem("added"), 16 * 3 * NE)
            for b in range(NB):
                sp.dma_start(AM[:, tiles(b), :], acc.rearrange("(t p) d -> p t d", p=P)[:, tiles(b), :]).then_inc(
                    sem(f"in_sum{b}"), 16)
            for b in range(NB):
                if b < NB - 1:
                    sp.wait_ge(sem("fin_ready"), b + 1)
                else:
                    sp.wait_ge(sem("fin_last"), 1)
                sp.dma_start(out.rearrange("(t p) d -> p t d", p=P)[:, tiles(b), :],
                             FIN[:, tiles(b), :]).then_inc(sem("stored"), 16)
            sp.wait_ge(sem("stored"), 16 * NB)

        @block.gpsimd
        def _(pool):
            nc.gpsimd.memset(VZ, 0.0).then_inc(sem("vz_zero"), 1)
            pool.wait_ge(sem("vz_zero"), 1)

            def spread_v(u):
                pool.wait_ge(sem("vlo_ready"), u // SB + 1)
                if u >= 2:
                    pool.wait_ge(sem("av_done"), SC * (u - 1))
                    pool.wait_ge(sem("vz_ready"), 8 * (u - 1))
                for part in range(2):
                    for half in range(2):
                        for head in range(2):
                            src = VP[CS * half:CS * half + CS, part, 2 * u:2 * u + 2, :].rearrange(
                                "p t (r a e) -> p t r a e", a=2, e=DH)[:, :, :, head, :]
                            nc.gpsimd.tensor_copy(strips(u, half, part, head), src).then_inc(sem("vz_ready"), 1)
                            pool.wait_ge(sem("vz_ready"), 8 * u + 4 * part + 2 * half + head + 1)

            def mask_state(c):
                n = state_number(c)
                pool.wait_ge(sem("raw_ready"), n + 1)
                if c > 2:
                    pool.wait_ge(sem("av_done"), c - 2)
                if n:
                    pool.wait_ge(sem("state_ready"), n)
                nc.gpsimd.tensor_tensor(SM[:, c % 4, :], SR[:, n % 4, :], const("blockdiag"), ALU.mult).then_inc(
                    sem("state_ready"), 1)

            def v_rest(b):
                pool.wait_ge(sem("vhi_ready"), b + 1)
                pool.wait_ge(sem("v_ready"), b + 1)
                nc.gpsimd.tensor_tensor(VP[:, 1, tiles(b), :], V[:, tiles(b), :], VP[:, 0, tiles(b), :],
                                        ALU.subtract).then_inc(sem("vlo_ready"), 1)

            v_rest(0)
            spread_v(0)
            spread_v(1)
            for b in range(1, NB):
                v_rest(b)
            for u in range(NS):
                for c in range(SC * u, SC * u + SC):
                    if c % TC < TC - 1:
                        mask_state(c)
                if u >= 1 and u + 1 < NS:
                    spread_v(u + 1)
                if u == CONTEXT_AT:
                    pool.wait_ge(sem("guhi_ready"), 1)
                    nc.gpsimd.tensor_tensor(GU[:, 1, :], W2[:, 0:2 * INNER], GU[:, 0, :], ALU.subtract).then_inc(
                        sem("gulo_ready"), 1)
            def residual(b):
                pool.wait_ge(sem("x1_ready"), b + 1)
                nc.gpsimd.tensor_tensor(X[:, tiles(b), :], X[:, tiles(b), :], X1[:, tiles(b), :],
                                        ALU.add).then_inc(sem("xx_ready"), 1)

            residual(0)
            residual(1)
            pool.wait_ge(sem("av_done"), NB * TC)
            pool.wait_ge(sem("ck_ready"), 1)
            for b in range(NB):
                nc.gpsimd.tensor_tensor(KX[:, b, :].rearrange("p (h k) -> p h k", h=H),
                                        CK[:, b * KC:(b + 1) * KC].unsqueeze(1).to_broadcast([P, H, KC]),
                                        const("head").unsqueeze(2).to_broadcast([P, H, KC]),
                                        ALU.mult).then_inc(sem("kx_ready"), 1)
                if b >= 2:
                    residual(b)
            for b in range(NB - 1):
                pool.wait_ge(sem("ln2_stats"), b + 1)
                nc.gpsimd.tensor_tensor(X3[:, tiles(b), :], R[:, tiles(b), :],
                                        mv[:, tiles(b), 0].unsqueeze(2).to_broadcast([P, TB, D]),
                                        ALU.subtract).then_inc(sem("x3_centred"), 1)
                pool.wait_ge(sem("x3_centred"), b + 1)
                pool.wait_ge(sem("ln2_rstd"), b + 1)
                nc.gpsimd.tensor_tensor(X3[:, tiles(b), :], X3[:, tiles(b), :],
                                        rstd[:, tiles(b)].unsqueeze(2).to_broadcast([P, TB, D]),
                                        ALU.mult).then_inc(sem("x3_ready"), 1)
            pool.wait_ge(sem("x3T_ready"), NU)
            nc.gpsimd.memset(XE, 0.0).then_inc(sem("xe_zero"), 1)
            pool.wait_ge(sem("xe_zero"), 1)
            pool.wait_ge(sem("x3_stored"), 16 * (2 * NU + 1))

            def gather(e):
                pool.wait_ge(sem("idx_ready"), 4 * (e + 1))
                if e >= XS:
                    pool.wait_ge(sem("ye_ready"), 3 * (e - XS + 1))
                for c in range(3):
                    nc.gpsimd.indirect_dma_start(
                        out=XE[0:CH[c], e % XS, c, :], out_offset=None, in_=rows,
                        in_offset=bass.IndirectOffsetOnAxis(ap=idx[0:CH[c], e, c:c + 1], axis=0),
                        bounds_check=N - 1, oob_is_err=False).then_inc(sem(f"gathered{e % XS}"), 16)

            def scatter(e):
                for c in range(3):
                    pool.wait_ge(sem("ye_ready"), 3 * e + c + 1)
                    if e and c == 0:
                        pool.wait_ge(sem("added"), 16 * 3 * e)
                    nc.gpsimd.indirect_dma_start(
                        out=acc, out_offset=bass.IndirectOffsetOnAxis(ap=idx[0:CH[c], e, c:c + 1], axis=0),
                        in_=YE[0:CH[c], 3 * (e % 2) + c, :], in_offset=None,
                        bounds_check=N - 1, oob_is_err=False, compute_op=ALU.add).then_inc(sem("added"), 16)

            for e in range(XS - 1):
                gather(e)
            for e in range(NE):
                if e + XS - 1 < NE:
                    gather(e + XS - 1)
                scatter(e)
            pool.wait_ge(sem("x3f_ready"), NB)
            for n, b in enumerate(ACT_BATCHES):
                pool.wait_ge(sem("ln3_applied"), n + 1)
                nc.gpsimd.tensor_tensor(AM[:, tiles(b), :], AM[:, tiles(b), :],
                                        vec("fg").unsqueeze(1).to_broadcast([P, TB, D]), ALU.mult).then_inc(
                                            sem("scaled_ready"), 1)
                pool.wait_ge(sem("scaled_ready"), n + 1)
                nc.gpsimd.tensor_tensor(AM[:, tiles(b), :], AM[:, tiles(b), :], X3F[:, tiles(b), :],
                                        ALU.add).then_inc(sem("sum_ready"), 1)

        @block.tensor
        def _(pe):
            def transposes(key, src, n=TB):
                room(pe, key)
                for t in range(n):
                    last = nc.tensor.transpose(bank(key)[:, t * P:(t + 1) * P], src(t), const("ident"))
                last.then_inc(bank_full[place[key]], 1)

            def done(key, last):
                last.then_inc(bank_full[place[key]], 1)


            def token_layout(key, b, w):
                room(pe, key)
                for t in range(TB):
                    s = TB * b + t
                    last = nc.tensor.matmul(bank(key)[:, t * D:(t + 1) * D], HT[:, s * P:(s + 1) * P], w,
                                            start=True, stop=True)
                done(key, last)

            pe.wait_ge(sem("in_const"), 16)

            def h_to_T(b):
                pe.wait_ge(sem("h_ready"), b + 1)
                transposes(("hT", b), lambda t: Hb[:, TB * b + t, :])

            h_to_T(0)
            h_to_T(1)
            pe.wait_ge(sem("in_w1"), 16)
            for b in range(NB):
                pe.wait_ge(sem("hT_ready"), b + 1)
                for n in "qk":
                    room(pe, (n, b))
                    done((n, b), nc.tensor.matmul(bank((n, b))[:], wa(n), HT[:, toks(b)], start=True, stop=True))
                if b + 2 < NB:
                    h_to_T(b + 2)
                token_layout(("kt", b), b, wa("k"))
                token_layout(("v", b), b, wa("v"))
            PARTS = ((0, 0), (0, 1), (1, 0))

            def scores(u):
                pe.wait_ge(sem("kexp_ready"), u // SB + 1)
                pe.wait_ge(sem("kexp_act"), u // SB + 1)
                pe.wait_ge(sem("qd_ready"), u // SB + 1)
                for g in range(HG):
                    key = ("s", u, g)
                    room(pe, key)
                    rows32 = slice(32 * g, 32 * g + 32)
                    for i in range(SC):
                        at = slice(CS * (SC * u + i), CS * (SC * u + i + 1))
                        for r in range(2):
                            for wk, wq in PARTS:
                                last = nc.tensor.matmul(bank(key)[:, (2 * i + r) * CS:(2 * i + r + 1) * CS],
                                                        KE[rows32, wk, SC * u + i, 2 * r:2 * r + 2, :].rearrange(
                                                            "p j s -> p (j s)"),
                                                        QP[rows32, wq, at], start=(wk == wq == 0), stop=(wk == 1))
                    done(key, last)

            def chunk_states(u):
                pe.wait_ge(sem("kd_ready"), u // SB + 1)
                pe.wait_ge(sem("v_ready"), u // SB + 1)
                for half in range(2):
                    key = ("kv", u, half)
                    room(pe, key)
                    here = slice(CS * half, CS * half + CS)
                    for k, c in enumerate(states(u, half)):
                        last = nc.tensor.matmul(bank(key)[:, k * D:(k + 1) * D], KD[here, c // 2, :],
                                                V[here, c // 2, :], start=True, stop=True)
                    done(key, last)

            def retained(c):
                b, u, i = c // TC, c // SC, c % SC
                if c % TC == 0 and b >= 2:
                    pe.wait_ge(sem("yn_ready"), b - 1)
                y = ybank[b % 2][:, (c % TC) * CS:(c % TC + 1) * CS]
                if c % TC:
                    pe.wait_ge(sem("state_ready"), state_number(c - 1) + 1)
                    nc.tensor.matmul(y, SM[:, (c - 1) % 4, :], QD[:, c * CS:(c + 1) * CS], start=True, stop=False)
                pe.wait_ge(sem("vz_ready"), 8 * (u + 1))
                for r in range(NPAIR):
                    g = r // 2
                    if i == 0 and r % 2 == 0:
                        pe.wait_ge(sem("plo_ready"), HG * u + g + 1)
                    for wv, wp in PARTS:
                        at = (2 * i + r % 2) * CS
                        last = nc.tensor.matmul(y, VS[:, u % 2, i, wv, r, :],
                                                PP[:, wp, HG * (u % 2) + g, at:at + CS],
                                                start=(c % TC == 0 and r == wv == wp == 0),
                                                stop=(r == NPAIR - 1 and wv == 1))
                last.then_inc(sem("av_done"), 1)

            def group_mean(b):
                key = ("gn", b)
                room(pe, key)
                pe.wait_ge(sem("gn_part"), b + 1)
                done(key, nc.tensor.matmul(bank(key)[:, 0:2], const("headmean"), gs[:, b, 0:2],
                                           start=True, stop=True))

            def retention_out(b):
                key = ("o", b)
                room(pe, key)
                pe.wait_ge(sem("yg_ready"), b + 1)
                for t in range(TB):
                    last = nc.tensor.matmul(bank(key)[:, t * D:(t + 1) * D],
                                            YG[:, b % 2, t * P:(t + 1) * P], wa("o"), start=True, stop=True)
                done(key, last)

            def h2_to_T(b):
                pe.wait_ge(sem("h2_ready"), b + 1)
                transposes(("h2T", b), lambda t: H2[:, TB * b + t, :])

            for u in range(NS + 1):
                if u < NS:
                    scores(u)
                    chunk_states(u)
                if u >= 1:
                    for c in range(SC * (u - 1), SC * u):
                        retained(c)
                if u == GATES_AT:
                    for b in range(NB):
                        key = ("g", b)
                        room(pe, key)
                        done(key, nc.tensor.matmul(bank(key)[:], wa("g"), HT[:, toks(b)], start=True, stop=True))
                if u == CONTEXT_AT:
                    pe.wait_ge(sem("in_w2"), 16)
                    room(pe, ("ck",))
                    done(("ck",), nc.tensor.matmul(bank(("ck",))[:, 0:NB * KC], wb("xk"), wb("ctx"),
                                                   start=True, stop=True))
                    for b in range(NB):
                        key = ("cv", b)
                        room(pe, key)
                        done(key, nc.tensor.matmul(bank(key)[:, 0:D], wb("ctxrep", b * P, P), wb("xv"),
                                                   start=True, stop=True))
                if u in GN_AT:
                    group_mean(GN_AT[u])
                if u in OUT_AT:
                    retention_out(OUT_AT[u])
                if u in H2T_AT:
                    h2_to_T(H2T_AT[u])

            def gates_up(b):
                pe.wait_ge(sem("h2lo_ready"), b + 1)
                pe.wait_ge(sem("gulo_ready"), 1)
                for m in range(3):
                    for name, at in (("ga", 128 * m), ("up", INNER + 128 * m)):
                        key = (name, b, m)
                        room(pe, key)
                        for ww, wh in PARTS:
                            last = nc.tensor.matmul(bank(key)[0:MB[m], :], GU[:, ww, at:at + MB[m]], H2P[:, b, wh, :],
                                                    start=(ww == wh == 0), stop=(ww == 1))
                        done(key, last)

            def down(b):
                key = ("dn", b)
                room(pe, key)
                pe.wait_ge(sem("a_ready"), 3 * (b + 1))
                for t in range(TB):
                    for m in range(3):
                        last = nc.tensor.matmul(bank(key)[:, t * D:(t + 1) * D],
                                                A[0:MB[m], 3 * (b % 2) + m, t * P:(t + 1) * P],
                                                wb("down", 128 * m, 128)[0:MB[m], :],
                                                start=(m == 0), stop=(m == 2))
                done(key, last)

            def x2_to_T(b):
                pe.wait_ge(sem("x2_ready"), b + 1)
                transposes(("x2T", b), lambda t: X2[:, TB * b + t, :])

            def cross_q(b):
                key = ("xq", b)
                room(pe, key)
                pe.wait_ge(sem("x2T_ready"), b + 1)
                done(key, nc.tensor.matmul(bank(key)[:], wb("xq"), HT[:, toks(b)], start=True, stop=True))

            group_mean(3)
            retention_out(2)
            h2_to_T(1)
            gates_up(0)
            retention_out(3)
            h2_to_T(2)
            gates_up(1)
            down(0)
            h2_to_T(3)
            gates_up(2)
            down(1)
            x2_to_T(0)
            gates_up(3)
            cross_q(0)
            down(2)
            x2_to_T(1)
            down(3)
            cross_q(1)

            pe.wait_ge(sem("kx_ready"), NB)
            pe.wait_ge(sem("vx_ready"), 1)
            for s in range(CROSS_STEPS):
                if s < NT:
                    key = ("xs", s)
                    pe.wait_ge(sem("xq_ready"), s // TB + 1)
                    room(pe, key)
                    done(key, nc.tensor.matmul(bank(key)[:], QT[:, s * P:(s + 1) * P], KX[:, s // TB, :],
                                               start=True, stop=True))
                if s in X2T_AT:
                    x2_to_T(X2T_AT[s])
                if s in XQ_AT:
                    cross_q(XQ_AT[s])
                if 2 <= s < NT + 2:
                    pe.wait_ge(sem("xp_ready"), s - 1)
                    transposes(("pT", s - 2), lambda t: SD[:, (s - 2) % 4, t * P:(t + 1) * P])
                if 4 <= s < NT + 4:
                    key = ("pv", s - 4)
                    room(pe, key)
                    pe.wait_ge(sem("pT_ready"), s - 3)
                    for g in range(HG):
                        last = nc.tensor.matmul(bank(key)[:, g * PV:(g + 1) * PV],
                                                PT[:, (s - 4) % 4, g * P:(g + 1) * P],
                                                VX[:, (s - 4) // TB, g, :], start=True, stop=True)
                    done(key, last)
                if s in OT_AT:
                    k = OT_AT[s]
                    pe.wait_ge(sem("att_ready"), sum(UNITS[k]))
                    transposes(("oT", k), lambda t: ATT[:, UNITS[k][0] + t, :], UNITS[k][1])
                if s in XO_AT:
                    k = XO_AT[s]
                    key = ("xo", k)
                    room(pe, key)
                    pe.wait_ge(sem("oT_ready"), k + 1)
                    for n in range(UNITS[k][1]):
                        t = UNITS[k][0] + n
                        last = nc.tensor.matmul(bank(key)[:, n * D:(n + 1) * D], OT[:, t * P:(t + 1) * P],
                                                wb("xo"), start=True, stop=True)
                    done(key, last)
                if s in X3T_AT:
                    k = X3T_AT[s]
                    x3_made(pe, k)
                    transposes(("x3T", k), lambda t: X3[:, UNITS[k][0] + t, :], UNITS[k][1])
                if s in RT_AT:
                    k = RT_AT[s]
                    key = ("rt", k)
                    room(pe, key)
                    pe.wait_ge(sem("x3T_ready"), k + 1)
                    for n in range(UNITS[k][1]):
                        t = UNITS[k][0] + n
                        last = nc.tensor.matmul(bank(key)[:, n * NE:(n + 1) * NE], HT[:, t * P:(t + 1) * P],
                                                wb("router"), start=True, stop=True)
                    done(key, last)
            for r in range(ROUNDS):
                key = ("cnt", r)
                room(pe, key)
                for t in range(NT):
                    if t in (0, NT_FIRST):
                        pe.wait_ge(sem("above_ready"), 2 * r + (t > 0) + 1)
                    last = nc.tensor.matmul(bank(key)[:, 0:NC * NE], onesb[:], above[:, :, :, t].rearrange(
                        "p c e -> p (c e)"), start=(t == 0), stop=(t == NT - 1))
                done(key, last)

            def ranks(key, marks, extra):
                if extra is not None:
                    nc.tensor.matmul(bank(key)[:, 0:P], onesb[:], extra, start=True, stop=False)
                nc.tensor.matmul(bank(key)[:, 0:P], onesb[:], running.rearrange("p e t -> p (e t)"),
                                 start=(extra is None), stop=False)
                done(key, nc.tensor.matmul(bank(key)[:, 0:P], laterb, marks.rearrange("p e t -> p (e t)"),
                                           start=False, stop=True))

            room(pe, ("eq",))
            pe.wait_ge(sem("eq_ready"), 1)
            ranks(("eq",), eq_th, gt_sum.unsqueeze(2).to_broadcast([P, NE, NT]))
            room(pe, ("sel",))
            pe.wait_ge(sem("run_ready"), 1)
            ranks(("sel",), sel, None)
            def slot_lists(e):
                key = ("idx", e)
                room(pe, key)
                pe.wait_ge(sem("onehot_ready"), e + 1)
                o = bank(key)[0:SLOT_A, 0:SLOT_B]
                for t in range(NT):
                    n = e * NT + t
                    nc.tensor.matmul(o, OA[:, n, :], OHI[:, n, :], start=(t == 0), stop=False)
                    last = nc.tensor.matmul(o, OA[:, n, :], OLO[:, n, :], start=False, stop=(t == NT - 1))
                done(key, last)

            def expert_rows_to_T(e):
                for c in range(3):
                    key = ("xeT", e, c)
                    room(pe, key)
                    pe.wait_ge(sem(f"gathered{e % XS}"), 16 * 3 * (e // XS + 1))
                    done(key, nc.tensor.transpose(bank(key)[:, 0:CH[c]], XE[0:CH[c], e % XS, c, 0:D],
                                                  const("ident")[0:CH[c], 0:CH[c]]))

            def expert_hidden(e):
                pe.wait_ge(sem("xeT_ready"), 3 * e + 3)
                for f in range(FB):
                    key = ("h1", e, f)
                    room(pe, key)
                    done(key, nc.tensor.matmul(bank(key)[:, 0:CAP], EW1[:, e, f * P:(f + 1) * P], XET[:, e % 2, :],
                                               start=True, stop=True))

            def expert_out(e, c):
                key = ("y", e, c)
                room(pe, key)
                pe.wait_ge(sem("h1_ready"), FB * (e + 1))
                o = bank(key)[0:CH[c], 0:D]
                for f in range(FB):
                    nc.tensor.matmul(o, H1A[e % 2][:, f, c * P:c * P + CH[c]], EW2[:, e, f, :],
                                     start=(f == 0), stop=False)
                done(key, nc.tensor.matmul(o, const("ones", 0, CH[c])[0:1, :], vec("b2", e * D, D)[0:1, :],
                                           start=False, stop=True))

            for e in range(4):
                slot_lists(e)
            expert_rows_to_T(0)
            slot_lists(4)
            pe.wait_ge(sem("in_ew"), 32)
            pe.wait_ge(sem("in_vec2"), 16)
            expert_hidden(0)
            expert_rows_to_T(1)
            for e in range(NE):
                if e + 1 < NE:
                    expert_hidden(e + 1)
                expert_out(e, 0)
                if e + 2 < NE:
                    expert_rows_to_T(e + 2)
                expert_out(e, 1)
                expert_out(e, 2)
                if e + 5 < NE:
                    slot_lists(e + 5)

        @block.scalar
        def _(act):
            chain = [0]

            def link(ins):
                chain[0] += 1
                ins.then_inc(sem("act_step"), 1)
                act.wait_ge(sem("act_step"), chain[0])

            def inv_sqrt(dst, tmp, src, name, scale, eps):
                link(nc.scalar.activation(tmp, src, ACT.Ln, bias=const(eps), scale=scale))
                nc.scalar.activation(dst, tmp, ACT.Exp, scale=-0.5).then_inc(sem(name), 1)

            act.preload_act_table_set("natural_log_exp_and_others")
            act.wait_ge(sem("in_const"), 16)
            act.wait_ge(sem("in_vec"), 16)

            def rms_rstd(b):
                act.wait_ge(sem("rms_sum"), b + 1)
                inv_sqrt(rstd[:, tiles(b)], lnv[:, tiles(b)], mv[:, tiles(b), 0], "rms_rstd", 1.0 / D, "eps6")

            def h_T(b):
                filled(act, ("hT", b))
                nc.scalar.activation(HT[:, toks(b)], bank(("hT", b))[:], ACT.Copy,
                                     scale=vec("ln1")).then_inc(sem("hT_ready"), 1)

            rms_rstd(0)
            rms_rstd(1)
            nc.scalar.activation(e_row, vec("gamma_row"), ACT.Exp, scale=-1.0).then_inc(sem("e_ready"), 1)
            nc.scalar.activation(e_pair, vec("gamma_pair"), ACT.Exp, scale=-1.0).then_inc(sem("e_ready"), 1)
            nc.scalar.activation(e_col, vec("gamma_col"), ACT.Exp, scale=-1.0).then_inc(sem("e_ready"), 1)
            act.wait_ge(sem("e1_ready"), 3)
            link(nc.scalar.activation(lg_pair, e_pair, ACT.Ln))
            link(nc.scalar.activation(lg_row, e_row, ACT.Ln))
            link(nc.scalar.activation(lg_col, e_col, ACT.Ln))
            h_T(0)
            h_T(1)
            link(nc.scalar.mul(small[:, 144:145], lg_col, -1.0))
            nc.scalar.activation(g64, lg_col, ACT.Exp, scale=-float(CS)).then_inc(sem("g64_ready"), 1)
            nc.scalar.activation(DQ[:], const("after"), ACT.Exp, scale=small[:, 144:145]).then_inc(sem("dq_ready"), 1)
            link(nc.scalar.mul(small[:, 145:146], const("left"), -1.0))
            nc.scalar.activation(DK[:].rearrange("p (h d) -> p h d", h=H),
                                 lg_row.unsqueeze(2).to_broadcast([P, H, DH]), ACT.Exp,
                                 scale=small[:, 145:146]).then_inc(sem("dk_ready"), 1)
            act.wait_ge(sem("logmask_ready"), 1)
            nc.scalar.activation(M[:, 0:512], M[:, 0:512], ACT.Exp, scale=-1.0).then_inc(sem("mask_exp"), 1)

            rms_rstd(2)
            rms_rstd(3)
            for b in range(NB):
                filled(act, ("q", b))
                nc.scalar.copy(QP[:, 0, toks(b)], bank(("q", b))[:]).then_inc(sem("q_ready"), 1)
                filled(act, ("k", b))
                if b >= 2:
                    act.wait_ge(sem("kexp_ready"), b - 1)
                    act.wait_ge(sem("kexp_act"), b - 1)
                nc.scalar.copy(KP[:, b % 2, 0, :], bank(("k", b))[:]).then_inc(sem("k_ready"), 1)
                if b + 2 < NB:
                    h_T(b + 2)
                filled(act, ("v", b))
                nc.scalar.copy(VP[:, 0, tiles(b), :], by_tile(bank(("v", b))[:])).then_inc(sem("vhi_ready"), 1)
                nc.scalar.copy(V[:, tiles(b), :], by_tile(bank(("v", b))[:])).then_inc(sem("v_ready"), 1)
                act.wait_ge(sem("k_ready"), b + 1)
                act.wait_ge(sem("klo_ready"), b + 1)
                for w in range(2):
                    last = nc.scalar.activation(KE[:, w, TC * b:TC * b + TC, HJ - 1, :],
                                                KP[:, b % 2, w, :].rearrange("p (c s) -> p c s", s=CS), ACT.Copy,
                                                scale=const("quad", HJ - 1, 1))
                last.then_inc(sem("kexp_act"), 1)
            def group_rstd(b):
                act.wait_ge(sem("gn_var"), b + 1)
                inv_sqrt(gs[:, b, 5:6], gs[:, b, 4:5], gs[:, b, 3:4], "gn_rstd", -1.0, "eps5")

            def group_apply(b):
                act.wait_ge(sem("gn_affine"), b + 1)
                if b >= 2:
                    act.wait_ge(sem("yg_ready"), b - 1)
                nc.scalar.activation(YN[:, b % 2, :], ybank[b % 2][:], ACT.Identity, bias=gs[:, b, 7:8],
                                     scale=gs[:, b, 6:7]).then_inc(sem("yn_ready"), 1)

            def rms2_rstd(b):
                act.wait_ge(sem("rms2_sum"), b + 1)
                inv_sqrt(rstd[:, tiles(b)], lnv[:, tiles(b)], mv[:, tiles(b), 0], "rms2_rstd", 1.0 / D, "eps6")

            def h2_T(b):
                filled(act, ("h2T", b))
                nc.scalar.activation(H2P[:, b, 0, :], bank(("h2T", b))[:], ACT.Copy,
                                     scale=vec("ln2")).then_inc(sem("h2T_ready"), 1)

            def silu(b):
                for m in range(3):
                    n = 3 * b + m
                    filled(act, ("ga", b, m))
                    if n >= 2:
                        act.wait_ge(sem("a_ready"), n - 1)
                    nc.scalar.activation(SG[0:MB[m], n % 2, :], bank(("ga", b, m))[0:MB[m], :],
                                         ACT.Silu).then_inc(sem("silu_ready"), 1)

            def ln_rstd(b, which, at=None):
                at = at or tiles(b)
                act.wait_ge(sem(f"{which}_stats"), b + 1)
                inv_sqrt(rstd[:, at], lnv[:, at], mv[:, at, 1], f"{which}_rstd", 1.0, "eps5")

            def x2_T(b):
                filled(act, ("x2T", b))
                nc.scalar.copy(HT[:, toks(b)], bank(("x2T", b))[:]).then_inc(sem("x2T_ready"), 1)

            def cross_q(b):
                filled(act, ("xq", b))
                nc.scalar.copy(QT[:, toks(b)], bank(("xq", b))[:]).then_inc(sem("xq_ready"), 1)

            for u in range(NS + 1):
                if u in H2_AT:
                    rms2_rstd(H2_AT[u])
                for g in range(HG) if u < NS else []:
                    n = HG * u + g
                    act.wait_ge(sem("p_ready"), n + 1)
                    if u >= 2:
                        act.wait_ge(sem("av_done"), SC * (u - 1))
                    nc.scalar.copy(PP[:, 0, n % 8, :], P32[:, n % 3, :]).then_inc(sem("phi_ready"), 1)
                if u == GATES_AT:
                    act.wait_ge(sem("in_w2"), 16)
                    nc.scalar.copy(GU[:, 0, :], W2[:, 0:2 * INNER]).then_inc(sem("guhi_ready"), 1)
                    for b in range(NB):
                        filled(act, ("g", b))
                        nc.scalar.activation(GT[:, toks(b)], bank(("g", b))[:], ACT.Sigmoid).then_inc(
                            sem("g_ready"), 1)
                    act.preload_act_table_set("natural_log_exp_and_others")
                if u in GN_AT:
                    group_rstd(GN_AT[u])
                if u in YG_AT:
                    group_apply(YG_AT[u])
                if u in H2T_AT:
                    h2_T(H2T_AT[u])
            group_rstd(3)
            h2_T(1)
            group_apply(3)
            rms2_rstd(2)
            act.wait_ge(sem("plo_ready"), HG * NS)
            silu(0)
            h2_T(2)
            act.preload_act_table_set("natural_log_exp_and_others")
            rms2_rstd(3)
            silu(1)
            h2_T(3)
            silu(2)
            act.preload_act_table_set("natural_log_exp_and_others")
            ln_rstd(0, "ln1")
            x2_T(0)
            silu(3)
            act.preload_act_table_set("natural_log_exp_and_others")
            ln_rstd(1, "ln1")
            cross_q(0)
            x2_T(1)
            ln_rstd(2, "ln1")
            cross_q(1)
            for s in range(CROSS_STEPS):
                if s < NT:
                    act.wait_ge(sem("sd_ready"), s + 1)
                    nc.scalar.activation(SD[:, s % 4, :], SD[:, s % 4, :], ACT.Exp, scale=SCALE).then_inc(
                        sem("xp_ready"), 1)
                if s in X2_AT:
                    ln_rstd(X2_AT[s], "ln1")
                if s in X2T_AT:
                    x2_T(X2T_AT[s])
                if s in XQ_AT:
                    cross_q(XQ_AT[s])
                if 2 <= s < NT + 2:
                    filled(act, ("pT", s - 2))
                    if s - 2 >= 4:
                        filled(act, ("pv", s - 6))
                    nc.scalar.copy(PT[:, (s - 2) % 4, :], bank(("pT", s - 2))[:]).then_inc(sem("pT_ready"), 1)
                if s in OT_AT:
                    k = OT_AT[s]
                    filled(act, ("oT", k))
                    nc.scalar.copy(OT[:, P * UNITS[k][0]:P * sum(UNITS[k])],
                                   bank(("oT", k))[:, 0:P * UNITS[k][1]]).then_inc(sem("oT_ready"), 1)
                if s in X3_AT:
                    ln_rstd(X3_AT[s], "ln2", unit(X3_AT[s]))
                if s in X3T_AT:
                    k = X3T_AT[s]
                    filled(act, ("x3T", k))
                    nc.scalar.copy(HT[:, P * UNITS[k][0]:P * sum(UNITS[k])],
                                   bank(("x3T", k))[:, 0:P * UNITS[k][1]]).then_inc(sem("x3T_ready"), 1)
            act.wait_ge(sem("top_ready"), 1)
            nc.scalar.activation(top[:, 2, :], top[:, 2, :], ACT.Exp).then_inc(sem("top_exp"), 1)
            act.preload_act_table_set("gelu_and_others")
            act.wait_ge(sem("in_vec2"), 16)
            for e in range(NE):
                for f in range(FB):
                    filled(act, ("h1", e, f))
                    if e >= 2:
                        filled(act, ("y", e - 2, 2))
                    nc.scalar.activation(H1A[e % 2][:, f, :], bank(("h1", e, f))[:, 0:CAP], ACT.Gelu,
                                         bias=vec("b1", e * FB + f, 1)).then_inc(sem("h1_ready"), 1)
            act.preload_act_table_set("natural_log_exp_and_others")

            def apply(b, dst, which, name):
                act.wait_ge(sem(f"{which}_shift"), b + 1)
                for t in range(TB * b, TB * b + TB):
                    last = nc.scalar.activation(dst[:, t, :], AM[:, t, :], ACT.Identity, bias=lnv[:, t:t + 1],
                                                scale=rstd[:, t:t + 1])
                last.then_inc(sem(name), 1)

            for b in range(NB):
                ln_rstd(b, "ln3")
                if b in ACT_BATCHES:
                    apply(b, AM, "ln3", "ln3_applied")
            for b in range(NB - 1):
                ln_rstd(b, "ln4")
                if b == NB - 2:
                    ln_rstd(NB - 1, "ln4")
                apply(b, FIN, "ln4", "fin_ready")

        @block.vector
        def _(dve):
            chain = [0]

            def link(ins):
                chain[0] += 1
                ins.then_inc(sem("dve_step"), 1)
                dve.wait_ge(sem("dve_step"), chain[0])

            tt, ts, stt = nc.vector.tensor_tensor, nc.vector.tensor_scalar, nc.vector.scalar_tensor_tensor

            def sum_squares(b, src, squares, name):
                link(tt(squares[:, tiles(b), :], src[:, tiles(b), :], src[:, tiles(b), :], ALU.mult))
                nc.vector.tensor_reduce(mv[:, tiles(b), 0], squares[:, tiles(b), :], AX, ALU.add).then_inc(
                    sem(name), 1)

            def rms_sum(b):
                dve.wait_ge(sem(f"in_x{b}"), 16)
                sum_squares(b, X, Hb, "rms_sum")

            def rms_apply(b):
                dve.wait_ge(sem("rms_rstd"), b + 1)
                tt(Hb[:, tiles(b), :], X[:, tiles(b), :], rstd[:, tiles(b)].unsqueeze(2).to_broadcast([P, TB, D]),
                   ALU.mult).then_inc(sem("h_ready"), 1)

            rms_sum(0)
            rms_sum(1)
            rms_apply(0)
            rms_apply(1)
            dve.wait_ge(sem("e_ready"), 3)
            link(ts(e_pair, e_pair, 1e19, None, ALU.min))
            ts(e_pair, e_pair, 1.0, None, ALU.add).then_inc(sem("e1_ready"), 1)
            link(ts(e_row, e_row, 1e19, None, ALU.min))
            ts(e_row, e_row, 1.0, None, ALU.add).then_inc(sem("e1_ready"), 1)
            link(ts(e_col, e_col, 1e19, None, ALU.min))
            ts(e_col, e_col, 1.0, None, ALU.add).then_inc(sem("e1_ready"), 1)
            dve.wait_ge(sem("g64_ready"), 1)
            mask = M[:, 0:512].rearrange("p (r t) -> p r t", r=NPAIR)
            tt(mask, const("dist").unsqueeze(1).to_broadcast([P, NPAIR, CS]),
               lg_pair.unsqueeze(2).to_broadcast([P, NPAIR, CS]), ALU.mult).then_inc(sem("logmask_ready"), 1)

            rms_sum(2)
            rms_sum(3)
            rms_apply(2)
            rms_apply(3)
            dve.wait_ge(sem("mask_exp"), 1)
            tt(mask, mask, const("causal").unsqueeze(1).to_broadcast([P, NPAIR, CS]), ALU.mult).then_inc(
                sem("mask_ready"), 1)
            for b in range(NB):
                filled(dve, ("q", b))
                dve.wait_ge(sem("q_ready"), b + 1)
                tt(QP[:, 1, toks(b)], bank(("q", b))[:], QP[:, 0, toks(b)], ALU.subtract).then_inc(sem("qlo_ready"), 1)
                dve.wait_ge(sem("dq_ready"), 1)
                tt(QD[:, toks(b)].rearrange("p (c t) -> p c t", t=CS),
                   bank(("q", b))[:].rearrange("p (c t) -> p c t", t=CS),
                   DQ[:].unsqueeze(1).to_broadcast([P, TC, CS]), ALU.mult).then_inc(sem("qd_ready"), 1)
                dve.wait_ge(sem("k_ready"), b + 1)
                if b >= 2:
                    dve.wait_ge(sem("kexp_ready"), b - 1)
                    dve.wait_ge(sem("kexp_act"), b - 1)
                tt(KP[:, b % 2, 1, :], bank(("k", b))[:], KP[:, b % 2, 0, :], ALU.subtract).then_inc(
                    sem("klo_ready"), 1)
                filled(dve, ("kt", b))
                dve.wait_ge(sem("dk_ready"), 1)
                tt(KD[:, tiles(b), :], by_tile(bank(("kt", b))[:]), DK[:].unsqueeze(1).to_broadcast([P, TB, D]),
                   ALU.mult).then_inc(sem("kd_ready"), 1)
                dve.wait_ge(sem("klo_ready"), b + 1)
                for w in range(2):
                    for j in range(HJ - 1):
                        last = ts(KE[:, w, TC * b:TC * b + TC, j, :],
                                  KP[:, b % 2, w, :].rearrange("p (c s) -> p c s", s=CS), const("quad", j, 1), None, ALU.mult)
                last.then_inc(sem("kexp_ready"), 1)

            dve.wait_ge(sem("mask_ready"), 1)

            def score_rest(n):
                dve.wait_ge(sem("phi_ready"), n + 1)
                tt(PP[:, 1, n % 8, :], P32[:, n % 3, :], PP[:, 0, n % 8, :], ALU.subtract).then_inc(
                    sem("plo_ready"), 1)

            def group_stats(b):
                dve.wait_ge(sem("av_done"), TC * (b + 1))
                link(nc.vector.bn_stats(stats[:, b, :], ybank[b % 2][:]))
                link(nc.vector.bn_aggr(gs[:, b, 0:2], stats[:, b, :]))
                stt(gs[:, b, 1:2], gs[:, b, 0:1], gs[:, b, 0:1], gs[:, b, 1:2], ALU.mult, ALU.add).then_inc(
                    sem("gn_part"), 1)

            def group_var(b):
                filled(dve, ("gn", b))
                link(nc.vector.tensor_copy(gs[:, b, 2:4], bank(("gn", b))[:, 0:2]))
                stt(gs[:, b, 3:4], gs[:, b, 2:3], gs[:, b, 2:3], gs[:, b, 3:4], ALU.mult,
                    ALU.subtract).then_inc(sem("gn_var"), 1)

            def group_affine(b):
                dve.wait_ge(sem("gn_rstd"), b + 1)
                link(tt(gs[:, b, 6:7], gs[:, b, 5:6], vec("gnw"), ALU.mult))
                link(stt(gs[:, b, 7:8], gs[:, b, 2:3], gs[:, b, 6:7], vec("gnb"), ALU.mult, ALU.subtract))
                ts(gs[:, b, 7:8], gs[:, b, 7:8], -1.0, None, ALU.mult).then_inc(sem("gn_affine"), 1)

            def gate_y(b):
                dve.wait_ge(sem("yn_ready"), b + 1)
                dve.wait_ge(sem("g_ready"), b + 1)
                if b >= 2:
                    filled(dve, ("o", b - 2))
                tt(YG[:, b % 2, :], YN[:, b % 2, :], GT[:, toks(b)], ALU.mult).then_inc(sem("yg_ready"), 1)

            def x1_out(b):
                filled(dve, ("o", b))
                tt(X1[:, tiles(b), :], by_tile(bank(("o", b))[:]), X[:, tiles(b), :], ALU.add).then_inc(
                    sem("x1_ready"), 1)

            def rms2_sum(b):
                dve.wait_ge(sem("x1_ready"), b + 1)
                filled(dve, ("kv", SB * (b + 1) - 1, 1))
                sum_squares(b, X1, H2, "rms2_sum")

            def rms2_apply(b):
                dve.wait_ge(sem("rms2_rstd"), b + 1)
                tt(H2[:, tiles(b), :], X1[:, tiles(b), :], rstd[:, tiles(b)].unsqueeze(2).to_broadcast([P, TB, D]),
                   ALU.mult).then_inc(sem("h2_ready"), 1)

            def h2_rest(b):
                filled(dve, ("h2T", b))
                dve.wait_ge(sem("h2T_ready"), b + 1)
                stt(H2P[:, b, 1, :], bank(("h2T", b))[:], vec("ln2"), H2P[:, b, 0, :], ALU.mult,
                    ALU.subtract).then_inc(sem("h2lo_ready"), 1)

            for u in range(NS + 1):
                if u - 1 in H2T_AT:
                    h2_rest(H2T_AT[u - 1])
                if u in GN_AT:
                    group_stats(GN_AT[u])
                if u in YG_AT:
                    group_affine(YG_AT[u])
                if u in H2_AT:
                    rms2_sum(H2_AT[u])
                if u < NS:
                    for g in range(HG):
                        n = HG * u + g
                        filled(dve, ("s", u, g))
                        if n >= 3:
                            dve.wait_ge(sem("plo_ready"), n - 2)
                        tt(P32[:, n % 3, :].rearrange("p (i c) -> p i c", i=SC),
                           bank(("s", u, g))[:].rearrange("p (i c) -> p i c", i=SC),
                           M[:, g * P:(g + 1) * P].unsqueeze(1).to_broadcast([P, SC, P]), ALU.mult).then_inc(
                               sem("p_ready"), 1)
                        if n:
                            score_rest(n - 1)
                    if u == NS - 1:
                        score_rest(HG * NS - 1)
                    for c in range(SC * u, SC * u + SC):
                        if c % TC == TC - 1:
                            continue
                        n = state_number(c)
                        half = c % 2
                        filled(dve, ("kv", u, half))
                        if n >= 4:
                            dve.wait_ge(sem("state_ready"), n - 3)
                        k = states(u, half).index(c)
                        kv = bank(("kv", u, half))[:, k * D:(k + 1) * D]
                        if c % TC == 0:
                            nc.vector.tensor_copy(SR[:, n % 4, :], kv).then_inc(sem("raw_ready"), 1)
                        else:
                            dve.wait_ge(sem("raw_ready"), n)
                            stt(SR[:, n % 4, :], SR[:, (n - 1) % 4, :], g64, kv, ALU.mult, ALU.add).then_inc(
                                sem("raw_ready"), 1)
                if u == CONTEXT_AT:
                    filled(dve, ("ck",))
                    nc.vector.tensor_copy(CK[:], bank(("ck",))[:, 0:NB * KC]).then_inc(sem("ck_ready"), 1)
                    for b in range(NB):
                        filled(dve, ("cv", b))
                        tt(VX[:, b, :, 0:32].rearrange("p g (j e) -> p g j e", j=HJ),
                           bank(("cv", b))[:, 0:D].rearrange("p (g j e) -> p g j e", g=HG, j=HJ),
                           const("keyhead").unsqueeze(1).unsqueeze(3).to_broadcast([P, HG, HJ, DH]), ALU.mult).then_inc(
                               sem("cv_ready"), 1)
                    nc.vector.tensor_copy(VX[:, :, :, 32:PV].rearrange("p b g j -> p (b g) j"),
                                          const("keyhead").unsqueeze(1).to_broadcast([P, NB * HG, HJ])).then_inc(
                                              sem("vx_ready"), 1)
                if u in GN_AT:
                    group_var(GN_AT[u])
                if u in YG_AT:
                    gate_y(YG_AT[u])
                if u in OUT_AT:
                    x1_out(OUT_AT[u])
                if u in H2_AT:
                    rms2_apply(H2_AT[u])

            def layer_stats(b, src, which, at=None):
                at = at or tiles(b)
                for t in range(at.start, at.stop):
                    last = nc.vector.bn_stats(stats[:, t, :], src[:, t, :])
                link(last)
                for t in range(at.start, at.stop):
                    last = nc.vector.bn_aggr(mv[:, t, :], stats[:, t, :])
                last.then_inc(sem(f"{which}_stats"), 1)

            def layer_apply(b, dst, src, which, at=None):
                at = at or tiles(b)
                dve.wait_ge(sem(f"{which}_rstd"), b + 1)
                dve.wait_ge(sem(f"{which}_stats"), b + 1)
                for t in range(at.start, at.stop):
                    last = ts(dst[:, t, :], src[:, t, :], mv[:, t, 0:1], rstd[:, t:t + 1], ALU.subtract, ALU.mult)
                return last

            def mlp_out(b):
                filled(dve, ("dn", b))
                dve.wait_ge(sem("xx_ready"), b + 1)
                tt(R[:, tiles(b), :], by_tile(bank(("dn", b))[:]), X[:, tiles(b), :], ALU.add).then_inc(
                    sem("r_ready"), 1)
                dve.wait_ge(sem("r_ready"), b + 1)
                layer_stats(b, R, "ln1")

            def mlp_act(b):
                for m in range(3):
                    n = 3 * b + m
                    filled(dve, ("up", b, m))
                    dve.wait_ge(sem("silu_ready"), n + 1)
                    if b >= 2:
                        filled(dve, ("dn", b - 2))
                    tt(A[0:MB[m], 3 * (b % 2) + m, :], bank(("up", b, m))[0:MB[m], :], SG[0:MB[m], n % 2, :],
                       ALU.mult).then_inc(sem("a_ready"), 1)

            def x2_out(b):
                layer_apply(b, X2, R, "ln1").then_inc(sem("x2_ready"), 1)

            group_stats(3)
            x1_out(2)
            group_var(3)
            rms2_sum(2)
            group_affine(3)
            h2_rest(1)
            rms2_apply(2)
            gate_y(3)
            mlp_act(0)
            x1_out(3)
            h2_rest(2)
            rms2_sum(3)
            rms2_apply(3)
            mlp_act(1)
            mlp_out(0)
            h2_rest(3)
            mlp_act(2)
            x2_out(0)
            mlp_out(1)
            mlp_act(3)
            x2_out(1)
            mlp_out(2)
            x2_out(2)
            mlp_out(3)

            nc.vector.tensor_copy(onesb[:], const("ones")).then_inc(sem("table_ready"), 1)
            nc.vector.tensor_copy(laterb, const("later")).then_inc(sem("table_ready"), 1)
            nc.vector.tensor_copy(segb, const("same_tile")).then_inc(sem("table_ready"), 1)
            for s in range(CROSS_STEPS):
                if s < NT:
                    filled(dve, ("xs", s))
                    sc = bank(("xs", s))[:].rearrange("p (h k) -> p h k", h=H)
                    nc.vector.tensor_reduce(xmax[:, s % 2, :], sc, AX, ALU.max).then_inc(sem("max_ready"), 1)
                if 4 <= s < NT + 4:
                    n = s - 4
                    filled(dve, ("pv", n))
                    pv = bank(("pv", n))[:, 0:HG * PV].rearrange("p (g c) -> p g c", g=HG)
                    den = xden[:, n % 2, :].rearrange("p (g j) -> p g j", g=HG)
                    nc.vector.reciprocal(den, pv[:, :, 32:PV]).then_inc(sem("den_ready"), 1)
                if s < NT:
                    if s >= 4:
                        filled(dve, ("pT", s - 4))
                    dve.wait_ge(sem("max_ready"), s + 1)
                    tt(SD[:, s % 4, :].rearrange("p (h k) -> p h k", h=H), sc,
                       xmax[:, s % 2, :].unsqueeze(2).to_broadcast([P, H, KC]), ALU.subtract).then_inc(
                           sem("sd_ready"), 1)
                if 4 <= s < NT + 4:
                    dve.wait_ge(sem("den_ready"), n + 1)
                    tt(ATT[:, n, :].rearrange("p (g j e) -> p g j e", g=HG, j=HJ),
                       pv[:, :, 0:32].rearrange("p g (j e) -> p g j e", j=HJ),
                       den.unsqueeze(3).to_broadcast([P, HG, HJ, DH]), ALU.mult).then_inc(sem("att_ready"), 1)
                if s in X2_AT:
                    x2_out(X2_AT[s])
                if s in XO_AT:
                    k = XO_AT[s]
                    filled(dve, ("xo", k))
                    tt(R[:, unit(k), :], by_tile(bank(("xo", k))[:, 0:D * UNITS[k][1]]), X2[:, unit(k), :],
                       ALU.add).then_inc(sem("r2_ready"), 1)
                    dve.wait_ge(sem("r2_ready"), k + 1)
                    layer_stats(k, R, "ln2", unit(k))
                if X3_AT.get(s, 0) >= NB - 1:
                    k = X3_AT[s]
                    layer_apply(k, X3, R, "ln2", unit(k)).then_inc(sem("x3_last"), 1)
                if s in RT_AT:
                    k = RT_AT[s]
                    filled(dve, ("rt", k))
                    tt(logits[:, unit(k), :],
                       bank(("rt", k))[:, 0:UNITS[k][1] * NE].rearrange("p (t e) -> p t e", e=NE),
                       vec("br").unsqueeze(1).to_broadcast([P, UNITS[k][1], NE]), ALU.add).then_inc(
                           sem("logits_ready"), 1)

            dve.wait_ge(sem("logits_ready"), NU)
            def wide(v):
                return v.unsqueeze(2).to_broadcast([P, NT, NE])

            def flat(v):
                return v.rearrange("p t e -> p (t e)")

            def pick(n, src, dst):
                link(nc.vector.tensor_reduce(top[:, n, :], src, AX, ALU.max))
                link(tt(dst, src, wide(top[:, n, :]), ALU.is_equal))
                link(nc.vector.tensor_tensor_scan(flat(rtmp), const("same_token"), flat(dst), 0.0, ALU.mult, ALU.add))
                link(stt(dst, rtmp, 1.0, dst, ALU.is_le, ALU.mult))

            pick(0, logits, pick1)
            link(stt(logits, pick1, -3e38, logits, ALU.mult, ALU.add))
            link(nc.vector.tensor_reduce(top[:, 1, :], logits, AX, ALU.max))
            tt(top[:, 2, :], top[:, 1, :], top[:, 0, :], ALU.subtract).then_inc(sem("top_ready"), 1)
            link(tt(pick2, logits, wide(top[:, 1, :]), ALU.is_equal))
            link(nc.vector.tensor_tensor_scan(flat(rtmp), const("same_token"), flat(pick2), 0.0, ALU.mult, ALU.add))
            link(stt(pick2, rtmp, 1.0, pick2, ALU.is_le, ALU.mult))
            stt(rtmp, pick1, -1.0, pick2, ALU.add, ALU.add).then_inc(sem("unpicked_ready"), 1)
            dve.wait_ge(sem("top_exp"), 1)
            link(ts(top[:, 4, :], top[:, 2, :], 1.0, None, ALU.add))
            link(nc.vector.reciprocal(top[:, 4, :], top[:, 4, :]))
            tt(top[:, 5, :], top[:, 2, :], top[:, 4, :], ALU.mult).then_inc(sem("gate2_ready"), 1)
            tt(pick1, pick1, wide(top[:, 4, :]), ALU.mult).then_inc(sem("gated_ready"), 1)
            dve.wait_ge(sem("gate2_ready"), 1)
            tt(pick2, pick2, wide(top[:, 5, :]), ALU.mult).then_inc(sem("gated_ready"), 1)
            dve.wait_ge(sem("gated_ready"), 1)
            dve.wait_ge(sem("unpicked_ready"), 1)
            tt(pick1, pick1, rtmp, ALU.add).then_inc(sem("gated_ready"), 1)
            dve.wait_ge(sem("gated_ready"), 3)
            tt(key_et.rearrange("p e t -> p t e"), pick1, pick2, ALU.add).then_inc(sem("gate_ready"), 1)
            tt(key_te, pick1, pick2, ALU.add).then_inc(sem("gates_ready"), 1)

            nc.vector.memset(cand[:, 0, 0, :], 0.0).then_inc(sem("thr_ready"), 1)
            dve.wait_ge(sem("in_bits"), 16)
            dve.wait_ge(sem("gate_ready"), 1)
            dve.wait_ge(sem("table_ready"), 3)
            for r in range(ROUNDS):
                dve.wait_ge(sem("thr_ready"), r + 1)
                tt(thr.bitcast(I32), cand[:, r % 2, 0:1, :].bitcast(I32).to_broadcast([P, NC, NE]),
                   BT[:, NC * r:NC * (r + 1)].unsqueeze(2).to_broadcast([P, NC, NE]), ALU.bitwise_or).then_inc(
                       sem("tries_ready"), 1)
                dve.wait_ge(sem("tries_ready"), r + 1)
                for t in (slice(0, NT_FIRST), slice(NT_FIRST, NT)):
                    shape = [P, NC, NE, t.stop - t.start]
                    tt(above[:, :, :, t], key_et[:, :, t].unsqueeze(1).to_broadcast(shape),
                       thr.unsqueeze(3).to_broadcast(shape), ALU.is_ge).then_inc(sem("above_ready"), 1)
                filled(dve, ("cnt", r))
                link(stt(cand[:, r % 2, 1:NC + 1, :], bank(("cnt", r))[:, 0:NC * NE].rearrange("p (c e) -> p c e", e=NE),
                         float(CAP), thr, ALU.is_ge, ALU.mult))
                nc.vector.tensor_reduce(cand[:, (r + 1) % 2, 0, :], cand[:, r % 2].rearrange("p c e -> p e c"), AX, ALU.max).then_inc(
                    sem("thr_ready"), 1)
            dve.wait_ge(sem("thr_ready"), ROUNDS + 1)
            found = cand[:, ROUNDS % 2, 0, :].unsqueeze(2).to_broadcast([P, NE, NT])
            link(tt(eq_th, key_et, found, ALU.is_equal))
            link(tt(gt_th, key_et, found, ALU.is_gt))
            link(nc.vector.tensor_tensor_scan(running.rearrange("p e t -> p (e t)"), segb,
                                              eq_th.rearrange("p e t -> p (e t)"), 0.0, ALU.mult, ALU.add))
            with nc.allow_low_precision("counts up to the number of tiles"):
                nc.vector.tensor_reduce(gt_sum, gt_th, AX, ALU.add).then_inc(sem("eq_ready"), 1)
            filled(dve, ("eq",))
            link(stt(eq_th, bank(("eq",))[:, 0:P].rearrange("p (e t) -> p e t", e=NE), float(CAP), eq_th,
                     ALU.is_le, ALU.mult))
            tt(sel, gt_th, eq_th, ALU.add).then_inc(sem("sel_ready"), 1)
            dve.wait_ge(sem("sel_ready"), 1)
            nc.vector.tensor_tensor_scan(running.rearrange("p e t -> p (e t)"), segb,
                                         sel.rearrange("p e t -> p (e t)"), 0.0, ALU.mult, ALU.add).then_inc(
                                             sem("run_ready"), 1)
            filled(dve, ("sel",))
            stt(slot.rearrange("p (e t) -> p e t", e=NE), bank(("sel",))[:, 0:P].rearrange("p (e t) -> p e t", e=NE),
                -1.0 - FAR, sel, ALU.add, ALU.mult).then_inc(sem("pos_ready"), 1)
            dve.wait_ge(sem("pos_ready"), 1)
            link(ts(slotI, slot, float(FAR), None, ALU.add))
            link(ts(posA.bitcast(I32), slotI, SLOT_A - 1, None, ALU.bitwise_and))
            link(ts(posB.bitcast(I32), slotI, 5, None, ALU.logical_shift_right))

            def one_hots(e):
                n = slice(NT * e, NT * (e + 1))
                link(tt(OB[:, n, :], const("iota_b").unsqueeze(1).to_broadcast([P, NT, SLOT_B]),
                        posB.bitcast(I32)[:, n].unsqueeze(2).to_broadcast([P, NT, SLOT_B]), ALU.is_equal))
                tt(OA[:, n, :], const("iota_a").unsqueeze(1).to_broadcast([P, NT, SLOT_A]),
                   posA.bitcast(I32)[:, n].unsqueeze(2).to_broadcast([P, NT, SLOT_A]),
                   ALU.is_equal).then_inc(sem("onehot_a"), 1)
                tt(OHI[:, n, :], OB[:, n, :], const("token_hi").unsqueeze(2).to_broadcast([P, NT, SLOT_B]),
                   ALU.mult).then_inc(sem("onehot_hi"), 1)
                ts(OLO[:, n, :], OB[:, n, :], const("token_lo"), None, ALU.mult).then_inc(sem("onehot_ready"), 1)

            def slot_tokens(e):
                filled(dve, ("idx", e))
                lists = bank(("idx", e))[0:SLOT_A, 0:SLOT_B]
                for q in range(4):
                    n = 3 if q < SLOT_B - 8 else 2
                    ts(idx[32 * q:32 * q + 32, e, 0:n], lists[:, q:SLOT_B:4], float(FAR), None,
                       ALU.add).then_inc(sem("idx_ready"), 1)

            def expert_rows(e):
                for c in range(3):
                    filled(dve, ("xeT", e, c))
                    nc.vector.tensor_copy(XET[:, e % 2, c * P:c * P + CH[c]],
                                          bank(("xeT", e, c))[:, 0:CH[c]]).then_inc(sem("xeT_ready"), 1)

            def gated(e, c):
                filled(dve, ("y", e, c))
                if e >= 2 and c == 0:
                    dve.wait_ge(sem("added"), 16 * 3 * (e - 1))
                ts(YE[0:CH[c], 3 * (e % 2) + c, :], bank(("y", e, c))[0:CH[c], 0:D],
                   XE[0:CH[c], e % XS, c, D + e:D + e + 1], None, ALU.mult).then_inc(sem("ye_ready"), 1)

            for e in range(5):
                one_hots(e)
                if e:
                    slot_tokens(e - 1)
            expert_rows(0)
            one_hots(5)
            slot_tokens(4)
            expert_rows(1)
            for e in range(NE):
                gated(e, 0)
                if e + 2 < NE:
                    expert_rows(e + 2)
                gated(e, 1)
                gated(e, 2)
                if e + 6 < NE:
                    one_hots(e + 6)
                if e + 5 < NE:
                    slot_tokens(e + 5)
                if e < NB:
                    tt(X3F[:, tiles(e), :], X3[:, tiles(e), :], vec("fb").unsqueeze(1).to_broadcast([P, TB, D]),
                       ALU.add).then_inc(sem("x3f_ready"), 1)

            def shift(b, which):
                dve.wait_ge(sem(f"{which}_rstd"), b + 1)
                stt(lnv[:, tiles(b)], mv[:, tiles(b), 0], -1.0, rstd[:, tiles(b)], ALU.mult, ALU.mult).then_inc(
                    sem(f"{which}_shift"), 1)

            def stats3(b):
                dve.wait_ge(sem(f"in_sum{b}"), 16)
                layer_stats(b, AM, "ln3")

            def centre3(b):
                dve.wait_ge(sem("ln3_stats"), b + 1)
                for t in range(TB * b, TB * b + TB):
                    last = stt(AM[:, t, :], AM[:, t, :], mv[:, t, 0:1], vec("fg"), ALU.subtract, ALU.mult)
                last.then_inc(sem("ln3_centred"), 1)

            def sum3(b):
                dve.wait_ge(sem("ln3_centred"), b - len(ACT_BATCHES) + 1)
                dve.wait_ge(sem("ln3_rstd"), b + 1)
                dve.wait_ge(sem("x3f_ready"), NB)
                for t in range(TB * b, TB * b + TB):
                    last = stt(AM[:, t, :], AM[:, t, :], rstd[:, t:t + 1], X3F[:, t, :], ALU.mult, ALU.add)
                last.then_inc(sem("sum3_ready"), 1)

            def stats4(b):
                if b in ACT_BATCHES:
                    dve.wait_ge(sem("sum_ready"), b + 1)
                else:
                    dve.wait_ge(sem("sum3_ready"), b - len(ACT_BATCHES) + 1)
                layer_stats(b, AM, "ln4")

            for b in ACT_BATCHES:
                stats3(b)
                shift(b, "ln3")
            stats3(3)
            centre3(3)
            stats4(0)
            sum3(3)
            shift(0, "ln4")
            stats4(1)
            stats4(2)
            shift(1, "ln4")
            stats4(3)
            shift(2, "ln4")
            layer_apply(NB - 1, FIN, AM, "ln4").then_inc(sem("fin_last"), 1)


def constants():
    c = np.zeros((P, NCONST), np.float32)
    i, j = np.arange(P)[:, None], np.arange(P)[None, :]

    def put(name, value):
        at, n = CONST[name]
        c[:, at:at + n] = value

    put("ident", i == j)
    put("blockdiag", i // DH == j // DH)
    put("headmean", (i // DH == j // DH) / DH)
    jc = np.arange(CS)[None, :]
    put("causal", jc >= i % CS)
    put("dist", np.maximum(jc - i % CS, 0))
    put("after", jc + 1)
    put("same_tile", j % NT > 0)
    put("later", -1.0 * (i > j))
    put("left", CS - 1 - i % CS)
    put("quad", (i % 32) // DH == np.arange(HJ))
    put("head", i // DH == np.arange(H))
    put("keyhead", i // KC == np.arange(HJ))
    put("iota_a", np.arange(SLOT_A))
    put("iota_b", np.arange(SLOT_B))
    put("token_hi", P * np.arange(NT) - FAR)
    put("token_lo", i)
    put("same_token", j % NE > 0)
    put("eps6", 1e-6)
    put("eps5", 1e-5)
    put("ones", 1)
    bits = np.zeros((P, NC * ROUNDS), np.int32)
    for r in range(ROUNDS):
        for n in range(NC):
            bits[:, NC * r + n] = (n + 1) << (BITS - ROUND_BITS * (r + 1))
    return c, bits


def kernel(**inputs):
    import concourse.bacc as bacc
    from concourse.bass_utils import run_bass_kernel_spmd

    a = {k: np.asarray(v) for k, v in inputs.items()}

    def attn(n):
        return a["L0_attn_" + n]

    c, bits = constants()
    w1 = np.concatenate([attn(n).T for n in ("Wq", "Wk", "Wv", "Wg", "Wo")], 1)
    down = np.zeros((P, 3, D), np.float32)
    for m in range(3):
        down[:MB[m], m] = attn("down_w").T[P * m:P * m + MB[m]]
    ctx = a["ctx_1024"].transpose(2, 0, 1)
    ctxrep = np.broadcast_to(ctx[:, :, None, :], (D, NB, HJ, KC))
    w2 = np.concatenate([attn("gate_w").T, attn("up_w").T, down.reshape(P, -1)]
                        + [a["L0_xattn_W_" + n].T for n in "qkvo"]
                        + [ctx.reshape(D, -1), ctxrep.reshape(D, -1), a["L0_ffn_Wr"]], 1)

    def row(v):
        return np.broadcast_to(v.reshape(1, -1), (P, v.size))

    vecs = np.concatenate([attn("ln1_w")[:, None], attn("ln2_w")[:, None], attn("gn_w")[:, None],
                           attn("gn_b")[:, None], np.repeat(attn("gamma"), DH)[:, None], row(attn("gamma")),
                           attn("gamma").reshape(NPAIR, 2).T.repeat(CS, 0),
                           row(a["L0_ffn_br"]), row(a["L0_ffn_gamma"]), row(a["L0_ffn_beta"]),
                           a["L0_ffn_b1"].reshape(NE * FB, P).T, row(a["L0_ffn_b2"])], 1)
    ew1 = a["L0_ffn_W1"].transpose(1, 0, 2)
    ew2 = a["L0_ffn_W2"].reshape(NE, FB, P, D).transpose(2, 0, 1, 3)
    arrays = {"x_dram": a["x"].reshape(N, D), "const_dram": c, "bits_dram": bits, "w1_dram": w1, "w2_dram": w2,
              "vec_dram": vecs, "ew1_dram": ew1, "ew2_dram": ew2}
    arrays = {k: np.ascontiguousarray(v) for k, v in arrays.items()}
    nc = bacc.Bacc("TRN2", target_bir_lowering=False, num_devices=1)
    args = [nc.dram_tensor(k, v.shape, mybir.dt.from_np(v.dtype), kind="ExternalInput").ap()
            for k, v in arrays.items()]
    args.append(nc.dram_tensor("out_dram", [N, D], F32, kind="ExternalOutput").ap())
    decoder_layer(nc, *args)
    r = run_bass_kernel_spmd(nc, [arrays], core_ids=[0])
    return r.results[0]["out_dram"].reshape(NB, T, D)
```
